# Optimizing a Trainium2 kernel written in Bass

```python
import numpy as np
import jax
import jax.numpy as jnp

def _softmax(x, axis=-1):
    return jax.nn.softmax(x, axis=axis)

def _gelu(x):
    return jax.nn.gelu(x, approximate=True)

def _silu(x):
    return jax.nn.silu(x)

def _sigmoid(x):
    return jax.nn.sigmoid(x)

def _layernorm(x, axis=-1, eps=1e-05):
    m = jnp.mean(x, axis=axis, keepdims=True)
    v = jnp.var(x, axis=axis, keepdims=True)
    return (x - m) / jnp.sqrt(v + eps)

def _scatter_add(tgt, idx, src, axis=0):
    return tgt.at[idx].add(src)

def _segment_sum(src, seg, n):
    return jax.ops.segment_sum(src, seg, n)
kernel_name = 'mk_decoder_postln_d2_seqx_r4_ff056c'

def setup_inputs(seed: int=0):
    np.random.seed(seed)
    _w = jnp.asarray

    def _rec_inputs():
        import jax
        import jax.numpy as jnp
        _rk = jax.random.key(seed)
        x = -0.0002928 + 1 * jax.random.normal(jax.random.fold_in(_rk, 1), (1, 2048, 256), jnp.float32)
        _lenS = 2048 - jax.random.randint(jax.random.fold_in(_rk, 7), (1,), 0, max(1, 2048 // 4) + 1, jnp.int32)
        _lenS2 = 1601 - jax.random.randint(jax.random.fold_in(_rk, 8), (1,), 0, max(1, 1601 // 4) + 1, jnp.int32)
        _ctx_1024P = jax.random.normal(jax.random.fold_in(_rk, 11), (1, 16, 256), jnp.float32)
        _ctx_1024c = jax.random.dirichlet(jax.random.fold_in(_rk, 511), 0.3 * jnp.ones((16,), jnp.float32), (1, 1601))
        _ctx_1024t = jnp.einsum('bsk,bkd->bsd', _ctx_1024c, _ctx_1024P)
        _ctx_1024t = _ctx_1024t * jax.lax.rsqrt(jnp.mean(jnp.square(_ctx_1024t)) + 1e-12) * 0.953939
        ctx_1024 = -1.39393e-06 + 0.999914 * (_ctx_1024t + 0.3 * jax.random.normal(jax.random.fold_in(_rk, 611), (1, 1601, 256), jnp.float32))
        _validS = jnp.arange(2048)[None, :] < _lenS[:, None]
        _validS2 = jnp.arange(1601)[None, :] < _lenS2[:, None]
        _causal = jnp.tril(jnp.ones((2048, 2048), dtype=bool))
        mask_1x1xSxS2_ik0 = jnp.where(jnp.broadcast_to(_validS2[0:1, None, None, :], (1, 1, 2048, 1601)), 0, 1).astype(jnp.int32)
        return (x, ctx_1024, mask_1x1xSxS2_ik0)
    x, ctx_1024, mask_1x1xSxS2_ik0 = _rec_inputs()

    def _L0_attn_setup():
        import math
        import jax, jax.numpy as jnp
        import numpy as np
        DIM = 256
        N_HEADS = 16
        HEAD_DIM = DIM // N_HEADS
        SEQ_LEN = 512
        BASE = 10000.0
        EPS = 1e-05

        def rope_cache(seq_len, dim):
            pos = jnp.arange(seq_len, dtype=jnp.float32)[:, None]
            di = jnp.arange(0, dim, 2, dtype=jnp.float32) / dim
            theta = pos * jnp.exp(-di * math.log(BASE))
            cos = jnp.repeat(jnp.cos(theta), 2, axis=1)
            sin = jnp.repeat(jnp.sin(theta), 2, axis=1)
            return (cos, sin)

        def rotate_half(x):
            x1 = x[..., ::2]
            x2 = x[..., 1::2]
            return jnp.concatenate((-x2, x1), axis=-1)

        def layernorm(x, gamma, beta):
            mu = jnp.mean(x, axis=-1, keepdims=True)
            var = jnp.var(x, axis=-1, keepdims=True)
            return (x - mu) * jax.lax.rsqrt(var + EPS) * gamma + beta
        key = jax.random.key(seed)
        ks = jax.random.split(key, 7)
        s = 1.0 / math.sqrt(DIM)
        return {'x': jax.random.normal(ks[0], (2, SEQ_LEN, DIM), dtype=jnp.float32), 'Wq': jax.random.normal(ks[1], (DIM, DIM), dtype=jnp.float32) * s, 'Wk': jax.random.normal(ks[2], (DIM, DIM), dtype=jnp.float32) * s, 'Wv': jax.random.normal(ks[3], (DIM, DIM), dtype=jnp.float32) * s, 'q_gamma': jnp.ones((HEAD_DIM,), jnp.float32), 'q_beta': jnp.zeros((HEAD_DIM,), jnp.float32), 'k_gamma': jnp.ones((HEAD_DIM,), jnp.float32), 'k_beta': jnp.zeros((HEAD_DIM,), jnp.float32), 'Wo': jax.random.normal(ks[4], (DIM, DIM), dtype=jnp.float32) * s, 'bo': jnp.zeros((DIM,), jnp.float32)}
    _L0_attn_all = _L0_attn_setup()
    _L0_attn_in = {k: v for k, v in _L0_attn_all.items() if k in ('Wq', 'Wk', 'Wv', 'q_gamma', 'q_beta', 'k_gamma', 'k_beta', 'Wo', 'bo')}
    del _L0_attn_all

    def _L0_xattn_setup():
        import jax, jax.numpy as jnp
        import numpy as np
        D_MODEL = 256
        NUM_HEADS = 16
        D_K = D_MODEL // NUM_HEADS
        B, S = (2, 512)
        NEG_INF = -1000000000.0
        key = jax.random.key(seed)
        ks = jax.random.split(key, 12)
        scale = 1.0 / np.sqrt(D_MODEL)
        q = jax.random.normal(ks[0], (B, S, D_MODEL), dtype=jnp.float32)
        k = jax.random.normal(ks[1], (B, S, D_MODEL), dtype=jnp.float32)
        v = jax.random.normal(ks[2], (B, S, D_MODEL), dtype=jnp.float32)
        mask = jnp.tril(jnp.ones((S, S), dtype=jnp.int32))[None, None, :, :]
        Wq = jax.random.normal(ks[3], (D_MODEL, D_MODEL), dtype=jnp.float32) * scale
        bq = jnp.zeros((D_MODEL,), dtype=jnp.float32)
        Wk = jax.random.normal(ks[4], (D_MODEL, D_MODEL), dtype=jnp.float32) * scale
        bk = jnp.zeros((D_MODEL,), dtype=jnp.float32)
        Wv = jax.random.normal(ks[5], (D_MODEL, D_MODEL), dtype=jnp.float32) * scale
        bv = jnp.zeros((D_MODEL,), dtype=jnp.float32)
        Wo = jax.random.normal(ks[6], (D_MODEL, D_MODEL), dtype=jnp.float32) * scale
        bo = jnp.zeros((D_MODEL,), dtype=jnp.float32)
        return {'q': q, 'k': k, 'v': v, 'mask': mask, 'Wq': Wq, 'bq': bq, 'Wk': Wk, 'bk': bk, 'Wv': Wv, 'bv': bv, 'Wo': Wo, 'bo': bo}
    _L0_xattn_all = _L0_xattn_setup()
    _L0_xattn_in = {k: v for k, v in _L0_xattn_all.items() if k in ('Wq', 'bq', 'Wk', 'bk', 'Wv', 'bv', 'Wo', 'bo')}
    del _L0_xattn_all

    def _L0_ffn_setup():
        import jax, jax.numpy as jnp
        import numpy as np
        FP8_MAX = 448.0

        def quant_fp8(x):
            amax = jnp.max(jnp.abs(x)).astype(jnp.float32)
            scale = jnp.minimum(FP8_MAX / jnp.maximum(amax, 1e-12), FP8_MAX)
            x_fp8 = jnp.clip(x * scale, -FP8_MAX, FP8_MAX).astype(jnp.float8_e4m3fn)
            return (x_fp8, 1.0 / scale)
        key = jax.random.key(seed)
        k1, k2, k3 = jax.random.split(key, 3)
        B, S, IN, OUT = (4, 2048, 256, 256)
        input = jax.random.normal(k1, (B, S, IN), dtype=jnp.float32)
        bound = 1.0 / np.sqrt(IN)
        weight = jax.random.uniform(k2, (OUT, IN), dtype=jnp.float32, minval=-bound, maxval=bound)
        bias = jax.random.uniform(k3, (OUT,), dtype=jnp.float32, minval=-bound, maxval=bound)
        return {'input': input, 'weight': weight, 'bias': bias}
    _L0_ffn_all = _L0_ffn_setup()
    _L0_ffn_in = {k: v for k, v in _L0_ffn_all.items() if k in ('weight', 'bias')}
    del _L0_ffn_all

    def _L1_attn_setup():
        import jax, jax.numpy as jnp
        import numpy as np
        import math
        B, T, C, H = (4, 512, 256, 16)
        EPS = 1e-10

        def layernorm(x):
            mean = jnp.mean(x, axis=-1, keepdims=True)
            xmu = x - mean
            var = jnp.mean(xmu * xmu, axis=-1, keepdims=True)
            return xmu / jnp.sqrt(var + EPS)

        def new_gelu(x):
            c = math.sqrt(2.0 / math.pi)
            return 0.5 * x * (1.0 + jnp.tanh(c * (x + 0.044715 * x * x * x)))

        def attention(x, w_attn, b_attn, w_proj, b_proj):
            b, t, cdim = x.shape
            d = cdim // H
            ca = x @ w_attn.T + b_attn
            q, k, v = jnp.split(ca, 3, axis=2)
            q = q.reshape(b, t, H, d)
            k = k.reshape(b, t, H, d)
            v = v.reshape(b, t, H, d)
            att = jnp.einsum('bthd,bshd->bhts', q, k) * (1.0 / math.sqrt(d))
            mask = jnp.tril(jnp.ones((t, t), dtype=bool))
            att = jnp.where(mask, att, -jnp.inf)
            att = jax.nn.softmax(att, axis=-1)
            y = jnp.einsum('bhts,bshd->bthd', att, v).reshape(b, t, cdim)
            return y @ w_proj.T + b_proj
        key = jax.random.key(seed)
        ks = jax.random.split(key, 9)
        s = 0.02
        return {'x': jax.random.normal(ks[0], (B, T, C), jnp.float32), 'w_attn': jax.random.normal(ks[1], (3 * C, C), jnp.float32) * s, 'b_attn': jax.random.normal(ks[2], (3 * C,), jnp.float32) * s, 'w_proj': jax.random.normal(ks[3], (C, C), jnp.float32) * s, 'b_proj': jax.random.normal(ks[4], (C,), jnp.float32) * s, 'w_fc': jax.random.normal(ks[5], (4 * C, C), jnp.float32) * s, 'b_fc': jax.random.normal(ks[6], (4 * C,), jnp.float32) * s, 'w_mlp_proj': jax.random.normal(ks[7], (C, 4 * C), jnp.float32) * s, 'b_mlp_proj': jax.random.normal(ks[8], (C,), jnp.float32) * s}
    _L1_attn_all = _L1_attn_setup()
    _L1_attn_in = {k: v for k, v in _L1_attn_all.items() if k in ('w_attn', 'b_attn', 'w_proj', 'b_proj', 'w_fc', 'b_fc', 'w_mlp_proj', 'b_mlp_proj')}
    del _L1_attn_all

    def _L1_xattn_setup():
        import jax, jax.numpy as jnp
        import numpy as np
        EMBED_DIM = 256
        NUM_HEADS = 16
        HEAD_DIM = EMBED_DIM // NUM_HEADS
        SCALE = HEAD_DIM ** (-0.5)

        def _split_heads(x, B):
            return x.reshape(B, -1, NUM_HEADS, HEAD_DIM).transpose(0, 2, 1, 3)
        key = jax.random.key(seed)
        ks = jax.random.split(key, 11)
        B, S, D = (2, 512, EMBED_DIM)
        std = D ** (-0.5)
        return {'query': jax.random.normal(ks[0], (B, S, D), jnp.float32), 'key': jax.random.normal(ks[1], (B, S, D), jnp.float32), 'value': jax.random.normal(ks[2], (B, S, D), jnp.float32), 'q_w': jax.random.normal(ks[3], (D, D), jnp.float32) * std, 'q_b': jnp.zeros((D,), jnp.float32), 'k_w': jax.random.normal(ks[4], (D, D), jnp.float32) * std, 'k_b': jnp.zeros((D,), jnp.float32), 'v_w': jax.random.normal(ks[5], (D, D), jnp.float32) * std, 'v_b': jnp.zeros((D,), jnp.float32), 'o_w': jax.random.normal(ks[6], (D, D), jnp.float32) * std, 'o_b': jnp.zeros((D,), jnp.float32)}
    _L1_xattn_all = _L1_xattn_setup()
    _L1_xattn_in = {k: v for k, v in _L1_xattn_all.items() if k in ('q_w', 'q_b', 'k_w', 'k_b', 'v_w', 'v_b', 'o_w', 'o_b')}
    del _L1_xattn_all

    def _L1_ffn_setup():
        import jax, jax.numpy as jnp
        import numpy as np
        DIM = 256
        INTER = 512
        E = 8
        TOPK = 2
        ROUTE_SCALE = 1.0

        def _mlp(x, w1, w2, w3):
            h = jax.nn.silu(x @ w1.T) * (x @ w3.T)
            return h @ w2.T
        key = jax.random.key(seed)
        ks = jax.random.split(key, 10)
        s_in = 0.02
        return {'x': jax.random.normal(ks[0], (4, 512, DIM), dtype=jnp.float32), 'gate_w': jax.random.normal(ks[1], (E, DIM), dtype=jnp.float32) * s_in, 'gate_bias': jax.random.normal(ks[2], (E,), dtype=jnp.float32) * 0.01, 'w1': jax.random.normal(ks[3], (E, INTER, DIM), dtype=jnp.float32) * s_in, 'w2': jax.random.normal(ks[4], (E, DIM, INTER), dtype=jnp.float32) * s_in, 'w3': jax.random.normal(ks[5], (E, INTER, DIM), dtype=jnp.float32) * s_in, 'sw1': jax.random.normal(ks[6], (INTER, DIM), dtype=jnp.float32) * s_in, 'sw2': jax.random.normal(ks[7], (DIM, INTER), dtype=jnp.float32) * s_in, 'sw3': jax.random.normal(ks[8], (INTER, DIM), dtype=jnp.float32) * s_in}
    _L1_ffn_all = _L1_ffn_setup()
    _L1_ffn_in = {k: v for k, v in _L1_ffn_all.items() if k in ('gate_w', 'gate_bias', 'w1', 'w2', 'w3', 'sw1', 'sw2', 'sw3')}
    del _L1_ffn_all
    return {'x': x, 'ctx_1024': ctx_1024, 'mask_1x1xSxS2_ik0': mask_1x1xSxS2_ik0, 'L0_attn_Wq': _L0_attn_in['Wq'], 'L0_attn_Wk': _L0_attn_in['Wk'], 'L0_attn_Wv': _L0_attn_in['Wv'], 'L0_attn_q_gamma': _L0_attn_in['q_gamma'], 'L0_attn_q_beta': _L0_attn_in['q_beta'], 'L0_attn_k_gamma': _L0_attn_in['k_gamma'], 'L0_attn_k_beta': _L0_attn_in['k_beta'], 'L0_attn_Wo': _L0_attn_in['Wo'], 'L0_attn_bo': _L0_attn_in['bo'], 'L0_xattn_Wq': _L0_xattn_in['Wq'], 'L0_xattn_bq': _L0_xattn_in['bq'], 'L0_xattn_Wk': _L0_xattn_in['Wk'], 'L0_xattn_bk': _L0_xattn_in['bk'], 'L0_xattn_Wv': _L0_xattn_in['Wv'], 'L0_xattn_bv': _L0_xattn_in['bv'], 'L0_xattn_Wo': _L0_xattn_in['Wo'], 'L0_xattn_bo': _L0_xattn_in['bo'], 'L0_ffn_weight': _L0_ffn_in['weight'], 'L0_ffn_bias': _L0_ffn_in['bias'], 'L1_attn_w_attn': _L1_attn_in['w_attn'], 'L1_attn_b_attn': _L1_attn_in['b_attn'], 'L1_attn_w_proj': _L1_attn_in['w_proj'], 'L1_attn_b_proj': _L1_attn_in['b_proj'], 'L1_attn_w_fc': _L1_attn_in['w_fc'], 'L1_attn_b_fc': _L1_attn_in['b_fc'], 'L1_attn_w_mlp_proj': _L1_attn_in['w_mlp_proj'], 'L1_attn_b_mlp_proj': _L1_attn_in['b_mlp_proj'], 'L1_xattn_q_w': _L1_xattn_in['q_w'], 'L1_xattn_q_b': _L1_xattn_in['q_b'], 'L1_xattn_k_w': _L1_xattn_in['k_w'], 'L1_xattn_k_b': _L1_xattn_in['k_b'], 'L1_xattn_v_w': _L1_xattn_in['v_w'], 'L1_xattn_v_b': _L1_xattn_in['v_b'], 'L1_xattn_o_w': _L1_xattn_in['o_w'], 'L1_xattn_o_b': _L1_xattn_in['o_b'], 'L1_ffn_gate_w': _L1_ffn_in['gate_w'], 'L1_ffn_gate_bias': _L1_ffn_in['gate_bias'], 'L1_ffn_w1': _L1_ffn_in['w1'], 'L1_ffn_w2': _L1_ffn_in['w2'], 'L1_ffn_w3': _L1_ffn_in['w3'], 'L1_ffn_sw1': _L1_ffn_in['sw1'], 'L1_ffn_sw2': _L1_ffn_in['sw2'], 'L1_ffn_sw3': _L1_ffn_in['sw3']}

def reference(x, ctx_1024, mask_1x1xSxS2_ik0, L0_attn_Wq, L0_attn_Wk, L0_attn_Wv, L0_attn_q_gamma, L0_attn_q_beta, L0_attn_k_gamma, L0_attn_k_beta, L0_attn_Wo, L0_attn_bo, L0_xattn_Wq, L0_xattn_bq, L0_xattn_Wk, L0_xattn_bk, L0_xattn_Wv, L0_xattn_bv, L0_xattn_Wo, L0_xattn_bo, L0_ffn_weight, L0_ffn_bias, L1_attn_w_attn, L1_attn_b_attn, L1_attn_w_proj, L1_attn_b_proj, L1_attn_w_fc, L1_attn_b_fc, L1_attn_w_mlp_proj, L1_attn_b_mlp_proj, L1_xattn_q_w, L1_xattn_q_b, L1_xattn_k_w, L1_xattn_k_b, L1_xattn_v_w, L1_xattn_v_b, L1_xattn_o_w, L1_xattn_o_b, L1_ffn_gate_w, L1_ffn_gate_bias, L1_ffn_w1, L1_ffn_w2, L1_ffn_w3, L1_ffn_sw1, L1_ffn_sw2, L1_ffn_sw3):
    import jax
    import jax.numpy as jnp

    def _L0_attn_ref(x, Wq, Wk, Wv, q_gamma, q_beta, k_gamma, k_beta, Wo, bo):
        import math
        import jax, jax.numpy as jnp
        import numpy as np
        DIM = 256
        N_HEADS = 16
        HEAD_DIM = DIM // N_HEADS
        SEQ_LEN = 512
        BASE = 10000.0
        EPS = 1e-05

        def rope_cache(seq_len, dim):
            pos = jnp.arange(seq_len, dtype=jnp.float32)[:, None]
            di = jnp.arange(0, dim, 2, dtype=jnp.float32) / dim
            theta = pos * jnp.exp(-di * math.log(BASE))
            cos = jnp.repeat(jnp.cos(theta), 2, axis=1)
            sin = jnp.repeat(jnp.sin(theta), 2, axis=1)
            return (cos, sin)

        def rotate_half(x):
            x1 = x[..., ::2]
            x2 = x[..., 1::2]
            return jnp.concatenate((-x2, x1), axis=-1)

        def layernorm(x, gamma, beta):
            mu = jnp.mean(x, axis=-1, keepdims=True)
            var = jnp.var(x, axis=-1, keepdims=True)
            return (x - mu) * jax.lax.rsqrt(var + EPS) * gamma + beta
        B, S, D = x.shape
        H, hd = (N_HEADS, HEAD_DIM)
        q = (x @ Wq.T).reshape(B, S, H, hd).transpose(0, 2, 1, 3)
        k = (x @ Wk.T).reshape(B, S, H, hd).transpose(0, 2, 1, 3)
        v = (x @ Wv.T).reshape(B, S, H, hd).transpose(0, 2, 1, 3)
        q = layernorm(q, q_gamma, q_beta)
        k = layernorm(k, k_gamma, k_beta)
        cos, sin = rope_cache(S, hd)
        cos = cos[None, None]
        sin = sin[None, None]
        q = q * cos + rotate_half(q) * sin
        k = k * cos + rotate_half(k) * sin
        scale = 1.0 / math.sqrt(hd)
        scores = scale * jnp.einsum('bhqd,bhkd->bhqk', q, k)
        mask = jnp.tril(jnp.ones((S, S), dtype=bool))
        scores = jnp.where(mask, scores, -jnp.inf)
        attn = jax.nn.softmax(scores, axis=-1)
        out = jnp.einsum('bhqk,bhkd->bhqd', attn, v)
        out = out.transpose(0, 2, 1, 3).reshape(B, S, D)
        return out @ Wo.T + bo

    def _L0_xattn_ref(q, k, v, mask, Wq, bq, Wk, bk, Wv, bv, Wo, bo):
        import jax, jax.numpy as jnp
        import numpy as np
        D_MODEL = 256
        NUM_HEADS = 16
        D_K = D_MODEL // NUM_HEADS
        B, S = (2, 512)
        NEG_INF = -1000000000.0
        qp = q @ Wq.T + bq
        kp = k @ Wk.T + bk
        vp = v @ Wv.T + bv

        def split_heads(x):
            b, s, _ = x.shape
            return x.reshape(b, s, NUM_HEADS, D_K).transpose(0, 2, 1, 3)
        qh, kh, vh = (split_heads(qp), split_heads(kp), split_heads(vp))
        scores = jnp.einsum('bhqd,bhkd->bhqk', qh, kh) / jnp.sqrt(jnp.float32(D_K))
        scores = jnp.where(mask == 0, NEG_INF, scores)
        attn = jax.nn.softmax(scores, axis=-1)
        ctx = jnp.einsum('bhqk,bhkd->bhqd', attn, vh)
        b = ctx.shape[0]
        out = ctx.transpose(0, 2, 1, 3).reshape(b, -1, NUM_HEADS * D_K)
        return out @ Wo.T + bo

    def _L0_ffn_ref(input, weight, bias):
        import jax, jax.numpy as jnp
        import numpy as np
        FP8_MAX = 448.0

        def quant_fp8(x):
            amax = jnp.max(jnp.abs(x)).astype(jnp.float32)
            scale = jnp.minimum(FP8_MAX / jnp.maximum(amax, 1e-12), FP8_MAX)
            x_fp8 = jnp.clip(x * scale, -FP8_MAX, FP8_MAX).astype(jnp.float8_e4m3fn)
            return (x_fp8, 1.0 / scale)
        prev_shape = input.shape
        x2d = input.reshape(-1, weight.shape[1])
        w_fp8, w_scale = quant_fp8(weight)
        x_fp8, x_scale = quant_fp8(x2d)
        acc = jnp.matmul(x_fp8.astype(jnp.float32), w_fp8.astype(jnp.float32).T)
        out2d = (acc * (x_scale * w_scale) + bias).astype(jnp.bfloat16)
        out = out2d.reshape(*prev_shape[:-1], weight.shape[0]).astype(input.dtype)
        return out

    def _L1_attn_ref(x, w_attn, b_attn, w_proj, b_proj, w_fc, b_fc, w_mlp_proj, b_mlp_proj):
        import jax, jax.numpy as jnp
        import numpy as np
        import math
        B, T, C, H = (4, 512, 256, 16)
        EPS = 1e-10

        def layernorm(x):
            mean = jnp.mean(x, axis=-1, keepdims=True)
            xmu = x - mean
            var = jnp.mean(xmu * xmu, axis=-1, keepdims=True)
            return xmu / jnp.sqrt(var + EPS)

        def new_gelu(x):
            c = math.sqrt(2.0 / math.pi)
            return 0.5 * x * (1.0 + jnp.tanh(c * (x + 0.044715 * x * x * x)))

        def attention(x, w_attn, b_attn, w_proj, b_proj):
            b, t, cdim = x.shape
            d = cdim // H
            ca = x @ w_attn.T + b_attn
            q, k, v = jnp.split(ca, 3, axis=2)
            q = q.reshape(b, t, H, d)
            k = k.reshape(b, t, H, d)
            v = v.reshape(b, t, H, d)
            att = jnp.einsum('bthd,bshd->bhts', q, k) * (1.0 / math.sqrt(d))
            mask = jnp.tril(jnp.ones((t, t), dtype=bool))
            att = jnp.where(mask, att, -jnp.inf)
            att = jax.nn.softmax(att, axis=-1)
            y = jnp.einsum('bhts,bshd->bthd', att, v).reshape(b, t, cdim)
            return y @ w_proj.T + b_proj
        x = x + attention(layernorm(x), w_attn, b_attn, w_proj, b_proj)
        h = new_gelu(layernorm(x) @ w_fc.T + b_fc)
        x = x + (h @ w_mlp_proj.T + b_mlp_proj)
        return x

    def _L1_xattn_ref(query, key, value, q_w, q_b, k_w, k_b, v_w, v_b, o_w, o_b):
        import jax, jax.numpy as jnp
        import numpy as np
        EMBED_DIM = 256
        NUM_HEADS = 16
        HEAD_DIM = EMBED_DIM // NUM_HEADS
        SCALE = HEAD_DIM ** (-0.5)

        def _split_heads(x, B):
            return x.reshape(B, -1, NUM_HEADS, HEAD_DIM).transpose(0, 2, 1, 3)
        B = query.shape[0]
        q = _split_heads(query @ q_w + q_b, B)
        k = _split_heads(key @ k_w + k_b, B)
        v = _split_heads(value @ v_w + v_b, B)
        scores = jnp.einsum('bhqd,bhkd->bhqk', q, k) * SCALE
        attn = jax.nn.softmax(scores, axis=-1)
        out = jnp.einsum('bhqk,bhkd->bhqd', attn, v)
        out = out.transpose(0, 2, 1, 3).reshape(B, -1, EMBED_DIM)
        return out @ o_w + o_b

    def _L1_ffn_ref(x, gate_w, gate_bias, w1, w2, w3, sw1, sw2, sw3):
        import jax, jax.numpy as jnp
        import numpy as np
        DIM = 256
        INTER = 512
        E = 8
        TOPK = 2
        ROUTE_SCALE = 1.0

        def _mlp(x, w1, w2, w3):
            h = jax.nn.silu(x @ w1.T) * (x @ w3.T)
            return h @ w2.T
        shape = x.shape
        xt = x.reshape(-1, DIM)
        T = xt.shape[0]
        logits = xt @ gate_w.T
        scores = jax.nn.softmax(logits.astype(jnp.float32), axis=-1)
        original_scores = scores
        biased = scores + gate_bias
        _, indices = jax.lax.top_k(biased, TOPK)
        weights = jnp.take_along_axis(original_scores, indices, axis=1)
        weights = (weights * ROUTE_SCALE).astype(x.dtype)
        combine = (jax.nn.one_hot(indices, E, dtype=weights.dtype) * weights[..., None]).sum(axis=1)
        y = jnp.zeros_like(xt)
        for e in range(E):
            y = y + _mlp(xt, w1[e], w2[e], w3[e]) * combine[:, e:e + 1]
        z = _mlp(xt, sw1, sw2, sw3)
        return (y + z).reshape(shape)
    x = _layernorm(x + _L0_attn_ref(x, L0_attn_Wq, L0_attn_Wk, L0_attn_Wv, L0_attn_q_gamma, L0_attn_q_beta, L0_attn_k_gamma, L0_attn_k_beta, L0_attn_Wo, L0_attn_bo), axis=-1)
    x = _layernorm(x + _L0_xattn_ref(x, ctx_1024, ctx_1024, mask_1x1xSxS2_ik0, L0_xattn_Wq, L0_xattn_bq, L0_xattn_Wk, L0_xattn_bk, L0_xattn_Wv, L0_xattn_bv, L0_xattn_Wo, L0_xattn_bo), axis=-1)
    x = _layernorm(x + _L0_ffn_ref(x, L0_ffn_weight, L0_ffn_bias), axis=-1)
    x = _layernorm(x + _L1_attn_ref(x, L1_attn_w_attn, L1_attn_b_attn, L1_attn_w_proj, L1_attn_b_proj, L1_attn_w_fc, L1_attn_b_fc, L1_attn_w_mlp_proj, L1_attn_b_mlp_proj), axis=-1)
    x = _layernorm(x + _L1_xattn_ref(x, ctx_1024, ctx_1024, L1_xattn_q_w, L1_xattn_q_b, L1_xattn_k_w, L1_xattn_k_b, L1_xattn_v_w, L1_xattn_v_b, L1_xattn_o_w, L1_xattn_o_b), axis=-1)
    x = _layernorm(x + _L1_ffn_ref(x, L1_ffn_gate_w, L1_ffn_gate_bias, L1_ffn_w1, L1_ffn_w2, L1_ffn_w3, L1_ffn_sw1, L1_ffn_sw2, L1_ffn_sw3), axis=-1)
    return x

_drawn_inputs = setup_inputs


def setup_inputs(seed=0):
    import zlib

    import numpy as np

    out = dict(_drawn_inputs(seed))
    spreads = {'L0_attn_q_gamma': (1.0, 0.6),
     'L0_attn_q_beta': (0.0, 0.692),
     'L0_attn_k_gamma': (1.0, 0.6),
     'L0_attn_k_beta': (0.0, 0.725),
     'L0_attn_bo': (0.0, 0.1),
     'L0_xattn_bq': (0.0, 0.373),
     'L0_xattn_bk': (0.0, 2.0),
     'L0_xattn_bv': (0.0, 0.1),
     'L0_xattn_bo': (0.0, 0.1),
     'L1_xattn_q_b': (0.0, 0.409),
     'L1_xattn_k_b': (0.0, 2.0),
     'L1_xattn_v_b': (0.0, 0.1),
     'L1_xattn_o_b': (0.0, 0.1)}
    factors = {'L1_attn_w_attn': 3.025,
     'L1_attn_b_attn': 8.0,
     'L1_attn_w_proj': 2.716,
     'L1_attn_b_proj': 6.315,
     'L1_attn_b_fc': 8.0,
     'L1_attn_b_mlp_proj': 6.551,
     'L1_ffn_gate_w': 8.0,
     'L1_ffn_gate_bias': 8.0,
     'L1_ffn_w1': 8.0,
     'L1_ffn_w2': 8.0,
     'L1_ffn_w3': 8.0,
     'L1_ffn_sw1': 8.0,
     'L1_ffn_sw2': 8.0,
     'L1_ffn_sw3': 8.0}
    for name, (base, spread) in spreads.items():
        noise = np.random.default_rng([zlib.crc32(name.encode()), seed]).standard_normal(out[name].shape)
        drawn = base * np.exp(spread * noise) if base else spread * noise
        out[name] = jnp.asarray(drawn.astype(out[name].dtype))
    for name, factor in factors.items():
        out[name] = (out[name] * factor).astype(out[name].dtype)
    return out
```

```python
from contextlib import ExitStack, contextmanager

import numpy as np

import concourse.bass as bass
from concourse import mybir

F32 = mybir.dt.float32
BF16 = mybir.dt.bfloat16
I32 = mybir.dt.int32
FP8 = mybir.dt.float8e4
ALU = mybir.AluOpType
ACT = mybir.ActivationFunctionType
AX = mybir.AxisListType.X
RMAX = bass.bass_isa.ReduceOp.max

P = 128
S = 2048
S2 = 1601
D = 256
H = 16
HD = D // H
NT = S // P
NT2 = -(-S2 // P)
NC = D // P
CH = 512
HALF = S // 2
SUB = HALF // 4
PARTS = [0, 1, 2, 0, 1, 0], [0, 0, 0, 1, 1, 2]
KQ = HD * 6
KM = KQ + 3
FF = 4 * D
NE = 9
INTER = 512
MASKED = -float(2 ** 30)
FIRST_SEMAPHORE, PHASE_SEMAPHORES = 160, 30
PHASES_SO_FAR = {}


def tiles(n, w):
    return [(a, min(w, n - a)) for a in range(0, n, w)]


@contextmanager
def phase(nc):
    number = nc.next_id()
    turns = PHASES_SO_FAR[id(nc)] = PHASES_SO_FAR.get(id(nc), 0) + 1
    first = FIRST_SEMAPHORE + PHASE_SEMAPHORES * (turns % 2)
    sems = []

    def sem(name):
        assert len(sems) < PHASE_SEMAPHORES
        sems.append(nc.alloc_semaphore(name=f"{name}_{number}", num=first + len(sems)))
        return sems[-1]

    yield sem
    nc.clear_and_free_semaphores(sems)


class Env:
    pass


class Chain:

    def __init__(self, eng, sem, start=0):
        self.eng, self.sem, self.n = eng, sem, start

    def link(self, ins):
        self.n += 1
        ins.then_inc(self.sem, 1)
        self.eng.wait_ge(self.sem, self.n)


def load_phase(nc, e):
    with phase(nc) as sem:
        loaded = sem("loaded")
        with nc.Block() as block:

            @block.sync
            def _(sp):
                pairs = [(e.ident, e.d["ident"])]
                pairs += [(e.wide[:, i * P:(i + 1) * P], e.d[n]) for i, n in enumerate(("masked", "upper", "lower"))]
                pairs += [(e.x_nat, e.d["x"].rearrange("(t p) c -> p t c", p=P)),
                          (e.xT, e.d["xT"].rearrange("(k p) t -> p k t", p=P))]
                for dst, src in pairs:
                    sp.dma_start(dst, src).then_inc(loaded, 16)
                sp.wait_ge(loaded, 16 * len(pairs))

            @block.vector
            def _(dve):
                nc.vector.memset(e.vbuf[0], 1.0)
                nc.vector.memset(e.vbuf[1], 1.0)
                nc.vector.memset(e.eps5, 1e-5)
                nc.vector.memset(e.eps10, 1e-10)
                dve.wait_ge(loaded, 16 * 6)
                nc.vector.tensor_copy(e.ident16, e.ident)
                for i, dst in enumerate((e.big16, e.upper16, e.lower16)):
                    nc.vector.tensor_copy(dst, e.wide[:, i * P:(i + 1) * P])


def transpose_phase(nc, e, src, dst):
    with phase(nc) as sem:
        turned = sem("turned")
        with nc.Block() as block:
            groups = [(c, g) for g in range(NT // 4) for c in range(NC)]

            @block.tensor
            def _(pe):
                for b, (c, g) in enumerate(groups):
                    for i in range(4):
                        last = nc.tensor.transpose(e.ps[:, b, i * P:(i + 1) * P],
                                                   src[:, 4 * g + i, c * P:(c + 1) * P], e.ident)
                    last.then_inc(turned, 1)

            @block.vector
            def _(dve):
                for b, (c, g) in enumerate(groups):
                    if b % 2 == 0:
                        dve.wait_ge(turned, b + 1)
                        nc.vector.tensor_copy(dst[:, c, g * CH:(g + 1) * CH], e.ps[:, b, :])

            @block.scalar
            def _(act):
                for b, (c, g) in enumerate(groups):
                    if b % 2 == 1:
                        act.wait_ge(turned, b + 1)
                        nc.scalar.activation(dst[:, c, g * CH:(g + 1) * CH], e.ps[:, b, :], ACT.Copy)


def split_phase(nc, e, loads, jobs):
    work = [(w, bias, scale, src, dst, o, a, n)
            for w, bias, scale, src, length, dst in jobs
            for o in range(NC) for a, n in tiles(length, CH)]
    with phase(nc) as sem:
        loaded, made, whole, high, rest, middle, low = (sem(n) for n in (
            "loaded", "made", "whole", "high", "rest", "middle", "low"))
        stored = [sem(f"stored{i}") for i in range(2)]
        with nc.Block() as block:

            @block.sync
            def _(sp):
                for dst, src in loads:
                    sp.dma_start(dst, src).then_inc(loaded, 16)
                for i, (w, bias, scale, src, dst, o, a, n) in enumerate(work):
                    sp.wait_ge(low, i + 1)
                    sp.wait_ge(middle, i + 1)
                    sp.wait_ge(high, i + 1)
                    sp.dma_start(dst.rearrange("s r t -> r s t")[o * P:(o + 1) * P, :, a:a + n],
                                 e.parts[i % 2][:, :, 0:n]).then_inc(stored[i % 2], 16)
                for j in range(2):
                    sp.wait_ge(stored[j], 16 * len(range(j, len(work), 2)))

            @block.tensor
            def _(pe):
                if loads:
                    pe.wait_ge(loaded, 16 * len(loads))
                for i, (w, bias, scale, src, dst, o, a, n) in enumerate(work):
                    if i >= 8:
                        pe.wait_ge(whole, i - 7)
                    if w is None:
                        for t in range(n // P):
                            last = nc.tensor.transpose(e.ps[:, i % 8, t * P:(t + 1) * P],
                                                       src[:, a // P + t, o * P:(o + 1) * P], e.ident)
                    else:
                        for c in range(NC):
                            last = nc.tensor.matmul(e.ps[:, i % 8, 0:n], w[:, c, o * P:(o + 1) * P],
                                                    src[:, c, a:a + n], start=(c == 0), stop=(c == NC - 1))
                    last.then_inc(made, 1)

            @block.vector
            def _(dve):
                if loads:
                    dve.wait_ge(loaded, 16 * len(loads))
                for i, (w, bias, scale, src, dst, o, a, n) in enumerate(work):
                    dve.wait_ge(made, i + 1)
                    if i >= 2:
                        dve.wait_ge(high, i - 1)
                    full = e.whole[i % 2][:, 0:n]
                    if bias is None:
                        nc.vector.tensor_scalar(full, e.ps[:, i % 8, 0:n], scale, None, ALU.mult).then_inc(whole, 1)
                    else:
                        nc.vector.tensor_scalar(full, e.ps[:, i % 8, 0:n], bias[:, o:o + 1], scale,
                                                ALU.add, ALU.mult).then_inc(whole, 1)
                    dve.wait_ge(high, i + 1)
                    if i >= 2:
                        dve.wait_ge(low, i - 1)
                    nc.vector.tensor_tensor(e.rest[i % 2][:, 0:n], full, e.parts[i % 2][:, 0, 0:n],
                                            ALU.subtract).then_inc(rest, 1)

            @block.scalar
            def _(act):
                for i, (w, bias, scale, src, dst, o, a, n) in enumerate(work):
                    act.wait_ge(whole, i + 1)
                    if i >= 2:
                        act.wait_ge(stored[i % 2], 16 * (i // 2))
                    nc.scalar.activation(e.parts[i % 2][:, 0, 0:n], e.whole[i % 2][:, 0:n],
                                         ACT.Copy).then_inc(high, 1)
                    act.wait_ge(rest, i + 1)
                    nc.scalar.activation(e.parts[i % 2][:, 1, 0:n], e.rest[i % 2][:, 0:n],
                                         ACT.Copy).then_inc(middle, 1)

            @block.gpsimd
            def _(pool):
                for i, (w, bias, scale, src, dst, o, a, n) in enumerate(work):
                    pool.wait_ge(middle, i + 1)
                    nc.gpsimd.tensor_tensor(e.parts[i % 2][:, 2, 0:n], e.rest[i % 2][:, 0:n],
                                            e.parts[i % 2][:, 1, 0:n], ALU.subtract).then_inc(low, 1)


def value_phase(nc, e, loads, w, src, length, bias_row):
    with phase(nc) as sem:
        loaded = sem("loaded")
        made = sem("made")
        kept = sem("kept")
        with nc.Block() as block:

            @block.sync
            def _(sp):
                for dst, s in loads:
                    sp.dma_start(dst, s).then_inc(loaded, 16)

            @block.tensor
            def _(pe):
                if loads:
                    pe.wait_ge(loaded, 16 * len(loads))
                for t, (a, n) in enumerate(tiles(length, P)):
                    if t >= 8:
                        pe.wait_ge(kept, t - 7)
                    for c in range(NC):
                        last = nc.tensor.matmul(e.ps[0:n, t % 8, 0:D], src[:, c, a:a + n], w[:, c, :],
                                                start=(c == 0), stop=(c == NC - 1))
                    last.then_inc(made, 1)

            @block.vector
            def _(dve):
                if loads:
                    dve.wait_ge(loaded, 16 * len(loads))
                for t, (a, n) in enumerate(tiles(length, P)):
                    dve.wait_ge(made, t + 1)
                    if bias_row is None:
                        nc.vector.tensor_copy(e.vall[0:n, t, :], e.ps[0:n, t % 8, 0:D]).then_inc(kept, 1)
                    else:
                        nc.vector.tensor_tensor(e.vall[0:n, t, :], e.ps[0:n, t % 8, 0:D], bias_row[0:n, :],
                                                ALU.add).then_inc(kept, 1)


def mask_phase(nc, e):
    with phase(nc) as sem:
        nat_in = [sem(f"nat_in{i}") for i in range(2)]
        tr_in = [sem(f"tr_in{i}") for i in range(2)]
        nat_done = sem("nat_done")
        tr_done = sem("tr_done")
        with nc.Block() as block:
            keys = tiles(S2, P)

            @block.sync
            def _(sp):
                for t in range(NT):
                    if t >= 2:
                        sp.wait_ge(nat_done, t - 1)
                    sp.dma_start(e.mask_in[t % 2][:, 0:S2], e.d["mask"][t * P:(t + 1) * P, :]).then_inc(nat_in[t % 2], 16)
                    if t < NT2:
                        a, n = keys[t]
                        if t >= 2:
                            sp.wait_ge(tr_done, t - 1)
                        sp.dma_start(e.maskT_in[t % 2][0:n, :], e.d["maskT"][a:a + n, :]).then_inc(tr_in[t % 2], 16)

            @block.vector
            def _(dve):
                for t in range(NT):
                    dve.wait_ge(nat_in[t % 2], 16 * (t // 2 + 1))
                    nc.vector.tensor_scalar(e.mask_add[:, t, :], e.mask_in[t % 2][:, 0:S2], 0.0, MASKED,
                                            ALU.is_equal, ALU.mult).then_inc(nat_done, 1)
                    if t < NT2:
                        n = keys[t][1]
                        dve.wait_ge(tr_in[t % 2], 16 * (t // 2 + 1))
                        nc.vector.tensor_scalar(e.mask_one[0:n, t, :], e.maskT_in[t % 2][0:n, :], 0.0, None,
                                                ALU.is_equal, saturate=False).then_inc(tr_done, 1)


def attention_phase(nc, e, keys, causal, masked):
    steps = []
    for half in range(2):
        for t, (a, n) in enumerate(tiles(keys, P)):
            first = max(0, a - half * HALF) if causal else 0
            if first < HALF:
                steps.append((half, t, first, n))
    ns = len(steps)
    half_end = [max(i for i, s in enumerate(steps) if s[0] == half) for half in range(2)]
    units = []
    for t in range(NT):
        if causal:
            pieces = tiles((t + 1) * P, CH)
        else:
            n = -(-keys // CH)
            w = -(-keys // n)
            pieces = tiles(keys, w)
        units += [(t, i, a, w) for i, (a, w) in enumerate(pieces)]
    nu = len(units)
    pieces_max = max(u[1] for u in units) + 1
    begin, end = 4, ns - 5
    share = [0] * ns
    for i in range(nu):
        share[begin + i * (end - begin) // nu] += 1
    at_step = [(sum(share[:i]), sum(share[:i + 1])) for i in range(ns)]
    n_units = nu + 1
    p_slots = 4

    with phase(nc) as sem:
        stacks_in = sem("stacks_in")
        max_out, max_in = sem("max_out"), sem("max_in")
        unit_ready, unit_used, unit_seen = sem("unit_ready"), sem("unit_used"), sem("unit_seen")
        s_ready, exp_done, pv_done = sem("s_ready"), sem("exp_done"), sem("pv_done")
        v_ready = sem("v_ready")
        o_copied, o_turned, o_done = sem("o_copied"), sem("o_turned"), sem("o_done")
        max_chain = sem("max_chain")
        norm_chain = sem("norm_chain")
        mpart_set, ones_set = sem("mpart_set"), sem("ones_set")
        with nc.Block() as block:

            S_PS = [e.ps[:, 0:2, :].rearrange("p a b -> p (a b)"), e.ps[:, 2:4, :].rearrange("p a b -> p (a b)")]
            M_PS = [e.ps[:, 4, :], e.ps[:, 5, :]]
            O_PS = [e.ps[:, 6, :], e.ps[:, 7, :]]

            def heads(eng, body):
                body(0, 0, False)
                body(1, 1, False)
                with eng.Fori(1, H // 2 - 1) as pair:
                    body(2 * pair, 0, False)
                    body(2 * pair + 1, 1, False)
                body(H - 2, 0, False)
                body(H - 1, 1, True)

            @block.sync
            def _(sp):
                def load(h, par):
                    for stack, parts, src, n in ((e.ks[par], PARTS[0], e.kd, keys), (e.qs[par], PARTS[1], e.qd, S)):
                        for slot, part in enumerate(parts):
                            sp.dma_start(stack[slot * HD:(slot + 1) * HD, 0:n],
                                         src[part, bass.ds(h * HD, HD), 0:n]).then_inc(stacks_in, 16)

                def place_max(h, par):
                    sp.wait_ge(max_chain, h * 4 + 4)
                    if not isinstance(h, int) or h > 0:
                        sp.wait_ge(max_in, 16 * h)
                    sp.dma_start(e.md.rearrange("s t q -> t s q"), e.mrow).then_inc(max_out, 16)
                    sp.wait_ge(max_out, 16 * (h + 1))
                    sp.dma_start(e.qs[par][KQ:KM, :], e.md.rearrange("s t q -> s (t q)")).then_inc(max_in, 16)

                def body(h, par, last):
                    if last:
                        return
                    if not (isinstance(h, int) and h == 0):
                        sp.wait_ge(pv_done, h * ns)
                    load(h + 1, 1 - par)
                    place_max(h + 1, 1 - par)

                load(0, 0)
                place_max(0, 0)
                heads(sp, body)

            @block.gpsimd
            def _(pool):
                def values(h, par):
                    for t, k, n in [(0, keys // P, P)] + ([(keys // P, 1, keys % P)] if keys % P else []):
                        last = nc.gpsimd.tensor_copy(e.vbuf[par][0:n, t:t + k, 0:HD],
                                                     e.vall[0:n, t:t + k, bass.ds(h * HD, HD)])
                    last.then_inc(v_ready, 1)

                def body(h, par, last):
                    if last:
                        return
                    if not (isinstance(h, int) and h == 0):
                        pool.wait_ge(pv_done, h * ns)
                    values(h + 1, 1 - par)

                values(0, 0)
                heads(pool, body)

            @block.scalar
            def _(act):
                def body(h, par, last):
                    for i, (half, t, first, n) in enumerate(steps):
                        act.wait_ge(s_ready, h * ns + i + 1)
                        if not isinstance(h, int) or h * ns + i >= p_slots:
                            act.wait_ge(pv_done, h * ns + i - p_slots + 1)
                        slot = (par * ns + i) % p_slots
                        nc.scalar.activation(e.prob[slot][0:n, first:HALF], S_PS[i % 2][0:n, first:HALF],
                                             ACT.Exp).then_inc(exp_done, 1)
                heads(act, body)

            @block.tensor
            def _(pe):
                def unit(h, par, u):
                    t, i, a, w = units[u]
                    g = h * n_units + u
                    if not isinstance(h, int) or g >= 2:
                        pe.wait_ge(unit_used, g - 1)
                    diagonal = causal and a + w == (t + 1) * P
                    last = nc.tensor.matmul(M_PS[(par * n_units + u) % 2][:, 0:w], e.qs[par][0:KQ, t * P:(t + 1) * P],
                                            e.ks[par][0:KQ, a:a + w], start=True, stop=not diagonal)
                    if diagonal:
                        last = nc.tensor.matmul(M_PS[(par * n_units + u) % 2][:, w - P:w], e.ident16, e.upper16,
                                                start=False, stop=True)
                    last.then_inc(unit_ready, 1)

                def turn_max(h, par):
                    g = h * n_units + nu
                    pe.wait_ge(unit_used, g - 1)
                    pe.wait_ge(max_chain, h * 4 + 1)
                    nc.tensor.transpose(M_PS[(par * n_units + nu) % 2][0:NT, 0:P], e.mfin, e.ident).then_inc(unit_ready, 1)

                def scores(h, par, i):
                    half, t, first, n = steps[i]
                    if not isinstance(h, int) or h * ns + i >= 2:
                        pe.wait_ge(exp_done, h * ns + i - 1)
                    if i == 0:
                        pe.wait_ge(max_in, 16 * (h + 1))
                    kt = e.ks[par][0:KM, t * P:t * P + n]
                    on_diagonal = causal and t * P >= half * HALF
                    for b in range(2):
                        lo = max(first, b * CH)
                        if lo >= (b + 1) * CH:
                            continue
                        diagonal = on_diagonal and lo == first
                        last = nc.tensor.matmul(S_PS[i % 2][0:n, lo:(b + 1) * CH], kt,
                                                e.qs[par][0:KM, half * HALF + lo:half * HALF + (b + 1) * CH],
                                                start=True, stop=not (diagonal or masked))
                        if diagonal:
                            last = nc.tensor.matmul(S_PS[i % 2][0:n, lo:lo + P], e.ident16, e.lower16,
                                                    start=False, stop=True)
                        if masked:
                            last = nc.tensor.matmul(S_PS[i % 2][0:n, lo:(b + 1) * CH], e.big16[0:n, 0:n],
                                                    e.mask_one[0:n, t, half * HALF + lo:half * HALF + (b + 1) * CH],
                                                    start=False, stop=True)
                    last.then_inc(s_ready, 1)

                def product(h, par, i):
                    half, t, first, n = steps[i]
                    pe.wait_ge(exp_done, h * ns + i + 1)
                    if t == 0:
                        if half == 0:
                            pe.wait_ge(v_ready, h + 1)
                        if not isinstance(h, int) or h > 0:
                            pe.wait_ge(o_done, (h - 1) * 2 + half + 1)
                    slot = (par * ns + i) % p_slots
                    for j in range(4):
                        lo = max(first - j * SUB, 0)
                        if lo >= SUB:
                            continue
                        stop = t == (half * HALF + (j + 1) * SUB) // P - 1 if causal else i == half_end[half]
                        last = nc.tensor.matmul(O_PS[half][32 * j:32 * j + 32, lo:SUB], e.vbuf[par][0:n, t, :],
                                                e.prob[slot][0:n, j * SUB + lo:(j + 1) * SUB],
                                                start=(t == 0), stop=stop)
                    last.then_inc(pv_done, 1)

                def turn_out(h, half):
                    pe.wait_ge(o_copied, h * 2 + half + 1)
                    for c in range(2):
                        last = nc.tensor.transpose(O_PS[half][:, SUB + c * P:SUB + (c + 1) * P],
                                                   e.osb[half][:, c * P:(c + 1) * P], e.ident)
                    last.then_inc(o_turned, 1)

                def body(h, par, last):
                    for i in range(ns):
                        if i + 2 < ns:
                            scores(h, par, i + 2)
                        elif not last:
                            scores(h + 1, 1 - par, i + 2 - ns)
                        product(h, par, i)
                        if i == half_end[0] + 2:
                            turn_out(h, 0)
                        if not last:
                            if at_step[i][0] == 0 and at_step[i][1] > 0:
                                pe.wait_ge(stacks_in, 16 * 12 * (h + 2))
                            for u in range(*at_step[i]):
                                unit(h + 1, 1 - par, u)
                            if i == end - 1:
                                turn_max(h + 1, 1 - par)
                    turn_out(h, 1)

                pe.wait_ge(stacks_in, 16 * 12)
                for u in range(nu):
                    unit(0, 0, u)
                turn_max(0, 0)
                pe.wait_ge(ones_set, 2)
                scores(0, 0, 0)
                scores(0, 0, 1)
                heads(pe, body)

            @block.vector
            def _(dve):
                def unit(h, par, u):
                    t, i, a, w = units[u]
                    dve.wait_ge(unit_ready, h * n_units + u + 1)
                    if masked:
                        if not isinstance(h, int) or h * n_units + u >= 4:
                            dve.wait_ge(unit_used, h * n_units + u - 3)
                        dve.sem_inc(unit_seen, 1)
                    src = M_PS[(par * n_units + u) % 2][:, 0:w]
                    if masked:
                        nc.vector.tensor_tensor_reduce(out=e.scrap[:, u % 4, 0:w], in0=src, in1=e.mask_add[:, t, a:a + w],
                                                       scale=1.0, scalar=-3.0e38, op0=ALU.add, op1=ALU.max,
                                                       accum_out=e.mpart[:, t, i:i + 1]).then_inc(unit_used, 1)
                    else:
                        nc.vector.tensor_reduce(e.mpart[:, t, i:i + 1], src, AX, ALU.max).then_inc(unit_used, 1)

                def finish_max(h, par):
                    chain = Chain(dve, max_chain, h * 4)
                    dve.wait_ge(unit_used, h * n_units + nu)
                    chain.link(nc.vector.tensor_reduce(e.mfin, e.mpart[:, :, 0:pieces_max], AX, ALU.max))
                    dve.wait_ge(unit_ready, h * n_units + nu + 1)
                    turned = M_PS[(par * n_units + nu) % 2][0:NT, 0:P]
                    if not isinstance(h, int) or h > 0:
                        dve.wait_ge(max_out, 16 * h)
                    chain.link(nc.vector.tensor_scalar(e.mrow[:, 0, :], turned, -1.0, None, ALU.mult))
                    chain.link(nc.vector.scalar_tensor_tensor(out=e.mrest, in0=turned, scalar=-1.0,
                                                              in1=e.mrow[:, 0, :], op0=ALU.mult, op1=ALU.subtract))
                    nc.vector.tensor_copy(e.mrow[:, 1, :], e.mrest).then_inc(unit_used, 1)
                    dve.wait_ge(unit_used, h * n_units + nu + 1)
                    chain.link(nc.vector.tensor_tensor(e.mrow[:, 2, :], e.mrest, e.mrow[:, 1, :], ALU.subtract))

                def copy_out(h, half):
                    dve.wait_ge(pv_done, h * ns + half_end[half] + 1)
                    nc.vector.tensor_copy(e.osb[half], O_PS[half][:, 0:SUB]).then_inc(o_copied, 1)

                def normalise(h, half):
                    dve.wait_ge(o_turned, h * 2 + half + 1)
                    turned = O_PS[half][:, SUB:2 * SUB].rearrange("p (c j r) -> p j c r", c=2, j=4)
                    nc.vector.reciprocal(e.rsum, turned[:, :, :, HD]).then_inc(norm_chain, 1)
                    dve.wait_ge(norm_chain, h * 2 + half + 1)
                    out = e.cn[:, half * 8:half * 8 + 8, bass.ds(h * HD, HD)].rearrange("p (j c) d -> p j c d", j=4)
                    nc.vector.tensor_tensor(out, turned[:, :, :, 0:HD],
                                            e.rsum.unsqueeze(3).broadcast_to([P, 4, 2, HD]), ALU.mult).then_inc(o_done, 1)

                def body(h, par, last):
                    for i in range(ns):
                        if i == half_end[0] + 2:
                            copy_out(h, 0)
                        if not last:
                            for u in range(*at_step[i]):
                                unit(h + 1, 1 - par, u)
                            if i == end - 1:
                                finish_max(h + 1, 1 - par)
                        if i == half_end[0] + 3:
                            normalise(h, 0)
                    copy_out(h, 1)
                    normalise(h, 1)

                nc.vector.memset(e.mpart, -3.0e38).then_inc(mpart_set, 1)
                for par in range(2):
                    nc.vector.memset(e.ks[par][KQ:KM, :], 1.0).then_inc(ones_set, 1)
                dve.wait_ge(mpart_set, 1)
                for u in range(nu):
                    unit(0, 0, u)
                finish_max(0, 0)
                heads(dve, body)


def rope_phase(nc, e):
    G = 4
    N = G * 2 * H
    groups = NT // G
    with phase(nc) as sem:
        loaded, made, centred, squared, spread, rooted, inverse, scaled = (sem(n) for n in (
            "loaded", "made", "centred", "squared", "spread", "rooted", "inverse", "scaled"))
        chain_sem, pool_sem, spread_tables = sem("chain"), sem("pool_chain"), sem("spread_tables")
        with nc.Block() as block:
            loads = [(e.w_a[:, :, 0:D], e.d["L0_attn_Wq"]), (e.w_a[:, :, D:2 * D], e.d["L0_attn_Wk"]),
                     (e.rope_cos, e.d["rope_cos"].rearrange("(t p) c -> p t c", p=P)),
                     (e.rope_sin, e.d["rope_sin"].rearrange("(t p) c -> p t c", p=P))]
            small = [(e.gamma_s[:, 0, :], "L0_attn_q_gamma"), (e.gamma_s[:, 1, :], "L0_attn_k_gamma"),
                     (e.beta_s[:, 0, :], "L0_attn_q_beta"), (e.beta_s[:, 1, :], "L0_attn_k_beta")]
            n_loads = len(loads) + len(small)

            def group_ps(g):
                return e.ps[:, (g % 2) * G:(g % 2) * G + G, :].rearrange("p t (r d) -> p (t r) d", d=HD)

            def rows(tile):
                return tile.rearrange("p (r d) -> p r d", d=HD)

            @block.sync
            def _(sp):
                for dst, src in loads[:2]:
                    sp.dma_start(dst, src.rearrange("(k p) o -> p k o", p=P)).then_inc(loaded, 16)
                for dst, src in loads[2:]:
                    sp.dma_start(dst, src).then_inc(loaded, 16)
                for dst, name in small:
                    sp.dma_start(dst, e.d[name].partition_broadcast(P)).then_inc(loaded, 16)

            @block.tensor
            def _(pe):
                pe.wait_ge(loaded, 16 * n_loads)
                for g in range(groups):
                    if g >= 2:
                        pe.wait_ge(centred, g - 1)
                    for i in range(G):
                        t = g * G + i
                        for c in range(NC):
                            last = nc.tensor.matmul(e.ps[:, (g % 2) * G + i, :], e.xT[:, c, t * P:(t + 1) * P],
                                                    e.w_a[:, c, :], start=(c == 0), stop=(c == NC - 1))
                    last.then_inc(made, 1)

            @block.scalar
            def _(act):
                for g in range(groups):
                    act.wait_ge(centred, g + 1)
                    if g >= 2:
                        act.wait_ge(spread, g - 1)
                    nc.scalar.activation(e.r_sq[g % 2], e.r_xc[g % 2], ACT.Square).then_inc(squared, 1)
                    act.wait_ge(spread, g + 1)
                    nc.scalar.activation(e.r_std[g % 2], e.r_var[g % 2], ACT.Sqrt, bias=e.eps5, scale=1.0 / HD).then_inc(rooted, 1)

            @block.gpsimd
            def _(pool):
                chain = Chain(pool, pool_sem)
                for g in range(groups):
                    pool.wait_ge(inverse, g + 1)
                    xc = e.r_xc[g % 2]
                    chain.link(nc.gpsimd.tensor_tensor(rows(xc), rows(xc), e.r_inv[g % 2].unsqueeze(2).broadcast_to([P, N, HD]), ALU.mult))
                    four = xc.rearrange("p (t c) -> p t c", t=G)
                    if g == 0:
                        pool.wait_ge(spread_tables, 1)
                    chain.link(nc.gpsimd.tensor_tensor(four, four, e.gamma.unsqueeze(1).broadcast_to([P, G, 2 * D]), ALU.mult))
                    nc.gpsimd.tensor_tensor(four, four, e.beta.unsqueeze(1).broadcast_to([P, G, 2 * D]), ALU.add).then_inc(scaled, 1)

            @block.vector
            def _(dve):
                chain = Chain(dve, chain_sem)
                dve.wait_ge(loaded, 16 * n_loads)
                for table, src in ((e.gamma, e.gamma_s), (e.beta, e.beta_s)):
                    last = nc.vector.tensor_copy(table.rearrange("p (a h d) -> p a h d", a=2, d=HD),
                                                 src.unsqueeze(2).broadcast_to([P, 2, H, HD]))
                last.then_inc(spread_tables, 1)

                def norm(g):
                    ps = group_ps(g)
                    dve.wait_ge(made, g + 1)
                    chain.link(nc.vector.tensor_reduce(e.r_sum[g % 2], ps, AX, ALU.add))
                    nc.vector.scalar_tensor_tensor(out=rows(e.r_xc[g % 2]), in0=e.r_sum[g % 2].unsqueeze(2).broadcast_to([P, N, HD]),
                                                   scalar=-1.0 / HD, in1=ps, op0=ALU.mult, op1=ALU.add).then_inc(centred, 1)
                    dve.wait_ge(squared, g + 1)
                    if g >= 2:
                        dve.wait_ge(rooted, g - 1)
                    nc.vector.tensor_reduce(e.r_var[g % 2], rows(e.r_sq[g % 2]), AX, ALU.add).then_inc(spread, 1)
                    dve.wait_ge(rooted, g + 1)
                    nc.vector.reciprocal(e.r_inv[g % 2], e.r_std[g % 2]).then_inc(inverse, 1)

                def rotate(g):
                    dve.wait_ge(scaled, g + 1)
                    x = e.r_xc[g % 2].rearrange("p (t r d) -> p t r d", t=G, d=HD)
                    pairs = e.r_xc[g % 2].rearrange("p (t r d two) -> p t r d two", t=G, two=2, d=HD // 2)
                    out = e.qkn[:, g * G:(g + 1) * G, :].rearrange("p t (r d) -> p t r d", d=HD)
                    tmp = e.r_sq[g % 2].rearrange("p (t r d) -> p t r d", t=G, d=HD)
                    ts = slice(g * G, (g + 1) * G)
                    for t in range(G):
                        c = e.rope_cos[:, g * G + t, :].unsqueeze(1).broadcast_to([P, 2 * H, HD])
                        s = e.rope_sin[:, g * G + t, :].unsqueeze(1).broadcast_to([P, 2 * H, HD])
                        nc.vector.tensor_tensor(out[:, t], x[:, t], c, ALU.mult)
                        nc.vector.tensor_tensor(tmp[:, t, :, 0:HD // 2], pairs[:, t, :, :, 1], s[:, :, 0:HD // 2], ALU.mult)
                        last = nc.vector.tensor_tensor(tmp[:, t, :, HD // 2:], pairs[:, t, :, :, 0], s[:, :, HD // 2:], ALU.mult)
                    chain.link(last)
                    chain.link(nc.vector.tensor_tensor(e.qkn[:, ts, :].rearrange("p t c -> p (t c)"),
                                                       e.qkn[:, ts, :].rearrange("p t c -> p (t c)"), e.r_sq[g % 2], ALU.add))

                norm(0)
                for g in range(groups):
                    if g + 1 < groups:
                        norm(g + 1)
                    rotate(g)


def output_phase(nc, e, loads, products, addend, bias_row, total, normed, eps, scale=None):
    with phase(nc) as sem:
        loaded, made, used, biased = sem("loaded"), sem("made"), sem("used"), sem("biased")
        measured, rooted, chain_sem, stored = sem("measured"), sem("rooted"), sem("chain"), sem("stored")
        normed_sem = sem("normed")
        with nc.Block() as block:
            store = normed is None
            dst = e.cn if store else normed

            @block.sync
            def _(sp):
                for d, s in loads:
                    sp.dma_start(d, s).then_inc(loaded, 16)
                if store:
                    for t in range(0, NT, 4):
                        sp.wait_ge(normed_sem, t + 4)
                        sp.dma_start(e.out.rearrange("(t p) c -> p t c", p=P)[:, t:t + 4, :],
                                     dst[:, t:t + 4, :]).then_inc(stored, 16)
                    sp.wait_ge(stored, 16 * NT // 4)

            @block.gpsimd
            def _(pool):
                if bias_row is not None and scale is None:
                    pool.wait_ge(loaded, 16 * len(loads))
                    for t in range(NT):
                        nc.gpsimd.tensor_tensor(total[:, t, :], addend[:, t, :], bias_row, ALU.add).then_inc(biased, 1)

            @block.tensor
            def _(pe):
                if products is None:
                    return
                if loads:
                    pe.wait_ge(loaded, 16 * len(loads))
                for t in range(NT):
                    if t >= 8:
                        pe.wait_ge(used, t - 7)
                    products(t, e.ps[:, t % 8, 0:D]).then_inc(made, 1)

            @block.vector
            def _(dve):
                chain = Chain(dve, chain_sem)
                if loads:
                    dve.wait_ge(loaded, 16 * len(loads))
                for t in range(NT):
                    y = total[:, t, :]
                    if products is not None:
                        dve.wait_ge(made, t + 1)
                        ps = e.ps[:, t % 8, 0:D]
                        if scale is not None:
                            nc.vector.scalar_tensor_tensor(out=e.rounded[t % 2], in0=ps, scalar=scale, in1=bias_row,
                                                           op0=ALU.mult, op1=ALU.add).then_inc(used, 1)
                            dve.wait_ge(used, t + 1)
                            chain.link(nc.vector.tensor_tensor(y, addend[:, t, :], e.rounded[t % 2], ALU.add))
                        else:
                            a = addend
                            if bias_row is not None:
                                dve.wait_ge(biased, t + 1)
                                a = total
                            nc.vector.tensor_tensor(y, ps, a[:, t, :], ALU.add).then_inc(used, 1)
                            dve.wait_ge(used, t + 1)
                    chain.link(nc.vector.bn_stats(e.stats[:, t, :], y))
                    last = nc.vector.bn_aggr(e.mv[:, t, :], e.stats[:, t, :])
                last.then_inc(measured, 1)
                dve.wait_ge(rooted, 1)
                chain.link(nc.vector.reciprocal(e.rstd, e.std))
                for t in range(NT):
                    nc.vector.tensor_scalar(dst[:, t, :], total[:, t, :], e.mv[:, t, 0:1], e.rstd[:, t:t + 1],
                                            ALU.subtract, ALU.mult).then_inc(normed_sem, 1)

            @block.scalar
            def _(act):
                act.wait_ge(measured, 1)
                nc.scalar.activation(e.std, e.mv[:, :, 1], ACT.Sqrt, bias=eps).then_inc(rooted, 1)


def fp8_phase(nc, e):
    with phase(nc) as sem:
        loaded, amax, chain_sem, reduced = sem("loaded"), sem("amax"), sem("chain"), sem("reduced")
        with nc.Block() as block:
            w = e.w_a[:, :, 0:D]
            jobs = [(e.xT[:, c, a:a + n], e.xq[:, c, a:a + n], 0) for c in range(NC) for a, n in tiles(S, CH)]
            jobs += [(w[:, c, :], e.wq[:, c, :], 1) for c in range(NC)]

            @block.sync
            def _(sp):
                sp.dma_start(w, e.d["L0_ffn_weight"].rearrange("(k p) o -> p k o", p=P)).then_inc(loaded, 16)
                sp.dma_start(e.b_row, e.d["L0_ffn_bias"].partition_broadcast(P)).then_inc(loaded, 16)

            @block.gpsimd
            def _(pool):
                pool.wait_ge(amax, 2)
                nc.gpsimd.partition_all_reduce(e.amax_all, e.amax, P, RMAX).then_inc(reduced, 1)

            @block.vector
            def _(dve):
                chain = Chain(dve, chain_sem)
                nc.vector.tensor_reduce(e.amax[:, 0:1], e.x_nat.rearrange("p t c -> p (t c)"), AX, ALU.max,
                                        apply_absolute_value=True).then_inc(amax, 1)
                dve.wait_ge(loaded, 32)
                nc.vector.tensor_reduce(e.amax[:, 1:2], w, mybir.AxisListType.XY, ALU.max,
                                        apply_absolute_value=True).then_inc(amax, 1)
                dve.wait_ge(reduced, 1)
                chain.link(nc.vector.tensor_scalar(e.amax_all, e.amax_all, 1e-12, None, ALU.max))
                chain.link(nc.vector.reciprocal(e.qscale, e.amax_all))
                chain.link(nc.vector.tensor_scalar(e.qscale, e.qscale, 448.0, 448.0, ALU.mult, ALU.min))
                chain.link(nc.vector.reciprocal(e.descale, e.qscale))
                chain.link(nc.vector.tensor_tensor(e.descale2, e.descale[:, 0:1], e.descale[:, 1:2], ALU.mult))
                for i, (src, dst, which) in enumerate(jobs):
                    n = src.shape[1]
                    v, m = e.whole[i % 2][:, 0:n], e.rest[i % 2][:, 0:n]
                    chain.link(nc.vector.tensor_scalar(v, src, e.qscale[:, which:which + 1], 448.0, ALU.mult, ALU.min))
                    chain.link(nc.vector.tensor_scalar(v, v, -448.0, None, ALU.max))
                    chain.link(nc.vector.tensor_scalar(m.bitcast(I32), v.bitcast(I32), 0x7F800000, None, ALU.bitwise_and))
                    chain.link(nc.vector.tensor_scalar(m, m, 2.0 ** -6, 1.5 * 2.0 ** 20, ALU.max, ALU.mult))
                    chain.link(nc.vector.tensor_tensor(v, v, m, ALU.add))
                    chain.link(nc.vector.tensor_tensor(dst, v, m, ALU.subtract))


def mlp_phase(nc, e):
    nf = FF // P
    with phase(nc) as sem:
        loaded, up_ready, act_done, down_ready, added = (sem(n) for n in (
            "loaded", "up_ready", "act_done", "down_ready", "added"))
        with nc.Block() as block:
            chunks = tiles(S, CH)

            @block.sync
            def _(sp):
                sp.dma_start(e.w_fc, e.d["L1_attn_w_fc"].rearrange("(k p) o -> p k o", p=P)).then_inc(loaded, 16)
                sp.dma_start(e.w_mp, e.d["L1_attn_w_mlp_proj"].rearrange("(k p) o -> p k o", p=P)).then_inc(loaded, 16)
                sp.dma_start(e.b_fc, e.d["L1_attn_b_fc_col"]).then_inc(loaded, 16)

            @block.tensor
            def _(pe):
                pe.wait_ge(loaded, 48)

                def up(i, a):
                    for f in range(nf):
                        g = i * nf + f
                        if g >= 4:
                            pe.wait_ge(act_done, g - 3)
                        for c in range(NC):
                            last = nc.tensor.matmul(e.ps[:, g % 4, :], e.w_fc[:, c, f * P:(f + 1) * P],
                                                    e.xT[:, c, a:a + CH], start=(c == 0), stop=(c == NC - 1))
                        last.then_inc(up_ready, 1)

                def down(i):
                    pe.wait_ge(act_done, (i + 1) * nf)
                    for t in range(4):
                        g = i * 4 + t
                        if g >= 4:
                            pe.wait_ge(added, g - 3)
                        for f in range(nf):
                            last = nc.tensor.matmul(e.ps[:, 4 + g % 4, 0:D], e.hT[i % 2][:, f, t * P:(t + 1) * P],
                                                    e.w_mp[:, f, :], start=(f == 0), stop=(f == nf - 1))
                        last.then_inc(down_ready, 1)

                for i, (a, n) in enumerate(chunks):
                    up(i, a)
                    if i:
                        down(i - 1)
                down(len(chunks) - 1)

            @block.scalar
            def _(act):
                act.wait_ge(loaded, 48)
                for i in range(len(chunks)):
                    if i >= 2:
                        act.wait_ge(down_ready, (i - 1) * 4)
                    for f in range(nf):
                        act.wait_ge(up_ready, i * nf + f + 1)
                        nc.scalar.activation(e.hT[i % 2][:, f, :], e.ps[:, (i * nf + f) % 4, :], ACT.Gelu_apprx_tanh,
                                             bias=e.b_fc[:, f:f + 1]).then_inc(act_done, 1)

            @block.vector
            def _(dve):
                for t in range(NT):
                    dve.wait_ge(down_ready, t + 1)
                    nc.vector.tensor_tensor(e.vall[:, t, :], e.vall[:, t, :], e.ps[:, 4 + t % 4, 0:D],
                                            ALU.add).then_inc(added, 1)


def gate_phase(nc, e):
    E = NE - 1
    with phase(nc) as sem:
        loaded, made, exped, chain_sem, copied = sem("loaded"), sem("made"), sem("exped"), sem("chain"), sem("copied")
        centred = sem("centred")
        with nc.Block() as block:
            shape3, shape4 = [P, NT, E], [P, NT, E, E]

            @block.sync
            def _(sp):
                sp.dma_start(e.w_gate, e.d["L1_ffn_gate_w"].rearrange("(k p) o -> p k o", p=P)).then_inc(loaded, 16)
                sp.dma_start(e.b_gate, e.d["L1_ffn_gate_bias"].partition_broadcast(P)).then_inc(loaded, 16)
                sp.dma_start(e.below, e.d["below"].partition_broadcast(P)).then_inc(loaded, 16)

            @block.gpsimd
            def _(pool):
                nc.gpsimd.tensor_copy(e.cn, e.x_nat).then_inc(copied, 1)

            @block.tensor
            def _(pe):
                pe.wait_ge(loaded, 48)
                for t in range(NT):
                    for c in range(NC):
                        last = nc.tensor.matmul(e.ps[:, 0, t * E:(t + 1) * E], e.xT[:, c, t * P:(t + 1) * P],
                                                e.w_gate[:, c, :], start=(c == 0), stop=(c == NC - 1))
                last.then_inc(made, 1)

            @block.scalar
            def _(act):
                act.wait_ge(centred, 1)
                nc.scalar.activation(e.g_p, e.g_p, ACT.Exp).then_inc(exped, 1)

            @block.vector
            def _(dve):
                chain = Chain(dve, chain_sem)
                logits = e.ps[:, 0, 0:NT * E].rearrange("p (t e) -> p t e", e=E)
                nc.vector.memset(e.comb, 1.0).then_inc(chain_sem, 1)
                chain.n += 1
                dve.wait_ge(loaded, 48)
                dve.wait_ge(made, 1)
                chain.link(nc.vector.tensor_reduce(e.g_r, logits, AX, ALU.max))
                nc.vector.tensor_tensor(e.g_p, logits, e.g_r.unsqueeze(2).broadcast_to(shape3), ALU.subtract).then_inc(centred, 1)
                dve.wait_ge(exped, 1)
                chain.link(nc.vector.tensor_reduce(e.g_r, e.g_p, AX, ALU.add))
                chain.link(nc.vector.reciprocal(e.g_r, e.g_r))
                chain.link(nc.vector.tensor_tensor(e.g_p, e.g_p, e.g_r.unsqueeze(2).broadcast_to(shape3), ALU.mult))
                chain.link(nc.vector.tensor_tensor(e.g_b, e.g_p, e.b_gate.unsqueeze(1).broadcast_to(shape3), ALU.add))
                rival = e.g_b.unsqueeze(2).broadcast_to(shape4)
                own = e.g_b.unsqueeze(3).broadcast_to(shape4)
                chain.link(nc.vector.tensor_tensor(e.g_eq, rival, own, ALU.is_equal))
                chain.link(nc.vector.tensor_tensor(e.g_eq.rearrange("p t i j -> p t (i j)"), e.g_eq.rearrange("p t i j -> p t (i j)"),
                                                   e.below.unsqueeze(1).broadcast_to([P, NT, E * E]), ALU.mult))
                chain.link(nc.vector.tensor_tensor(e.g_gt, rival, own, ALU.is_gt))
                chain.link(nc.vector.tensor_tensor(e.g_gt, e.g_gt, e.g_eq, ALU.add))
                chain.link(nc.vector.tensor_reduce(e.g_b, e.g_gt, AX, ALU.add))
                chain.link(nc.vector.tensor_scalar(e.g_b, e.g_b, 2.0, None, ALU.is_lt))
                chain.link(nc.vector.tensor_tensor(e.comb[:, :, 0:E], e.g_b, e.g_p, ALU.mult))


def moe_phase(nc, e):
    ni = INTER // P
    nch = S // CH
    with phase(nc) as sem:
        weights_in = sem("weights_in")
        weight_col = sem("weight_col")
        ab_ready, silu_done, h_done, y_ready, y_added = (sem(n) for n in (
            "ab_ready", "silu_done", "h_done", "y_ready", "y_added"))
        with nc.Block() as block:

            def experts(eng, body):
                body(0, 0, True)
                body(1, 1, False)
                body(2, 0, False)
                with eng.Fori(1, (NE - 1) // 2) as pair:
                    body(2 * pair + 1, 1, False)
                    body(2 * pair + 2, 0, False)

            @block.sync
            def _(sp):
                def load(x, par):
                    for dst, name in zip(e.moe_w[par], ("w1", "w3", "w2")):
                        src = e.d["moe_" + name]
                        rows = src.shape[0] // NE
                        sp.dma_start(dst, src[bass.ds(x * rows, rows), :].rearrange("(k p) o -> p k o", p=P)).then_inc(weights_in, 16)

                load(0, 0)
                load(1, 1)
                with sp.Fori(0, (NE - 1) // 2 - 1) as pair:
                    for j in range(2):
                        sp.wait_ge(y_ready, (2 * pair + 1 + j) * NT)
                        load(2 * pair + 2 + j, j)
                sp.wait_ge(y_ready, (NE - 2) * NT)
                load(NE - 1, 0)

            @block.gpsimd
            def _(pool):
                def body(x, par, first):
                    if not (isinstance(x, int) and x < 2):
                        pool.wait_ge(y_added, (x - 1) * NT)
                    nc.gpsimd.tensor_copy(e.comb_x[par], e.comb[:, :, bass.ds(x, 1)].rearrange("p t o -> p (t o)")
                                          ).then_inc(weight_col, 1)
                body(0, 0, True)
                body(1, 1, True)
                body(2, 0, False)
                with pool.Fori(1, (NE - 1) // 2) as pair:
                    body(2 * pair + 1, 1, False)
                    body(2 * pair + 2, 0, False)

            @block.tensor
            def _(pe):
                def up(x, par, c):
                    w1, w3, w2 = e.moe_w[par]
                    for i in range(ni):
                        k = x * nch * ni + c * ni + i
                        if not (isinstance(x, int) and k < 2):
                            pe.wait_ge(h_done, k - 1)
                        for b, w in enumerate((w1, w3)):
                            for h in range(NC):
                                last = nc.tensor.matmul(e.ps[:, 2 * (i % 2) + b, :], w[:, h, i * P:(i + 1) * P],
                                                        e.xT[:, h, c * CH:(c + 1) * CH], start=(h == 0), stop=(h == NC - 1))
                        last.then_inc(ab_ready, 1)

                def down(x, par, c):
                    w2 = e.moe_w[par][2]
                    pe.wait_ge(h_done, x * nch * ni + (c + 1) * ni)
                    for t in range(4):
                        g = x * NT + c * 4 + t
                        if not (isinstance(x, int) and g < 4):
                            pe.wait_ge(y_added, g - 3)
                        for i in range(ni):
                            last = nc.tensor.matmul(e.ps[:, 4 + t, 0:D], e.moe_h[c % 2][:, i, t * P:(t + 1) * P],
                                                    w2[:, i, :], start=(i == 0), stop=(i == ni - 1))
                        last.then_inc(y_ready, 1)

                def body(x, par, first):
                    for c in range(nch):
                        if c == 0:
                            pe.wait_ge(weights_in, 16 * 3 * (x + 1) if not first else 16 * 6)
                        up(x, par, c)
                        if c:
                            down(x, par, c - 1)
                        elif not first:
                            down(x - 1, 1 - par, nch - 1)
                experts(pe, body)
                down(NE - 1, 0, nch - 1)

            @block.scalar
            def _(act):
                def body(x, par, first):
                    for c in range(nch):
                        for i in range(ni):
                            k = x * nch * ni + c * ni + i
                            act.wait_ge(ab_ready, k + 1)
                            if not (isinstance(x, int) and k < 2):
                                act.wait_ge(h_done, k - 1)
                            nc.scalar.activation(e.moe_s[i % 2], e.ps[:, 2 * (i % 2), :], ACT.Silu).then_inc(silu_done, 1)
                experts(act, body)

            @block.vector
            def _(dve):
                def gated(x, par, c):
                    if not (isinstance(x, int) and x * nch + c < 2):
                        dve.wait_ge(y_ready, x * NT + (c - 1) * 4)
                    for i in range(ni):
                        dve.wait_ge(silu_done, x * nch * ni + c * ni + i + 1)
                        nc.vector.tensor_tensor(e.moe_h[c % 2][:, i, :], e.moe_s[i % 2], e.ps[:, 2 * (i % 2) + 1, :],
                                                ALU.mult).then_inc(h_done, 1)

                def add(x, par, c):
                    dve.wait_ge(weight_col, x + 1)
                    for t in range(4):
                        g = x * NT + c * 4 + t
                        dve.wait_ge(y_ready, g + 1)
                        tile = e.cn[:, c * 4 + t, :]
                        if not (isinstance(x, int) and x == 0):
                            dve.wait_ge(y_added, g + 1 - NT)
                        nc.vector.scalar_tensor_tensor(out=tile, in0=e.ps[:, 4 + t, 0:D],
                                                       scalar=e.comb_x[par][:, c * 4 + t:c * 4 + t + 1], in1=tile,
                                                       op0=ALU.mult, op1=ALU.add).then_inc(y_added, 1)

                def body(x, par, first):
                    for c in range(nch):
                        gated(x, par, c)
                        if c:
                            add(x, par, c - 1)
                        elif not first:
                            add(x - 1, 1 - par, nch - 1)
                experts(dve, body)
                add(NE - 1, 0, nch - 1)


def build(nc, dram, out):
    e = Env()
    e.d, e.out = dram, out
    with ExitStack() as ctx:
        def sb(name, cols, dt=F32, rows=P):
            return ctx.enter_context(nc.sbuf_tensor(name, [rows, cols], dt))[:, :]

        def dr(name, shape, dt):
            return nc.dram_tensor(name, shape, dt, kind="Internal").ap()

        e.qd, e.kd = dr("q_parts", (3, D, S), BF16), dr("k_parts", (3, D, S), BF16)
        e.md = dr("max_parts", (3, NT, P), BF16)

        def natural(ap):
            return ap.rearrange("p (t c) -> p t c", c=D)

        def halves(ap):
            return ap.rearrange("p (k n) -> p k n", k=NC)

        e.x_nat = natural(sb("x_nat", NT * D))
        e.xT = halves(sb("xT", NC * S))
        e.cn = natural(sb("cn", NT * D))
        e.vall = natural(sb("vall", NT * D))
        arena = sb("arena", 19500)
        stacks = sb("stacks", 4096)
        probs = sb("probs", 4 * HALF)
        vbufs = sb("vbufs", 2 * NT * 32)
        wbuf = sb("wbuf", 4 * 2 * D)
        e.vbuf = [vbufs[:, i * NT * 32:(i + 1) * NT * 32].rearrange("p (t r) -> p t r", r=32) for i in range(2)]
        e.osb = [sb(f"osb{i}", SUB) for i in range(2)]
        e.ident = sb("ident", P)
        e.ident16, e.big16 = sb("ident16", P, BF16), sb("big16", P, BF16)
        e.upper16, e.lower16 = sb("upper16", P, BF16), sb("lower16", P, BF16)
        e.w_a = halves(wbuf[:, 0:1024])
        e.w_v = halves(wbuf[:, 1024:1536])
        e.w_o = halves(wbuf[:, 1536:2048])
        e.b_row = sb("b_row", D)
        e.bv_row = sb("bv_row", D)
        bcol = sb("bcol", 4)
        e.bq_col, e.bk_col = bcol[:, 0:2], bcol[:, 2:4]
        e.mpart = sb("mpart", NT * 4).rearrange("p (t i) -> p t i", i=4)
        e.mfin = sb("mfin", NT)
        e.mrow = sb("mrow", 3 * P, BF16, NT).rearrange("t (s q) -> t s q", s=3)
        e.mrest = sb("mrest", P, F32, NT)
        e.rsum = sb("rsum", 8).rearrange("p (j c) -> p j c", j=4)
        e.scrap = sb("scrap", 4 * CH, BF16).rearrange("p (s n) -> p s n", s=4)
        e.stats = sb("stats", NT * 6).rearrange("p (t s) -> p t s", s=6)
        e.mv = sb("mv", NT * 2).rearrange("p (t s) -> p t s", s=2)
        e.std, e.rstd = sb("std", NT), sb("rstd", NT)
        small = sb("small", 16)
        e.eps5, e.eps10 = small[:, 0:1], small[:, 1:2]
        e.amax, e.amax_all = small[:, 2:4], small[:, 4:6]
        e.qscale, e.descale, e.descale2 = small[:, 8:10], small[:, 10:12], small[:, 12:13]
        rounded = sb("rounded", 2 * D, BF16)
        e.rounded = [rounded[:, i * D:(i + 1) * D] for i in range(2)]
        e.ps = ctx.enter_context(nc.psum_tensor("ps", [P, 8, CH], F32))

        s16 = stacks.bitcast(BF16)
        e.ks = [s16[:, i * S:(i + 1) * S] for i in range(2)]
        e.qs = [s16[:, (2 + i) * S:(3 + i) * S] for i in range(2)]
        e.prob = [probs[:, i * HALF:(i + 1) * HALF] for i in range(4)]
        e.ctxT = probs[:, 0:NC * S2].rearrange("p (k n) -> p k n", k=NC)
        cut = stacks[:, 0:7 * CH]
        e.whole = [cut[:, i * CH:(i + 1) * CH] for i in range(2)]
        e.rest = [cut[:, (2 + i) * CH:(3 + i) * CH] for i in range(2)]
        c16 = cut[:, 2048:3584].bitcast(BF16)
        e.parts = [c16[:, i * 3 * CH:(i + 1) * 3 * CH].rearrange("p (s n) -> p s n", s=3) for i in range(2)]

        e.mask_add = arena[:, 0:NT * S2 // 2].bitcast(BF16).rearrange("p (t n) -> p t n", t=NT)
        at = NT * S2 // 2
        e.mask_one = arena[:, at:at + NT2 * S // 4].bitcast(FP8).rearrange("p (t n) -> p t n", t=NT2)
        p32 = probs.bitcast(I32)
        e.mask_in = [p32[:, i * S2:(i + 1) * S2] for i in range(2)]
        e.maskT_in = [e.cn.rearrange("p t c -> p (t c)").bitcast(I32)[:, i * S:(i + 1) * S] for i in range(2)]

        e.wide = arena[:, 0:3 * P]

        a = 0

        def take(n):
            nonlocal a
            a += n
            return arena[:, a - n:a]
        e.qkn = take(NT * 2 * D).rearrange("p (t c) -> p t c", t=NT)
        e.r_xc, e.r_sq = [take(2048) for _ in range(2)], [take(2048) for _ in range(2)]
        e.rope_cos, e.rope_sin = e.vall[:, 0], e.vall[:, 1]
        e.rope_cos, e.rope_sin = (v.rearrange("p (t d) -> p t d", t=NT) for v in (e.rope_cos, e.rope_sin))
        cnf = e.cn.rearrange("p t c -> p (t c)")
        e.gamma, e.beta = cnf[:, 0:512], cnf[:, 512:1024]
        e.gamma_s, e.beta_s = (cnf[:, 1024 + 32 * i:1056 + 32 * i].rearrange("p (a d) -> p a d", a=2) for i in range(2))
        e.r_sum, e.r_var, e.r_std, e.r_inv = ([cnf[:, 1088 + 256 * i + 128 * j:1088 + 256 * i + 128 * (j + 1)] for j in range(2)]
                                              for i in range(4))

        e.xq = arena[:, 0:S].bitcast(BF16).rearrange("p (k n) -> p k n", k=NC)
        e.wq = arena[:, S:S + D].bitcast(BF16).rearrange("p (k n) -> p k n", k=NC)

        a = 0
        e.w_fc = take(NC * FF).rearrange("p (k n) -> p k n", k=NC)
        e.w_mp = take(FF // P * D).rearrange("p (k n) -> p k n", n=D)
        e.hT = [take(FF // P * CH).rearrange("p (f n) -> p f n", n=CH) for _ in range(2)]
        e.b_fc = take(FF // P)

        a = 0
        e.moe_w = [[take(NC * INTER).rearrange("p (k n) -> p k n", k=NC), take(NC * INTER).rearrange("p (k n) -> p k n", k=NC),
                    take(INTER // P * D).rearrange("p (k n) -> p k n", n=D)] for _ in range(2)]
        e.moe_h = [take(INTER // P * CH).rearrange("p (i n) -> p i n", n=CH) for _ in range(2)]
        e.moe_s = [take(CH) for _ in range(2)]
        E = NE - 1
        e.comb = take(NT * NE).rearrange("p (t x) -> p t x", t=NT)
        e.comb_x = [take(NT) for _ in range(2)]
        e.w_gate = take(NC * E).rearrange("p (k n) -> p k n", k=NC)
        e.b_gate, e.below = take(E), take(E * E)
        e.g_r = take(NT)
        e.g_p, e.g_b = (take(NT * E).rearrange("p (t x) -> p t x", t=NT) for _ in range(2))
        e.g_eq, e.g_gt = (take(NT * E * E).rearrange("p (t i j) -> p t i j", t=NT, i=E) for _ in range(2))

        d = dram

        def mat(dst, name):
            return dst, d[name].rearrange("(k p) o -> p k o", p=P)

        def row(dst, name):
            return dst, d[name].partition_broadcast(P)

        def col(dst, name):
            return dst, d[name + "_col"]

        def from_xT(w):
            def products(t, bank):
                for c in range(NC):
                    last = nc.tensor.matmul(bank, e.xT[:, c, t * P:(t + 1) * P], w[:, c, :],
                                            start=(c == 0), stop=(c == NC - 1))
                return last
            return products

        def quantised(t, bank):
            for c in range(NC):
                last = nc.tensor.matmul(bank, e.xq[:, c, t * P:(t + 1) * P], e.wq[:, c, :],
                                        start=(c == 0), stop=(c == NC - 1))
            return last

        q_scale = HD ** -0.5
        wq_a, wk_a = e.w_a[:, :, 0:D], e.w_a[:, :, D:2 * D]

        load_phase(nc, e)
        rope_phase(nc, e)
        split_phase(nc, e, [], [(None, None, q_scale, e.qkn[:, :, 0:D], S, e.qd),
                                (None, None, 1.0, e.qkn[:, :, D:2 * D], S, e.kd)])
        value_phase(nc, e, [mat(e.w_v, "L0_attn_Wv")], e.w_v, e.xT, S, None)
        attention_phase(nc, e, S, True, False)
        transpose_phase(nc, e, e.cn, e.xT)
        output_phase(nc, e, [mat(e.w_o, "L0_attn_Wo"), row(e.b_row, "L0_attn_bo")], from_xT(e.w_o),
                     e.x_nat, e.b_row, e.x_nat, e.x_nat, e.eps5)

        def cross(names, masked):
            wq, bq, wk, bk, wv, bv, wo, bo = names
            transpose_phase(nc, e, e.x_nat, e.xT)
            if masked:
                mask_phase(nc, e)
            split_phase(nc, e, [mat(wq_a, wq), mat(wk_a, wk), col(e.bq_col, bq), col(e.bk_col, bk),
                                (e.ctxT, d["ctxT"].rearrange("(k p) t -> p k t", p=P))],
                        [(wq_a, e.bq_col, q_scale, e.xT, S, e.qd), (wk_a, e.bk_col, 1.0, e.ctxT, S2, e.kd)])
            value_phase(nc, e, [mat(e.w_v, wv), row(e.bv_row, bv)], e.w_v, e.ctxT, S2, e.bv_row)
            attention_phase(nc, e, S2, False, masked)
            transpose_phase(nc, e, e.cn, e.xT)
            output_phase(nc, e, [mat(e.w_o, wo), row(e.b_row, bo)], from_xT(e.w_o), e.x_nat, e.b_row,
                         e.x_nat, e.x_nat, e.eps5)

        cross(["L0_xattn_" + n for n in ("Wq", "bq", "Wk", "bk", "Wv", "bv", "Wo", "bo")], True)
        transpose_phase(nc, e, e.x_nat, e.xT)
        fp8_phase(nc, e)
        output_phase(nc, e, [], quantised, e.x_nat, e.b_row, e.x_nat, e.x_nat, e.eps5, scale=e.descale2)

        output_phase(nc, e, [], None, None, None, e.x_nat, e.cn, e.eps10)
        transpose_phase(nc, e, e.cn, e.xT)
        w, b = d["L1_attn_w_attn"], d["L1_attn_b_attn"]
        split_phase(nc, e, [(e.w_a, w[:, 0:2 * D].rearrange("(k p) o -> p k o", p=P)),
                            (e.bq_col, d["L1_attn_b_attn_col"][:, 0:NC]),
                            (e.bk_col, d["L1_attn_b_attn_col"][:, NC:2 * NC])],
                    [(wq_a, e.bq_col, q_scale, e.xT, S, e.qd), (wk_a, e.bk_col, 1.0, e.xT, S, e.kd)])
        value_phase(nc, e, [(e.w_v, w[:, 2 * D:3 * D].rearrange("(k p) o -> p k o", p=P)),
                            (e.bv_row, b[2 * D:3 * D].partition_broadcast(P))], e.w_v, e.xT, S, e.bv_row)
        attention_phase(nc, e, S, True, False)
        transpose_phase(nc, e, e.cn, e.xT)
        output_phase(nc, e, [mat(e.w_o, "L1_attn_w_proj"), row(e.b_row, "L1_attn_b_proj")], from_xT(e.w_o),
                     e.x_nat, e.b_row, e.vall, e.cn, e.eps10)
        transpose_phase(nc, e, e.cn, e.xT)
        mlp_phase(nc, e)
        sum_phase(nc, e, [row(e.b_row, "L1_attn_b_mlp_proj")])
        output_phase(nc, e, [], None, None, None, e.x_nat, e.x_nat, e.eps5)

        cross(["L1_xattn_" + n for n in ("q_w", "q_b", "k_w", "k_b", "v_w", "v_b", "o_w", "o_b")], False)
        transpose_phase(nc, e, e.x_nat, e.xT)
        gate_phase(nc, e)
        moe_phase(nc, e)
        output_phase(nc, e, [], None, None, None, e.cn, None, e.eps5)


def sum_phase(nc, e, loads):
    with phase(nc) as sem:
        loaded, first = sem("loaded"), sem("first")
        with nc.Block() as block:

            @block.sync
            def _(sp):
                for dst, src in loads:
                    sp.dma_start(dst, src).then_inc(loaded, 16)

            @block.gpsimd
            def _(pool):
                pool.wait_ge(loaded, 16 * len(loads))
                for t in range(NT):
                    nc.gpsimd.tensor_tensor(e.vall[:, t, :], e.vall[:, t, :], e.b_row, ALU.add).then_inc(first, 1)

            @block.vector
            def _(dve):
                for t in range(NT):
                    dve.wait_ge(first, t + 1)
                    nc.vector.tensor_tensor(e.x_nat[:, t, :], e.x_nat[:, t, :], e.vall[:, t, :], ALU.add)


_TRANSPOSED = ["L0_attn_Wq", "L0_attn_Wk", "L0_attn_Wv", "L0_attn_Wo", "L0_xattn_Wq", "L0_xattn_Wk",
               "L0_xattn_Wv", "L0_xattn_Wo", "L0_ffn_weight", "L1_attn_w_attn", "L1_attn_w_proj",
               "L1_attn_w_fc", "L1_attn_w_mlp_proj", "L1_ffn_gate_w"]
_PLAIN = ["L0_attn_q_gamma", "L0_attn_q_beta", "L0_attn_k_gamma", "L0_attn_k_beta", "L0_attn_bo",
          "L0_xattn_bv", "L0_xattn_bo", "L0_ffn_bias", "L1_attn_b_attn",
          "L1_attn_b_proj", "L1_attn_b_mlp_proj", "L1_xattn_q_w", "L1_xattn_k_w", "L1_xattn_v_w", "L1_xattn_v_b", "L1_xattn_o_w", "L1_xattn_o_b",
          "L1_ffn_gate_bias"]

_COLUMNS = ["L0_xattn_bq", "L0_xattn_bk", "L1_attn_b_attn", "L1_attn_b_fc", "L1_xattn_q_b", "L1_xattn_k_b"]


def constants():
    f = np.float32
    rows, cols = np.arange(P)[:, None], np.arange(P)[None, :]
    theta = np.arange(S, dtype=f)[:, None] * np.exp(-(np.arange(0, HD, 2, dtype=f) / f(HD)) * f(np.log(10000.0)))
    cos, sin = np.repeat(np.cos(theta), 2, axis=1), np.repeat(np.sin(theta), 2, axis=1)
    sin = np.concatenate([-sin[:, :HD // 2], sin[:, HD // 2:]], axis=1)
    E = NE - 1
    return {
        "ident": np.eye(P, dtype=f), "masked": f(MASKED) * np.eye(P, dtype=f),
        "upper": np.where(cols > rows, f(MASKED), f(0)),
        "lower": np.where(rows > cols, f(MASKED), f(0)),
        "rope_cos": cos.astype(f), "rope_sin": sin.astype(f),
        "below": (np.arange(E)[None, :] < np.arange(E)[:, None]).astype(f).reshape(-1),
    }


def kernel(**inputs):
    import concourse.bacc as bacc
    from concourse.bass_utils import run_bass_kernel_spmd

    nc = bacc.Bacc("TRN2", target_bir_lowering=False, num_devices=1)
    a = {k: np.asarray(v) for k, v in inputs.items()}
    laid = dict(constants())
    laid["x"] = a["x"][0]
    laid["xT"] = a["x"][0].T
    laid["ctxT"] = a["ctx_1024"][0].T
    laid["mask"] = a["mask_1x1xSxS2_ik0"][0, 0]
    laid["maskT"] = a["mask_1x1xSxS2_ik0"][0, 0].T
    for name in _TRANSPOSED:
        laid[name] = a[name].T
    for name in _PLAIN:
        laid[name] = a[name]
    for name in _COLUMNS:
        laid[name + "_col"] = a[name].reshape(-1, P).T
    for name in ("w1", "w3", "w2"):
        both = np.concatenate([a["L1_ffn_" + name], a["L1_ffn_s" + name][None]])
        laid["moe_" + name] = both.transpose(0, 2, 1).reshape(-1, both.shape[1])
    arrays, dram = {}, {}
    for name, v in laid.items():
        arrays[f"in_{name}"] = np.ascontiguousarray(v)
        dram[name] = nc.dram_tensor(f"in_{name}", v.shape, mybir.dt.from_np(v.dtype), kind="ExternalInput").ap()
    out = nc.dram_tensor("out_x", (S, D), F32, kind="ExternalOutput").ap()
    build(nc, dram, out)
    r = run_bass_kernel_spmd(nc, [arrays], core_ids=[0])
    return r.results[0]["out_x"].reshape(1, S, D)
```

```python
from contextlib import ExitStack, contextmanager

import numpy as np

import concourse.bass as bass
from concourse import mybir

F32 = mybir.dt.float32
BF16 = mybir.dt.bfloat16
I32 = mybir.dt.int32
FP8 = mybir.dt.float8e4
ALU = mybir.AluOpType
ACT = mybir.ActivationFunctionType
AX = mybir.AxisListType.X
RMAX = bass.bass_isa.ReduceOp.max

P = 128
S = 2048
S2 = 1601
D = 256
H = 16
HD = D // H
NT = S // P
NT2 = -(-S2 // P)
NC = D // P
CH = 512
HALF = S // 2
SUB = HALF // 4
PARTS = [0, 1, 2, 0, 1, 0], [0, 0, 0, 1, 1, 2]
KQ = HD * 6
KM = KQ + 3
FF = 4 * D
NE = 9
INTER = 512
MASKED = -float(2 ** 30)
FIRST_SEMAPHORE, PHASE_SEMAPHORES = 160, 30
PHASES_SO_FAR = {}


def tiles(n, w):
    return [(a, min(w, n - a)) for a in range(0, n, w)]


@contextmanager
def phase(nc):
    number = nc.next_id()
    turns = PHASES_SO_FAR[id(nc)] = PHASES_SO_FAR.get(id(nc), 0) + 1
    first = FIRST_SEMAPHORE + PHASE_SEMAPHORES * (turns % 2)
    sems = []

    def sem(name):
        assert len(sems) < PHASE_SEMAPHORES
        sems.append(nc.alloc_semaphore(name=f"{name}_{number}", num=first + len(sems)))
        return sems[-1]

    yield sem
    nc.clear_and_free_semaphores(sems)


class Env:
    pass


class Chain:

    def __init__(self, eng, sem, start=0):
        self.eng, self.sem, self.n = eng, sem, start

    def link(self, ins):
        self.n += 1
        ins.then_inc(self.sem, 1)
        self.eng.wait_ge(self.sem, self.n)


def load_phase(nc, e):
    with phase(nc) as sem:
        loaded = sem("loaded")
        with nc.Block() as block:

            @block.sync
            def _(sp):
                pairs = [(e.ident, e.d["ident"])]
                pairs += [(e.wide[:, i * P:(i + 1) * P], e.d[n]) for i, n in enumerate(("masked", "upper", "lower"))]
                pairs += [(e.x_nat, e.d["x"].rearrange("(t p) c -> p t c", p=P)),
                          (e.xT, e.d["xT"].rearrange("(k p) t -> p k t", p=P))]
                for dst, src in pairs:
                    sp.dma_start(dst, src).then_inc(loaded, 16)
                sp.wait_ge(loaded, 16 * len(pairs))

            @block.vector
            def _(dve):
                for vbuf in e.vbuf:
                    nc.vector.memset(vbuf, 1.0)
                nc.vector.memset(e.eps5, 1e-5)
                nc.vector.memset(e.eps10, 1e-10)
                dve.wait_ge(loaded, 16 * 6)
                nc.vector.tensor_copy(e.ident16, e.ident)
                for i, dst in enumerate((e.big16, e.upper16, e.lower16)):
                    nc.vector.tensor_copy(dst, e.wide[:, i * P:(i + 1) * P])


def transpose_phase(nc, e, src, dst):
    with phase(nc) as sem:
        turned = sem("turned")
        with nc.Block() as block:
            groups = [(c, g) for g in range(NT // 4) for c in range(NC)]

            @block.tensor
            def _(pe):
                for b, (c, g) in enumerate(groups):
                    for i in range(4):
                        last = nc.tensor.transpose(e.ps[:, b, i * P:(i + 1) * P],
                                                   src[:, 4 * g + i, c * P:(c + 1) * P], e.ident)
                    last.then_inc(turned, 1)

            @block.vector
            def _(dve):
                for b, (c, g) in enumerate(groups):
                    if b % 2 == 0:
                        dve.wait_ge(turned, b + 1)
                        nc.vector.tensor_copy(dst[:, c, g * CH:(g + 1) * CH], e.ps[:, b, :])

            @block.scalar
            def _(act):
                for b, (c, g) in enumerate(groups):
                    if b % 2 == 1:
                        act.wait_ge(turned, b + 1)
                        nc.scalar.activation(dst[:, c, g * CH:(g + 1) * CH], e.ps[:, b, :], ACT.Copy)


def split_phase(nc, e, loads, jobs):
    work = [(w, bias, scale, src, dst, o, a, n)
            for w, bias, scale, src, length, dst in jobs
            for o in range(NC) for a, n in tiles(length, CH)]
    with phase(nc) as sem:
        loaded, made, whole, high, rest, middle, low = (sem(n) for n in (
            "loaded", "made", "whole", "high", "rest", "middle", "low"))
        stored = [sem(f"stored{i}") for i in range(2)]
        with nc.Block() as block:

            @block.sync
            def _(sp):
                for dst, src in loads:
                    sp.dma_start(dst, src).then_inc(loaded, 16)
                for i, (w, bias, scale, src, dst, o, a, n) in enumerate(work):
                    sp.wait_ge(low, i + 1)
                    sp.wait_ge(middle, i + 1)
                    sp.wait_ge(high, i + 1)
                    sp.dma_start(dst.rearrange("s r t -> r s t")[o * P:(o + 1) * P, :, a:a + n],
                                 e.parts[i % 2][:, :, 0:n]).then_inc(stored[i % 2], 16)
                for j in range(2):
                    sp.wait_ge(stored[j], 16 * len(range(j, len(work), 2)))

            @block.tensor
            def _(pe):
                if loads:
                    pe.wait_ge(loaded, 16 * len(loads))
                for i, (w, bias, scale, src, dst, o, a, n) in enumerate(work):
                    if i >= 8:
                        pe.wait_ge(whole, i - 7)
                    if w is None:
                        for t in range(n // P):
                            last = nc.tensor.transpose(e.ps[:, i % 8, t * P:(t + 1) * P],
                                                       src[:, a // P + t, o * P:(o + 1) * P], e.ident)
                    else:
                        for c in range(NC):
                            last = nc.tensor.matmul(e.ps[:, i % 8, 0:n], w[:, c, o * P:(o + 1) * P],
                                                    src[:, c, a:a + n], start=(c == 0), stop=(c == NC - 1))
                    last.then_inc(made, 1)

            @block.vector
            def _(dve):
                if loads:
                    dve.wait_ge(loaded, 16 * len(loads))
                for i, (w, bias, scale, src, dst, o, a, n) in enumerate(work):
                    dve.wait_ge(made, i + 1)
                    if i >= 2:
                        dve.wait_ge(high, i - 1)
                    full = e.whole[i % 2][:, 0:n]
                    if bias is None:
                        nc.vector.tensor_scalar(full, e.ps[:, i % 8, 0:n], scale, None, ALU.mult).then_inc(whole, 1)
                    else:
                        nc.vector.tensor_scalar(full, e.ps[:, i % 8, 0:n], bias[:, o:o + 1], scale,
                                                ALU.add, ALU.mult).then_inc(whole, 1)
                    dve.wait_ge(high, i + 1)
                    if i >= 2:
                        dve.wait_ge(low, i - 1)
                    nc.vector.tensor_tensor(e.rest[i % 2][:, 0:n], full, e.parts[i % 2][:, 0, 0:n],
                                            ALU.subtract).then_inc(rest, 1)

            @block.scalar
            def _(act):
                for i, (w, bias, scale, src, dst, o, a, n) in enumerate(work):
                    act.wait_ge(whole, i + 1)
                    if i >= 2:
                        act.wait_ge(stored[i % 2], 16 * (i // 2))
                    nc.scalar.activation(e.parts[i % 2][:, 0, 0:n], e.whole[i % 2][:, 0:n],
                                         ACT.Copy).then_inc(high, 1)
                    act.wait_ge(rest, i + 1)
                    nc.scalar.activation(e.parts[i % 2][:, 1, 0:n], e.rest[i % 2][:, 0:n],
                                         ACT.Copy).then_inc(middle, 1)

            @block.gpsimd
            def _(pool):
                for i, (w, bias, scale, src, dst, o, a, n) in enumerate(work):
                    pool.wait_ge(middle, i + 1)
                    nc.gpsimd.tensor_tensor(e.parts[i % 2][:, 2, 0:n], e.rest[i % 2][:, 0:n],
                                            e.parts[i % 2][:, 1, 0:n], ALU.subtract).then_inc(low, 1)


def value_phase(nc, e, loads, w, src, length, bias_row):
    with phase(nc) as sem:
        loaded = sem("loaded")
        made = sem("made")
        kept = sem("kept")
        with nc.Block() as block:

            @block.sync
            def _(sp):
                for dst, s in loads:
                    sp.dma_start(dst, s).then_inc(loaded, 16)

            @block.tensor
            def _(pe):
                if loads:
                    pe.wait_ge(loaded, 16 * len(loads))
                for t, (a, n) in enumerate(tiles(length, P)):
                    if t >= 8:
                        pe.wait_ge(kept, t - 7)
                    for c in range(NC):
                        last = nc.tensor.matmul(e.ps[0:n, t % 8, 0:D], src[:, c, a:a + n], w[:, c, :],
                                                start=(c == 0), stop=(c == NC - 1))
                    last.then_inc(made, 1)

            @block.vector
            def _(dve):
                if loads:
                    dve.wait_ge(loaded, 16 * len(loads))
                for t, (a, n) in enumerate(tiles(length, P)):
                    dve.wait_ge(made, t + 1)
                    if bias_row is None:
                        nc.vector.tensor_copy(e.vall[0:n, t, :], e.ps[0:n, t % 8, 0:D]).then_inc(kept, 1)
                    else:
                        nc.vector.tensor_tensor(e.vall[0:n, t, :], e.ps[0:n, t % 8, 0:D], bias_row[0:n, :],
                                                ALU.add).then_inc(kept, 1)


def mask_phase(nc, e):
    with phase(nc) as sem:
        nat_in = [sem(f"nat_in{i}") for i in range(2)]
        tr_in = [sem(f"tr_in{i}") for i in range(2)]
        nat_done = sem("nat_done")
        tr_done = sem("tr_done")
        with nc.Block() as block:
            keys = tiles(S2, P)

            @block.sync
            def _(sp):
                for t in range(NT):
                    if t >= 2:
                        sp.wait_ge(nat_done, t - 1)
                    sp.dma_start(e.mask_in[t % 2][:, 0:S2], e.d["mask"][t * P:(t + 1) * P, :]).then_inc(nat_in[t % 2], 16)
                    if t < NT2:
                        a, n = keys[t]
                        if t >= 2:
                            sp.wait_ge(tr_done, t - 1)
                        sp.dma_start(e.maskT_in[t % 2][0:n, :], e.d["maskT"][a:a + n, :]).then_inc(tr_in[t % 2], 16)

            @block.vector
            def _(dve):
                for t in range(NT):
                    dve.wait_ge(nat_in[t % 2], 16 * (t // 2 + 1))
                    nc.vector.tensor_scalar(e.mask_add[:, t, :], e.mask_in[t % 2][:, 0:S2], 0.0, MASKED,
                                            ALU.is_equal, ALU.mult).then_inc(nat_done, 1)
                    if t < NT2:
                        n = keys[t][1]
                        dve.wait_ge(tr_in[t % 2], 16 * (t // 2 + 1))
                        nc.vector.tensor_scalar(e.mask_one[0:n, t, :], e.maskT_in[t % 2][0:n, :], 0.0, None,
                                                ALU.is_equal, saturate=False).then_inc(tr_done, 1)


def attention_phase(nc, e, keys, causal, masked):
    steps = []
    for half in range(2):
        for t, (a, n) in enumerate(tiles(keys, P)):
            first = max(0, a - half * HALF) if causal else 0
            if first < HALF:
                steps.append((half, t, first, n))
    ns = len(steps)
    half_end = [max(i for i, s in enumerate(steps) if s[0] == half) for half in range(2)]
    units = []
    for t in range(NT):
        if causal:
            pieces = tiles((t + 1) * P, CH)
        else:
            pieces = tiles(keys, -(-keys // -(-keys // CH)))
        units += [(t, i, a, w) for i, (a, w) in enumerate(pieces)]
    nu = len(units)
    assert nu % 2 == 0
    pieces_max = max(u[1] for u in units) + 1
    n_units = nu + 1
    p_slots = 4

    lead = (0.34 if causal else 0.2 if not masked else 0.16) * sum(HALF - s[2] for s in steps)
    width = [HALF - s[2] for s in steps]
    turn = max(i for i in range(ns) if sum(width[i + 1:ns - 2]) >= lead)
    order = list(range(turn + 2, ns)) + list(range(turn + 1))
    share = {i: 0 for i in range(ns)}
    done = 0
    for n, i in enumerate(order):
        upto = nu * sum(width[j] for j in order[:n + 1]) // sum(width[j] for j in order)
        share[i] = (done, upto)
        done = upto
    early = {i: share[i] for i in range(turn + 2, ns)}
    late = {i: share[i] for i in range(turn + 1)}
    early_units = max([b for a, b in early.values()], default=0)

    with phase(nc) as sem:
        sp_waited = sem("sp_waited")
        stacks_in = sem("stacks_in")
        max_out, max_in = sem("max_out"), sem("max_in")
        unit_ready, unit_used, unit_seen = sem("unit_ready"), sem("unit_used"), sem("unit_seen")
        s_ready, exp_done, pv_done = sem("s_ready"), sem("exp_done"), sem("pv_done")
        v_ready = sem("v_ready")
        o_copied, o_turned, o_done = sem("o_copied"), sem("o_turned"), sem("o_done")
        max_chain, norm_chain = sem("max_chain"), sem("norm_chain")
        mpart_set, ones_set = sem("mpart_set"), sem("ones_set")
        with nc.Block() as block:

            S_PS = [e.ps[:, 0:2, :].rearrange("p a b -> p (a b)"), e.ps[:, 2:4, :].rearrange("p a b -> p (a b)")]
            M_PS = [e.ps[:, 4, :], e.ps[:, 5, :]]
            O_PS = [e.ps[:, 6, :], e.ps[:, 7, :]]

            def heads(eng, body):
                body(0, (0, 1, 2), False, True, True)
                body(1, (1, 2, 0), True, True, True)
                with eng.Fori(0, (H - 4) // 3) as three:
                    for j in range(3):
                        body(3 * three + (2 + j), tuple((2 + j + k) % 3 for k in range(3)), True, True, True)
                body(H - 2, tuple((H - 2 + k) % 3 for k in range(3)), True, True, False)
                body(H - 1, tuple((H - 1 + k) % 3 for k in range(3)), True, False, False)

            def p_slot(h, i):
                if i >= p_slots:
                    return i % p_slots, h * ns + i - p_slots + 1
                before = max(j for j in range(ns) if j % p_slots == i)
                return i, (h - 1) * ns + before + 1

            @block.sync
            def _(sp):
                def load(h, buf):
                    for stack, parts, src, n in ((e.ks[buf], PARTS[0], e.kd, keys), (e.qs[buf], PARTS[1], e.qd, S)):
                        for slot, part in enumerate(parts):
                            sp.dma_start(stack[slot * HD:(slot + 1) * HD, 0:n],
                                         src[part, bass.ds(h * HD, HD), 0:n]).then_inc(stacks_in, 16)

                def place_max(h, buf, before):
                    sp.wait_ge(max_chain, h * 4 + 4)
                    sp.sem_inc(sp_waited, 1)
                    if before:
                        sp.wait_ge(max_in, 16 * h)
                        sp.sem_inc(sp_waited, 1)
                    sp.dma_start(e.md.rearrange("s t q -> t s q"), e.mrow).then_inc(max_out, 16)
                    sp.wait_ge(max_out, 16 * (h + 1))
                    sp.sem_inc(sp_waited, 1)
                    sp.dma_start(e.qs[buf][KQ:KM, :], e.md.rearrange("s t q -> s (t q)")).then_inc(max_in, 16)

                def body(h, bufs, has_last, has_next, has_second):
                    if has_second:
                        if has_last:
                            sp.wait_ge(pv_done, h * ns)
                            sp.sem_inc(sp_waited, 1)
                        load(h + 2, bufs[2])
                    if has_next:
                        place_max(h + 1, bufs[1], True)

                load(0, 0)
                load(1, 1)
                place_max(0, 0, False)
                heads(sp, body)

            @block.gpsimd
            def _(pool):
                def values(h, buf):
                    for t, k, n in [(0, keys // P, P)] + ([(keys // P, 1, keys % P)] if keys % P else []):
                        last = nc.gpsimd.tensor_copy(e.vbuf[buf][0:n, t:t + k, 0:HD],
                                                     e.vall[0:n, t:t + k, bass.ds(h * HD, HD)])
                    last.then_inc(v_ready, 1)

                def body(h, bufs, has_last, has_next, has_second):
                    if has_next:
                        if has_last:
                            pool.wait_ge(pv_done, h * ns)
                        values(h + 1, bufs[1])

                values(0, 0)
                heads(pool, body)

            @block.scalar
            def _(act):
                def body(h, bufs, has_last, has_next, has_second):
                    for i, (half, t, first, n) in enumerate(steps):
                        act.wait_ge(s_ready, h * ns + i + 1)
                        slot, free = p_slot(h, i)
                        if has_last or i >= p_slots:
                            act.wait_ge(pv_done, free)
                        nc.scalar.activation(e.prob[slot][0:n, first:HALF], S_PS[i % 2][0:n, first:HALF],
                                             ACT.Exp).then_inc(exp_done, 1)
                heads(act, body)

            @block.tensor
            def _(pe):
                def unit(h, buf, u, before=True):
                    t, i, a, w = units[u]
                    g = h * n_units + u
                    if u >= 2:
                        pe.wait_ge(unit_used, g - 1)
                    elif before:
                        pe.wait_ge(unit_used, g - u)
                    diagonal = causal and a + w == (t + 1) * P
                    last = nc.tensor.matmul(M_PS[u % 2][:, 0:w], e.qs[buf][0:KQ, t * P:(t + 1) * P],
                                            e.ks[buf][0:KQ, a:a + w], start=True, stop=not diagonal)
                    if diagonal:
                        last = nc.tensor.matmul(M_PS[u % 2][:, w - P:w], e.ident16, e.upper16,
                                                start=False, stop=True)
                    last.then_inc(unit_ready, 1)

                def turn_max(h):
                    pe.wait_ge(unit_used, h * n_units + nu - 1)
                    pe.wait_ge(max_chain, h * 4 + 1)
                    nc.tensor.transpose(M_PS[nu % 2][0:NT, 0:P], e.mfin, e.ident).then_inc(unit_ready, 1)

                def scores(h, buf, i, before=True, between=None):
                    half, t, first, n = steps[i]
                    if before or i >= 2:
                        pe.wait_ge(exp_done, h * ns + i - 1)
                    if i == 0:
                        pe.wait_ge(max_in, 16 * (h + 1))
                    kt = e.ks[buf][0:KM, t * P:t * P + n]
                    on_diagonal = causal and t * P >= half * HALF
                    for b in range(2):
                        lo = max(first, b * CH)
                        if lo >= (b + 1) * CH:
                            continue
                        if b == 1 and between:
                            between()
                        diagonal = on_diagonal and lo == first
                        last = nc.tensor.matmul(S_PS[i % 2][0:n, lo:(b + 1) * CH], kt,
                                                e.qs[buf][0:KM, half * HALF + lo:half * HALF + (b + 1) * CH],
                                                start=True, stop=not (diagonal or masked))
                        if diagonal:
                            last = nc.tensor.matmul(S_PS[i % 2][0:n, lo:lo + P], e.ident16, e.lower16,
                                                    start=False, stop=True)
                        if masked:
                            last = nc.tensor.matmul(S_PS[i % 2][0:n, lo:(b + 1) * CH], e.big16[0:n, 0:n],
                                                    e.mask_one[0:n, t, half * HALF + lo:half * HALF + (b + 1) * CH],
                                                    start=False, stop=True)
                    last.then_inc(s_ready, 1)

                def product(h, buf, i, before):
                    half, t, first, n = steps[i]
                    pe.wait_ge(exp_done, h * ns + i + 1)
                    if t == 0:
                        if half == 0:
                            pe.wait_ge(v_ready, h + 1)
                        if before:
                            pe.wait_ge(o_done, (h - 1) * 2 + half + 1)
                    slot = i % p_slots
                    for j in range(4):
                        lo = max(first - j * SUB, 0)
                        if lo >= SUB:
                            continue
                        stop = t == (half * HALF + (j + 1) * SUB) // P - 1 if causal else i == half_end[half]
                        last = nc.tensor.matmul(O_PS[half][32 * j:32 * j + 32, lo:SUB], e.vbuf[buf][0:n, t, :],
                                                e.prob[slot][0:n, j * SUB + lo:(j + 1) * SUB],
                                                start=(t == 0), stop=stop)
                    last.then_inc(pv_done, 1)

                def turn_out(h, half):
                    pe.wait_ge(o_copied, h * 2 + half + 1)
                    for c in range(2):
                        last = nc.tensor.transpose(O_PS[half][:, SUB + c * P:SUB + (c + 1) * P],
                                                   e.osb[half][:, c * P:(c + 1) * P], e.ident)
                    last.then_inc(o_turned, 1)

                def body(h, bufs, has_last, has_next, has_second):
                    for i in range(ns):
                        now = []
                        if has_next and i in late:
                            now = [(h + 1, bufs[1], u) for u in range(*late[i])]
                        if has_second and i in early:
                            if i == turn + 2:
                                pe.wait_ge(stacks_in, 16 * 12 * (h + 3))
                            now = [(h + 2, bufs[2], u) for u in range(*early[i])]
                        if i == turn + 1 and has_next:
                            turn_max(h + 1)

                        def some(n):
                            for _ in range(min(n, len(now))):
                                unit(*now.pop(0))

                        quarter = -(-len(now) // 4)
                        some(quarter)
                        if i + 2 < ns:
                            scores(h, bufs[0], i + 2, between=lambda: some(quarter))
                        elif has_next:
                            scores(h + 1, bufs[1], i + 2 - ns, between=lambda: some(quarter))
                        some(quarter)
                        product(h, bufs[0], i, has_last)
                        some(len(now))
                        if i == half_end[0] + 2:
                            turn_out(h, 0)
                        if i == 3 and has_last:
                            turn_out(h - 1, 1)
                    if not has_next:
                        turn_out(h, 1)

                pe.wait_ge(stacks_in, 16 * 24)
                for u in range(nu):
                    unit(0, 0, u, before=False)
                turn_max(0)
                for u in range(early_units):
                    unit(1, 1, u)
                pe.wait_ge(ones_set, 3)
                scores(0, 0, 0, before=False)
                scores(0, 0, 1, before=False)
                heads(pe, body)

            @block.vector
            def _(dve):
                def unit(h, u, before=True):
                    t, i, a, w = units[u]
                    g = h * n_units + u
                    dve.wait_ge(unit_ready, g + 1)
                    src = M_PS[u % 2][:, 0:w]
                    if masked:
                        if before or u >= 4:
                            dve.wait_ge(unit_used, g - 3)
                        dve.sem_inc(unit_seen, 1)
                        nc.vector.tensor_tensor_reduce(out=e.scrap[:, u % 4, 0:w], in0=src, in1=e.mask_add[:, t, a:a + w],
                                                       scale=1.0, scalar=-3.0e38, op0=ALU.add, op1=ALU.max,
                                                       accum_out=e.mpart[:, t, i:i + 1]).then_inc(unit_used, 1)
                    else:
                        nc.vector.tensor_reduce(e.mpart[:, t, i:i + 1], src, AX, ALU.max).then_inc(unit_used, 1)

                def finish_max(h):
                    dve.wait_ge(unit_used, h * n_units + nu)
                    nc.vector.tensor_reduce(e.mfin, e.mpart[:, :, 0:pieces_max], AX, ALU.max).then_inc(max_chain, 1)

                def cut_max(h, before=True):
                    chain = Chain(dve, max_chain, h * 4 + 1)
                    dve.wait_ge(unit_ready, h * n_units + nu + 1)
                    turned = M_PS[nu % 2][0:NT, 0:P]
                    if before:
                        dve.wait_ge(max_out, 16 * h)
                    chain.link(nc.vector.tensor_scalar(e.mrow[:, 0, :], turned, -1.0, None, ALU.mult))
                    chain.link(nc.vector.scalar_tensor_tensor(out=e.mrest, in0=turned, scalar=-1.0,
                                                              in1=e.mrow[:, 0, :], op0=ALU.mult, op1=ALU.subtract))
                    nc.vector.tensor_copy(e.mrow[:, 1, :], e.mrest).then_inc(unit_used, 1)
                    dve.wait_ge(unit_used, h * n_units + nu + 1)
                    nc.vector.tensor_tensor(e.mrow[:, 2, :], e.mrest, e.mrow[:, 1, :], ALU.subtract).then_inc(max_chain, 1)

                def copy_out(h, half):
                    dve.wait_ge(pv_done, h * ns + half_end[half] + 1)
                    nc.vector.tensor_copy(e.osb[half], O_PS[half][:, 0:SUB]).then_inc(o_copied, 1)

                def normalise(h, half):
                    dve.wait_ge(o_turned, h * 2 + half + 1)
                    turned = O_PS[half][:, SUB:2 * SUB].rearrange("p (c j r) -> p j c r", c=2, j=4)
                    nc.vector.reciprocal(e.rsum, turned[:, :, :, HD]).then_inc(norm_chain, 1)
                    dve.wait_ge(norm_chain, h * 2 + half + 1)
                    out = e.cn[:, half * 8:half * 8 + 8, bass.ds(h * HD, HD)].rearrange("p (j c) d -> p j c d", j=4)
                    nc.vector.tensor_tensor(out, turned[:, :, :, 0:HD],
                                            e.rsum.unsqueeze(3).broadcast_to([P, 4, 2, HD]), ALU.mult).then_inc(o_done, 1)

                def body(h, bufs, has_last, has_next, has_second):
                    for i in range(ns):
                        if i == half_end[0] + 2:
                            copy_out(h, 0)
                        if i == 2 and has_last:
                            copy_out(h - 1, 1)
                        if has_next and i in late:
                            for u in range(*late[i]):
                                unit(h + 1, u)
                        if has_next and i == turn:
                            finish_max(h + 1)
                        if has_next and i == turn + 1:
                            cut_max(h + 1)
                        if has_second and i in early:
                            for u in range(*early[i]):
                                unit(h + 2, u)
                        if i == half_end[0] + 3:
                            normalise(h, 0)
                        if i == 4 and has_last:
                            normalise(h - 1, 1)
                    if not has_next:
                        copy_out(h, 1)
                        normalise(h, 1)

                nc.vector.memset(e.mpart, -3.0e38).then_inc(mpart_set, 1)
                for ks in e.ks:
                    nc.vector.memset(ks[KQ:KM, :], 1.0).then_inc(ones_set, 1)
                dve.wait_ge(mpart_set, 1)
                for u in range(nu):
                    unit(0, u, before=False)
                finish_max(0)
                cut_max(0, before=False)
                for u in range(early_units):
                    unit(1, u)
                heads(dve, body)


def rope_phase(nc, e):
    G = 4
    N = G * 2 * H
    groups = NT // G
    with phase(nc) as sem:
        loaded, made, centred, squared, spread, rooted, inverse, scaled = (sem(n) for n in (
            "loaded", "made", "centred", "squared", "spread", "rooted", "inverse", "scaled"))
        chain_sem, pool_sem, spread_tables = sem("chain"), sem("pool_chain"), sem("spread_tables")
        with nc.Block() as block:
            loads = [(e.w_a[:, :, 0:D], e.d["L0_attn_Wq"]), (e.w_a[:, :, D:2 * D], e.d["L0_attn_Wk"]),
                     (e.rope_cos, e.d["rope_cos"].rearrange("(t p) c -> p t c", p=P)),
                     (e.rope_sin, e.d["rope_sin"].rearrange("(t p) c -> p t c", p=P))]
            small = [(e.gamma_s[:, 0, :], "L0_attn_q_gamma"), (e.gamma_s[:, 1, :], "L0_attn_k_gamma"),
                     (e.beta_s[:, 0, :], "L0_attn_q_beta"), (e.beta_s[:, 1, :], "L0_attn_k_beta")]
            n_loads = len(loads) + len(small)

            def group_ps(g):
                return e.ps[:, (g % 2) * G:(g % 2) * G + G, :].rearrange("p t (r d) -> p (t r) d", d=HD)

            def rows(tile):
                return tile.rearrange("p (r d) -> p r d", d=HD)

            @block.sync
            def _(sp):
                for dst, src in loads[:2]:
                    sp.dma_start(dst, src.rearrange("(k p) o -> p k o", p=P)).then_inc(loaded, 16)
                for dst, src in loads[2:]:
                    sp.dma_start(dst, src).then_inc(loaded, 16)
                for dst, name in small:
                    sp.dma_start(dst, e.d[name].partition_broadcast(P)).then_inc(loaded, 16)

            @block.tensor
            def _(pe):
                pe.wait_ge(loaded, 16 * n_loads)
                for g in range(groups):
                    if g >= 2:
                        pe.wait_ge(centred, g - 1)
                    for i in range(G):
                        t = g * G + i
                        for c in range(NC):
                            last = nc.tensor.matmul(e.ps[:, (g % 2) * G + i, :], e.xT[:, c, t * P:(t + 1) * P],
                                                    e.w_a[:, c, :], start=(c == 0), stop=(c == NC - 1))
                    last.then_inc(made, 1)

            @block.scalar
            def _(act):
                for g in range(groups):
                    act.wait_ge(centred, g + 1)
                    if g >= 2:
                        act.wait_ge(spread, g - 1)
                    nc.scalar.activation(e.r_sq[g % 2], e.r_xc[g % 2], ACT.Square).then_inc(squared, 1)
                    act.wait_ge(spread, g + 1)
                    nc.scalar.activation(e.r_std[g % 2], e.r_var[g % 2], ACT.Sqrt, bias=e.eps5, scale=1.0 / HD).then_inc(rooted, 1)

            @block.gpsimd
            def _(pool):
                chain = Chain(pool, pool_sem)
                for g in range(groups):
                    pool.wait_ge(inverse, g + 1)
                    xc = e.r_xc[g % 2]
                    chain.link(nc.gpsimd.tensor_tensor(rows(xc), rows(xc), e.r_inv[g % 2].unsqueeze(2).broadcast_to([P, N, HD]), ALU.mult))
                    four = xc.rearrange("p (t c) -> p t c", t=G)
                    if g == 0:
                        pool.wait_ge(spread_tables, 1)
                    chain.link(nc.gpsimd.tensor_tensor(four, four, e.gamma.unsqueeze(1).broadcast_to([P, G, 2 * D]), ALU.mult))
                    nc.gpsimd.tensor_tensor(four, four, e.beta.unsqueeze(1).broadcast_to([P, G, 2 * D]), ALU.add).then_inc(scaled, 1)

            @block.vector
            def _(dve):
                chain = Chain(dve, chain_sem)
                dve.wait_ge(loaded, 16 * n_loads)
                for table, src in ((e.gamma, e.gamma_s), (e.beta, e.beta_s)):
                    last = nc.vector.tensor_copy(table.rearrange("p (a h d) -> p a h d", a=2, d=HD),
                                                 src.unsqueeze(2).broadcast_to([P, 2, H, HD]))
                last.then_inc(spread_tables, 1)

                def norm(g):
                    ps = group_ps(g)
                    dve.wait_ge(made, g + 1)
                    chain.link(nc.vector.tensor_reduce(e.r_sum[g % 2], ps, AX, ALU.add))
                    nc.vector.scalar_tensor_tensor(out=rows(e.r_xc[g % 2]), in0=e.r_sum[g % 2].unsqueeze(2).broadcast_to([P, N, HD]),
                                                   scalar=-1.0 / HD, in1=ps, op0=ALU.mult, op1=ALU.add).then_inc(centred, 1)
                    dve.wait_ge(squared, g + 1)
                    if g >= 2:
                        dve.wait_ge(rooted, g - 1)
                    nc.vector.tensor_reduce(e.r_var[g % 2], rows(e.r_sq[g % 2]), AX, ALU.add).then_inc(spread, 1)
                    dve.wait_ge(rooted, g + 1)
                    nc.vector.reciprocal(e.r_inv[g % 2], e.r_std[g % 2]).then_inc(inverse, 1)

                def rotate(g):
                    dve.wait_ge(scaled, g + 1)
                    x = e.r_xc[g % 2].rearrange("p (t r d) -> p t r d", t=G, d=HD)
                    pairs = e.r_xc[g % 2].rearrange("p (t r d two) -> p t r d two", t=G, two=2, d=HD // 2)
                    out = e.qkn[:, g * G:(g + 1) * G, :].rearrange("p t (r d) -> p t r d", d=HD)
                    tmp = e.r_sq[g % 2].rearrange("p (t r d) -> p t r d", t=G, d=HD)
                    ts = slice(g * G, (g + 1) * G)
                    for t in range(G):
                        c = e.rope_cos[:, g * G + t, :].unsqueeze(1).broadcast_to([P, 2 * H, HD])
                        s = e.rope_sin[:, g * G + t, :].unsqueeze(1).broadcast_to([P, 2 * H, HD])
                        nc.vector.tensor_tensor(out[:, t], x[:, t], c, ALU.mult)
                        nc.vector.tensor_tensor(tmp[:, t, :, 0:HD // 2], pairs[:, t, :, :, 1], s[:, :, 0:HD // 2], ALU.mult)
                        last = nc.vector.tensor_tensor(tmp[:, t, :, HD // 2:], pairs[:, t, :, :, 0], s[:, :, HD // 2:], ALU.mult)
                    chain.link(last)
                    chain.link(nc.vector.tensor_tensor(e.qkn[:, ts, :].rearrange("p t c -> p (t c)"),
                                                       e.qkn[:, ts, :].rearrange("p t c -> p (t c)"), e.r_sq[g % 2], ALU.add))

                norm(0)
                for g in range(groups):
                    if g + 1 < groups:
                        norm(g + 1)
                    rotate(g)


def output_phase(nc, e, loads, products, addend, bias_row, total, normed, eps, scale=None):
    with phase(nc) as sem:
        loaded, made, used, biased = sem("loaded"), sem("made"), sem("used"), sem("biased")
        measured, rooted, chain_sem, stored = sem("measured"), sem("rooted"), sem("chain"), sem("stored")
        normed_sem = sem("normed")
        with nc.Block() as block:
            store = normed is None
            dst = e.cn if store else normed

            @block.sync
            def _(sp):
                for d, s in loads:
                    sp.dma_start(d, s).then_inc(loaded, 16)
                if store:
                    for t in range(0, NT, 4):
                        sp.wait_ge(normed_sem, t + 4)
                        sp.dma_start(e.out.rearrange("(t p) c -> p t c", p=P)[:, t:t + 4, :],
                                     dst[:, t:t + 4, :]).then_inc(stored, 16)
                    sp.wait_ge(stored, 16 * NT // 4)

            @block.gpsimd
            def _(pool):
                if bias_row is not None and scale is None:
                    pool.wait_ge(loaded, 16 * len(loads))
                    for t in range(NT):
                        nc.gpsimd.tensor_tensor(total[:, t, :], addend[:, t, :], bias_row, ALU.add).then_inc(biased, 1)

            @block.tensor
            def _(pe):
                if products is None:
                    return
                if loads:
                    pe.wait_ge(loaded, 16 * len(loads))
                for t in range(NT):
                    if t >= 8:
                        pe.wait_ge(used, t - 7)
                    products(t, e.ps[:, t % 8, 0:D]).then_inc(made, 1)

            @block.vector
            def _(dve):
                chain = Chain(dve, chain_sem)
                if loads:
                    dve.wait_ge(loaded, 16 * len(loads))
                for t in range(NT):
                    y = total[:, t, :]
                    if products is not None:
                        dve.wait_ge(made, t + 1)
                        ps = e.ps[:, t % 8, 0:D]
                        if scale is not None:
                            nc.vector.scalar_tensor_tensor(out=e.rounded[t % 2], in0=ps, scalar=scale, in1=bias_row,
                                                           op0=ALU.mult, op1=ALU.add).then_inc(used, 1)
                            dve.wait_ge(used, t + 1)
                            chain.link(nc.vector.tensor_tensor(y, addend[:, t, :], e.rounded[t % 2], ALU.add))
                        else:
                            a = addend
                            if bias_row is not None:
                                dve.wait_ge(biased, t + 1)
                                a = total
                            nc.vector.tensor_tensor(y, ps, a[:, t, :], ALU.add).then_inc(used, 1)
                            dve.wait_ge(used, t + 1)
                    chain.link(nc.vector.bn_stats(e.stats[:, t, :], y))
                    last = nc.vector.bn_aggr(e.mv[:, t, :], e.stats[:, t, :])
                last.then_inc(measured, 1)
                dve.wait_ge(rooted, 1)
                chain.link(nc.vector.reciprocal(e.rstd, e.std))
                for t in range(NT):
                    nc.vector.tensor_scalar(dst[:, t, :], total[:, t, :], e.mv[:, t, 0:1], e.rstd[:, t:t + 1],
                                            ALU.subtract, ALU.mult).then_inc(normed_sem, 1)

            @block.scalar
            def _(act):
                act.wait_ge(measured, 1)
                nc.scalar.activation(e.std, e.mv[:, :, 1], ACT.Sqrt, bias=eps).then_inc(rooted, 1)


def fp8_phase(nc, e):
    with phase(nc) as sem:
        loaded, amax, chain_sem, reduced = sem("loaded"), sem("amax"), sem("chain"), sem("reduced")
        with nc.Block() as block:
            w = e.w_a[:, :, 0:D]
            jobs = [(e.xT[:, c, a:a + n], e.xq[:, c, a:a + n], 0) for c in range(NC) for a, n in tiles(S, CH)]
            jobs += [(w[:, c, :], e.wq[:, c, :], 1) for c in range(NC)]

            @block.sync
            def _(sp):
                sp.dma_start(w, e.d["L0_ffn_weight"].rearrange("(k p) o -> p k o", p=P)).then_inc(loaded, 16)
                sp.dma_start(e.b_row, e.d["L0_ffn_bias"].partition_broadcast(P)).then_inc(loaded, 16)

            @block.gpsimd
            def _(pool):
                pool.wait_ge(amax, 2)
                nc.gpsimd.partition_all_reduce(e.amax_all, e.amax, P, RMAX).then_inc(reduced, 1)

            @block.vector
            def _(dve):
                chain = Chain(dve, chain_sem)
                nc.vector.tensor_reduce(e.amax[:, 0:1], e.x_nat.rearrange("p t c -> p (t c)"), AX, ALU.max,
                                        apply_absolute_value=True).then_inc(amax, 1)
                dve.wait_ge(loaded, 32)
                nc.vector.tensor_reduce(e.amax[:, 1:2], w, mybir.AxisListType.XY, ALU.max,
                                        apply_absolute_value=True).then_inc(amax, 1)
                dve.wait_ge(reduced, 1)
                chain.link(nc.vector.tensor_scalar(e.amax_all, e.amax_all, 1e-12, None, ALU.max))
                chain.link(nc.vector.reciprocal(e.qscale, e.amax_all))
                chain.link(nc.vector.tensor_scalar(e.qscale, e.qscale, 448.0, 448.0, ALU.mult, ALU.min))
                chain.link(nc.vector.reciprocal(e.descale, e.qscale))
                chain.link(nc.vector.tensor_tensor(e.descale2, e.descale[:, 0:1], e.descale[:, 1:2], ALU.mult))
                for i, (src, dst, which) in enumerate(jobs):
                    n = src.shape[1]
                    v, m = e.whole[i % 2][:, 0:n], e.rest[i % 2][:, 0:n]
                    chain.link(nc.vector.tensor_scalar(v, src, e.qscale[:, which:which + 1], 448.0, ALU.mult, ALU.min))
                    chain.link(nc.vector.tensor_scalar(v, v, -448.0, None, ALU.max))
                    chain.link(nc.vector.tensor_scalar(m.bitcast(I32), v.bitcast(I32), 0x7F800000, None, ALU.bitwise_and))
                    chain.link(nc.vector.tensor_scalar(m, m, 2.0 ** -6, 1.5 * 2.0 ** 20, ALU.max, ALU.mult))
                    chain.link(nc.vector.tensor_tensor(v, v, m, ALU.add))
                    chain.link(nc.vector.tensor_tensor(dst, v, m, ALU.subtract))


def mlp_phase(nc, e):
    nf = FF // P
    with phase(nc) as sem:
        loaded, up_ready, act_done, down_ready, added = (sem(n) for n in (
            "loaded", "up_ready", "act_done", "down_ready", "added"))
        with nc.Block() as block:
            chunks = tiles(S, CH)

            @block.sync
            def _(sp):
                sp.dma_start(e.w_fc, e.d["L1_attn_w_fc"].rearrange("(k p) o -> p k o", p=P)).then_inc(loaded, 16)
                sp.dma_start(e.w_mp, e.d["L1_attn_w_mlp_proj"].rearrange("(k p) o -> p k o", p=P)).then_inc(loaded, 16)
                sp.dma_start(e.b_fc, e.d["L1_attn_b_fc_col"]).then_inc(loaded, 16)

            @block.tensor
            def _(pe):
                pe.wait_ge(loaded, 48)

                def up(i, a):
                    for f in range(nf):
                        g = i * nf + f
                        if g >= 4:
                            pe.wait_ge(act_done, g - 3)
                        for c in range(NC):
                            last = nc.tensor.matmul(e.ps[:, g % 4, :], e.w_fc[:, c, f * P:(f + 1) * P],
                                                    e.xT[:, c, a:a + CH], start=(c == 0), stop=(c == NC - 1))
                        last.then_inc(up_ready, 1)

                def down(i):
                    pe.wait_ge(act_done, (i + 1) * nf)
                    for t in range(4):
                        g = i * 4 + t
                        if g >= 4:
                            pe.wait_ge(added, g - 3)
                        for f in range(nf):
                            last = nc.tensor.matmul(e.ps[:, 4 + g % 4, 0:D], e.hT[i % 2][:, f, t * P:(t + 1) * P],
                                                    e.w_mp[:, f, :], start=(f == 0), stop=(f == nf - 1))
                        last.then_inc(down_ready, 1)

                for i, (a, n) in enumerate(chunks):
                    up(i, a)
                    if i:
                        down(i - 1)
                down(len(chunks) - 1)

            @block.scalar
            def _(act):
                act.wait_ge(loaded, 48)
                for i in range(len(chunks)):
                    if i >= 2:
                        act.wait_ge(down_ready, (i - 1) * 4)
                    for f in range(nf):
                        act.wait_ge(up_ready, i * nf + f + 1)
                        nc.scalar.activation(e.hT[i % 2][:, f, :], e.ps[:, (i * nf + f) % 4, :], ACT.Gelu_apprx_tanh,
                                             bias=e.b_fc[:, f:f + 1]).then_inc(act_done, 1)

            @block.vector
            def _(dve):
                for t in range(NT):
                    dve.wait_ge(down_ready, t + 1)
                    nc.vector.tensor_tensor(e.vall[:, t, :], e.vall[:, t, :], e.ps[:, 4 + t % 4, 0:D],
                                            ALU.add).then_inc(added, 1)


def gate_phase(nc, e):
    E = NE - 1
    with phase(nc) as sem:
        loaded, made, exped, chain_sem, copied = sem("loaded"), sem("made"), sem("exped"), sem("chain"), sem("copied")
        centred = sem("centred")
        with nc.Block() as block:
            shape3, shape4 = [P, NT, E], [P, NT, E, E]

            @block.sync
            def _(sp):
                sp.dma_start(e.w_gate, e.d["L1_ffn_gate_w"].rearrange("(k p) o -> p k o", p=P)).then_inc(loaded, 16)
                sp.dma_start(e.b_gate, e.d["L1_ffn_gate_bias"].partition_broadcast(P)).then_inc(loaded, 16)
                sp.dma_start(e.below, e.d["below"].partition_broadcast(P)).then_inc(loaded, 16)

            @block.gpsimd
            def _(pool):
                nc.gpsimd.tensor_copy(e.cn, e.x_nat).then_inc(copied, 1)

            @block.tensor
            def _(pe):
                pe.wait_ge(loaded, 48)
                for t in range(NT):
                    for c in range(NC):
                        last = nc.tensor.matmul(e.ps[:, 0, t * E:(t + 1) * E], e.xT[:, c, t * P:(t + 1) * P],
                                                e.w_gate[:, c, :], start=(c == 0), stop=(c == NC - 1))
                last.then_inc(made, 1)

            @block.scalar
            def _(act):
                act.wait_ge(centred, 1)
                nc.scalar.activation(e.g_p, e.g_p, ACT.Exp).then_inc(exped, 1)

            @block.vector
            def _(dve):
                chain = Chain(dve, chain_sem)
                logits = e.ps[:, 0, 0:NT * E].rearrange("p (t e) -> p t e", e=E)
                nc.vector.memset(e.comb, 1.0).then_inc(chain_sem, 1)
                chain.n += 1
                dve.wait_ge(loaded, 48)
                dve.wait_ge(made, 1)
                chain.link(nc.vector.tensor_reduce(e.g_r, logits, AX, ALU.max))
                nc.vector.tensor_tensor(e.g_p, logits, e.g_r.unsqueeze(2).broadcast_to(shape3), ALU.subtract).then_inc(centred, 1)
                dve.wait_ge(exped, 1)
                chain.link(nc.vector.tensor_reduce(e.g_r, e.g_p, AX, ALU.add))
                chain.link(nc.vector.reciprocal(e.g_r, e.g_r))
                chain.link(nc.vector.tensor_tensor(e.g_p, e.g_p, e.g_r.unsqueeze(2).broadcast_to(shape3), ALU.mult))
                chain.link(nc.vector.tensor_tensor(e.g_b, e.g_p, e.b_gate.unsqueeze(1).broadcast_to(shape3), ALU.add))
                rival = e.g_b.unsqueeze(2).broadcast_to(shape4)
                own = e.g_b.unsqueeze(3).broadcast_to(shape4)
                chain.link(nc.vector.tensor_tensor(e.g_eq, rival, own, ALU.is_equal))
                chain.link(nc.vector.tensor_tensor(e.g_eq.rearrange("p t i j -> p t (i j)"), e.g_eq.rearrange("p t i j -> p t (i j)"),
                                                   e.below.unsqueeze(1).broadcast_to([P, NT, E * E]), ALU.mult))
                chain.link(nc.vector.tensor_tensor(e.g_gt, rival, own, ALU.is_gt))
                chain.link(nc.vector.tensor_tensor(e.g_gt, e.g_gt, e.g_eq, ALU.add))
                chain.link(nc.vector.tensor_reduce(e.g_b, e.g_gt, AX, ALU.add))
                chain.link(nc.vector.tensor_scalar(e.g_b, e.g_b, 2.0, None, ALU.is_lt))
                chain.link(nc.vector.tensor_tensor(e.comb[:, :, 0:E], e.g_b, e.g_p, ALU.mult))


def moe_phase(nc, e):
    ni = INTER // P
    nch = S // CH
    with phase(nc) as sem:
        weights_in = sem("weights_in")
        weight_col = sem("weight_col")
        ab_ready, silu_done, h_done, y_ready, y_added = (sem(n) for n in (
            "ab_ready", "silu_done", "h_done", "y_ready", "y_added"))
        with nc.Block() as block:

            def experts(eng, body):
                body(0, 0, True)
                body(1, 1, False)
                body(2, 0, False)
                with eng.Fori(1, (NE - 1) // 2) as pair:
                    body(2 * pair + 1, 1, False)
                    body(2 * pair + 2, 0, False)

            @block.sync
            def _(sp):
                def load(x, par):
                    for dst, name in zip(e.moe_w[par], ("w1", "w3", "w2")):
                        src = e.d["moe_" + name]
                        rows = src.shape[0] // NE
                        sp.dma_start(dst, src[bass.ds(x * rows, rows), :].rearrange("(k p) o -> p k o", p=P)).then_inc(weights_in, 16)

                load(0, 0)
                load(1, 1)
                with sp.Fori(0, (NE - 1) // 2 - 1) as pair:
                    for j in range(2):
                        sp.wait_ge(y_ready, (2 * pair + 1 + j) * NT)
                        load(2 * pair + 2 + j, j)
                sp.wait_ge(y_ready, (NE - 2) * NT)
                load(NE - 1, 0)

            @block.gpsimd
            def _(pool):
                def body(x, par, first):
                    if not (isinstance(x, int) and x < 2):
                        pool.wait_ge(y_added, (x - 1) * NT)
                    nc.gpsimd.tensor_copy(e.comb_x[par], e.comb[:, :, bass.ds(x, 1)].rearrange("p t o -> p (t o)")
                                          ).then_inc(weight_col, 1)
                body(0, 0, True)
                body(1, 1, True)
                body(2, 0, False)
                with pool.Fori(1, (NE - 1) // 2) as pair:
                    body(2 * pair + 1, 1, False)
                    body(2 * pair + 2, 0, False)

            @block.tensor
            def _(pe):
                def up(x, par, c):
                    w1, w3, w2 = e.moe_w[par]
                    for i in range(ni):
                        k = x * nch * ni + c * ni + i
                        if not (isinstance(x, int) and k < 2):
                            pe.wait_ge(h_done, k - 1)
                        for b, w in enumerate((w1, w3)):
                            for h in range(NC):
                                last = nc.tensor.matmul(e.ps[:, 2 * (i % 2) + b, :], w[:, h, i * P:(i + 1) * P],
                                                        e.xT[:, h, c * CH:(c + 1) * CH], start=(h == 0), stop=(h == NC - 1))
                        last.then_inc(ab_ready, 1)

                def down(x, par, c):
                    w2 = e.moe_w[par][2]
                    pe.wait_ge(h_done, x * nch * ni + (c + 1) * ni)
                    for t in range(4):
                        g = x * NT + c * 4 + t
                        if not (isinstance(x, int) and g < 4):
                            pe.wait_ge(y_added, g - 3)
                        for i in range(ni):
                            last = nc.tensor.matmul(e.ps[:, 4 + t, 0:D], e.moe_h[c % 2][:, i, t * P:(t + 1) * P],
                                                    w2[:, i, :], start=(i == 0), stop=(i == ni - 1))
                        last.then_inc(y_ready, 1)

                def body(x, par, first):
                    for c in range(nch):
                        if c == 0:
                            pe.wait_ge(weights_in, 16 * 3 * (x + 1) if not first else 16 * 6)
                        up(x, par, c)
                        if c:
                            down(x, par, c - 1)
                        elif not first:
                            down(x - 1, 1 - par, nch - 1)
                experts(pe, body)
                down(NE - 1, 0, nch - 1)

            @block.scalar
            def _(act):
                def body(x, par, first):
                    for c in range(nch):
                        for i in range(ni):
                            k = x * nch * ni + c * ni + i
                            act.wait_ge(ab_ready, k + 1)
                            if not (isinstance(x, int) and k < 2):
                                act.wait_ge(h_done, k - 1)
                            nc.scalar.activation(e.moe_s[i % 2], e.ps[:, 2 * (i % 2), :], ACT.Silu).then_inc(silu_done, 1)
                experts(act, body)

            @block.vector
            def _(dve):
                def gated(x, par, c):
                    if not (isinstance(x, int) and x * nch + c < 2):
                        dve.wait_ge(y_ready, x * NT + (c - 1) * 4)
                    for i in range(ni):
                        dve.wait_ge(silu_done, x * nch * ni + c * ni + i + 1)
                        nc.vector.tensor_tensor(e.moe_h[c % 2][:, i, :], e.moe_s[i % 2], e.ps[:, 2 * (i % 2) + 1, :],
                                                ALU.mult).then_inc(h_done, 1)

                def add(x, par, c):
                    dve.wait_ge(weight_col, x + 1)
                    for t in range(4):
                        g = x * NT + c * 4 + t
                        dve.wait_ge(y_ready, g + 1)
                        tile = e.cn[:, c * 4 + t, :]
                        if not (isinstance(x, int) and x == 0):
                            dve.wait_ge(y_added, g + 1 - NT)
                        nc.vector.scalar_tensor_tensor(out=tile, in0=e.ps[:, 4 + t, 0:D],
                                                       scalar=e.comb_x[par][:, c * 4 + t:c * 4 + t + 1], in1=tile,
                                                       op0=ALU.mult, op1=ALU.add).then_inc(y_added, 1)

                def body(x, par, first):
                    for c in range(nch):
                        gated(x, par, c)
                        if c:
                            add(x, par, c - 1)
                        elif not first:
                            add(x - 1, 1 - par, nch - 1)
                experts(dve, body)
                add(NE - 1, 0, nch - 1)


def build(nc, dram, out):
    e = Env()
    e.d, e.out = dram, out
    with ExitStack() as ctx:
        def sb(name, cols, dt=F32, rows=P):
            return ctx.enter_context(nc.sbuf_tensor(name, [rows, cols], dt))[:, :]

        def dr(name, shape, dt):
            return nc.dram_tensor(name, shape, dt, kind="Internal").ap()

        e.qd, e.kd = dr("q_parts", (3, D, S), BF16), dr("k_parts", (3, D, S), BF16)
        e.md = dr("max_parts", (3, NT, P), BF16)

        def natural(ap):
            return ap.rearrange("p (t c) -> p t c", c=D)

        def halves(ap):
            return ap.rearrange("p (k n) -> p k n", k=NC)

        e.x_nat = natural(sb("x_nat", NT * D))
        e.xT = halves(sb("xT", NC * S))
        e.cn = natural(sb("cn", NT * D))
        e.vall = natural(sb("vall", NT * D))
        arena = sb("arena", 19500)
        stacks = sb("stacks", 6 * S // 2)
        probs = sb("probs", 4 * HALF)
        vbufs = sb("vbufs", 3 * NT * 32)
        wbuf = sb("wbuf", 4 * 2 * D)
        e.vbuf = [vbufs[:, i * NT * 32:(i + 1) * NT * 32].rearrange("p (t r) -> p t r", r=32) for i in range(3)]
        e.osb = [sb(f"osb{i}", SUB) for i in range(2)]
        e.ident = sb("ident", P)
        e.ident16, e.big16 = sb("ident16", P, BF16), sb("big16", P, BF16)
        e.upper16, e.lower16 = sb("upper16", P, BF16), sb("lower16", P, BF16)
        e.w_a = halves(wbuf[:, 0:1024])
        e.w_v = halves(wbuf[:, 1024:1536])
        e.w_o = halves(wbuf[:, 1536:2048])
        e.b_row = sb("b_row", D)
        e.bv_row = sb("bv_row", D)
        bcol = sb("bcol", 4)
        e.bq_col, e.bk_col = bcol[:, 0:2], bcol[:, 2:4]
        e.mpart = sb("mpart", NT * 4).rearrange("p (t i) -> p t i", i=4)
        e.mfin = sb("mfin", NT)
        e.mrow = sb("mrow", 3 * P, BF16, NT).rearrange("t (s q) -> t s q", s=3)
        e.mrest = sb("mrest", P, F32, NT)
        e.rsum = sb("rsum", 8).rearrange("p (j c) -> p j c", j=4)
        e.scrap = sb("scrap", 4 * CH, BF16).rearrange("p (s n) -> p s n", s=4)
        e.stats = sb("stats", NT * 6).rearrange("p (t s) -> p t s", s=6)
        e.mv = sb("mv", NT * 2).rearrange("p (t s) -> p t s", s=2)
        e.std, e.rstd = sb("std", NT), sb("rstd", NT)
        small = sb("small", 16)
        e.eps5, e.eps10 = small[:, 0:1], small[:, 1:2]
        e.amax, e.amax_all = small[:, 2:4], small[:, 4:6]
        e.qscale, e.descale, e.descale2 = small[:, 8:10], small[:, 10:12], small[:, 12:13]
        rounded = sb("rounded", 2 * D, BF16)
        e.rounded = [rounded[:, i * D:(i + 1) * D] for i in range(2)]
        e.ps = ctx.enter_context(nc.psum_tensor("ps", [P, 8, CH], F32))

        s16 = stacks.bitcast(BF16)
        e.ks = [s16[:, i * S:(i + 1) * S] for i in range(3)]
        e.qs = [s16[:, (3 + i) * S:(4 + i) * S] for i in range(3)]
        e.prob = [probs[:, i * HALF:(i + 1) * HALF] for i in range(4)]
        e.ctxT = probs[:, 0:NC * S2].rearrange("p (k n) -> p k n", k=NC)
        cut = stacks[:, 0:7 * CH]
        e.whole = [cut[:, i * CH:(i + 1) * CH] for i in range(2)]
        e.rest = [cut[:, (2 + i) * CH:(3 + i) * CH] for i in range(2)]
        c16 = cut[:, 2048:3584].bitcast(BF16)
        e.parts = [c16[:, i * 3 * CH:(i + 1) * 3 * CH].rearrange("p (s n) -> p s n", s=3) for i in range(2)]

        e.mask_add = arena[:, 0:NT * S2 // 2].bitcast(BF16).rearrange("p (t n) -> p t n", t=NT)
        at = NT * S2 // 2
        e.mask_one = arena[:, at:at + NT2 * S // 4].bitcast(FP8).rearrange("p (t n) -> p t n", t=NT2)
        p32 = probs.bitcast(I32)
        e.mask_in = [p32[:, i * S2:(i + 1) * S2] for i in range(2)]
        e.maskT_in = [e.cn.rearrange("p t c -> p (t c)").bitcast(I32)[:, i * S:(i + 1) * S] for i in range(2)]

        e.wide = arena[:, 0:3 * P]

        a = 0

        def take(n):
            nonlocal a
            a += n
            return arena[:, a - n:a]
        e.qkn = take(NT * 2 * D).rearrange("p (t c) -> p t c", t=NT)
        e.r_xc, e.r_sq = [take(2048) for _ in range(2)], [take(2048) for _ in range(2)]
        e.rope_cos, e.rope_sin = e.vall[:, 0], e.vall[:, 1]
        e.rope_cos, e.rope_sin = (v.rearrange("p (t d) -> p t d", t=NT) for v in (e.rope_cos, e.rope_sin))
        cnf = e.cn.rearrange("p t c -> p (t c)")
        e.gamma, e.beta = cnf[:, 0:512], cnf[:, 512:1024]
        e.gamma_s, e.beta_s = (cnf[:, 1024 + 32 * i:1056 + 32 * i].rearrange("p (a d) -> p a d", a=2) for i in range(2))
        e.r_sum, e.r_var, e.r_std, e.r_inv = ([cnf[:, 1088 + 256 * i + 128 * j:1088 + 256 * i + 128 * (j + 1)] for j in range(2)]
                                              for i in range(4))

        e.xq = arena[:, 0:S].bitcast(BF16).rearrange("p (k n) -> p k n", k=NC)
        e.wq = arena[:, S:S + D].bitcast(BF16).rearrange("p (k n) -> p k n", k=NC)

        a = 0
        e.w_fc = take(NC * FF).rearrange("p (k n) -> p k n", k=NC)
        e.w_mp = take(FF // P * D).rearrange("p (k n) -> p k n", n=D)
        e.hT = [take(FF // P * CH).rearrange("p (f n) -> p f n", n=CH) for _ in range(2)]
        e.b_fc = take(FF // P)

        a = 0
        e.moe_w = [[take(NC * INTER).rearrange("p (k n) -> p k n", k=NC), take(NC * INTER).rearrange("p (k n) -> p k n", k=NC),
                    take(INTER // P * D).rearrange("p (k n) -> p k n", n=D)] for _ in range(2)]
        e.moe_h = [take(INTER // P * CH).rearrange("p (i n) -> p i n", n=CH) for _ in range(2)]
        e.moe_s = [take(CH) for _ in range(2)]
        E = NE - 1
        e.comb = take(NT * NE).rearrange("p (t x) -> p t x", t=NT)
        e.comb_x = [take(NT) for _ in range(2)]
        e.w_gate = take(NC * E).rearrange("p (k n) -> p k n", k=NC)
        e.b_gate, e.below = take(E), take(E * E)
        e.g_r = take(NT)
        e.g_p, e.g_b = (take(NT * E).rearrange("p (t x) -> p t x", t=NT) for _ in range(2))
        e.g_eq, e.g_gt = (take(NT * E * E).rearrange("p (t i j) -> p t i j", t=NT, i=E) for _ in range(2))

        d = dram

        def mat(dst, name):
            return dst, d[name].rearrange("(k p) o -> p k o", p=P)

        def row(dst, name):
            return dst, d[name].partition_broadcast(P)

        def col(dst, name):
            return dst, d[name + "_col"]

        def from_xT(w):
            def products(t, bank):
                for c in range(NC):
                    last = nc.tensor.matmul(bank, e.xT[:, c, t * P:(t + 1) * P], w[:, c, :],
                                            start=(c == 0), stop=(c == NC - 1))
                return last
            return products

        def quantised(t, bank):
            for c in range(NC):
                last = nc.tensor.matmul(bank, e.xq[:, c, t * P:(t + 1) * P], e.wq[:, c, :],
                                        start=(c == 0), stop=(c == NC - 1))
            return last

        q_scale = HD ** -0.5
        wq_a, wk_a = e.w_a[:, :, 0:D], e.w_a[:, :, D:2 * D]

        load_phase(nc, e)
        rope_phase(nc, e)
        split_phase(nc, e, [], [(None, None, q_scale, e.qkn[:, :, 0:D], S, e.qd),
                                (None, None, 1.0, e.qkn[:, :, D:2 * D], S, e.kd)])
        value_phase(nc, e, [mat(e.w_v, "L0_attn_Wv")], e.w_v, e.xT, S, None)
        attention_phase(nc, e, S, True, False)
        transpose_phase(nc, e, e.cn, e.xT)
        output_phase(nc, e, [mat(e.w_o, "L0_attn_Wo"), row(e.b_row, "L0_attn_bo")], from_xT(e.w_o),
                     e.x_nat, e.b_row, e.x_nat, e.x_nat, e.eps5)

        def cross(names, masked):
            wq, bq, wk, bk, wv, bv, wo, bo = names
            transpose_phase(nc, e, e.x_nat, e.xT)
            if masked:
                mask_phase(nc, e)
            split_phase(nc, e, [mat(wq_a, wq), mat(wk_a, wk), col(e.bq_col, bq), col(e.bk_col, bk),
                                (e.ctxT, d["ctxT"].rearrange("(k p) t -> p k t", p=P))],
                        [(wq_a, e.bq_col, q_scale, e.xT, S, e.qd), (wk_a, e.bk_col, 1.0, e.ctxT, S2, e.kd)])
            value_phase(nc, e, [mat(e.w_v, wv), row(e.bv_row, bv)], e.w_v, e.ctxT, S2, e.bv_row)
            attention_phase(nc, e, S2, False, masked)
            transpose_phase(nc, e, e.cn, e.xT)
            output_phase(nc, e, [mat(e.w_o, wo), row(e.b_row, bo)], from_xT(e.w_o), e.x_nat, e.b_row,
                         e.x_nat, e.x_nat, e.eps5)

        cross(["L0_xattn_" + n for n in ("Wq", "bq", "Wk", "bk", "Wv", "bv", "Wo", "bo")], True)
        transpose_phase(nc, e, e.x_nat, e.xT)
        fp8_phase(nc, e)
        output_phase(nc, e, [], quantised, e.x_nat, e.b_row, e.x_nat, e.x_nat, e.eps5, scale=e.descale2)

        output_phase(nc, e, [], None, None, None, e.x_nat, e.cn, e.eps10)
        transpose_phase(nc, e, e.cn, e.xT)
        w, b = d["L1_attn_w_attn"], d["L1_attn_b_attn"]
        split_phase(nc, e, [(e.w_a, w[:, 0:2 * D].rearrange("(k p) o -> p k o", p=P)),
                            (e.bq_col, d["L1_attn_b_attn_col"][:, 0:NC]),
                            (e.bk_col, d["L1_attn_b_attn_col"][:, NC:2 * NC])],
                    [(wq_a, e.bq_col, q_scale, e.xT, S, e.qd), (wk_a, e.bk_col, 1.0, e.xT, S, e.kd)])
        value_phase(nc, e, [(e.w_v, w[:, 2 * D:3 * D].rearrange("(k p) o -> p k o", p=P)),
                            (e.bv_row, b[2 * D:3 * D].partition_broadcast(P))], e.w_v, e.xT, S, e.bv_row)
        attention_phase(nc, e, S, True, False)
        transpose_phase(nc, e, e.cn, e.xT)
        output_phase(nc, e, [mat(e.w_o, "L1_attn_w_proj"), row(e.b_row, "L1_attn_b_proj")], from_xT(e.w_o),
                     e.x_nat, e.b_row, e.vall, e.cn, e.eps10)
        transpose_phase(nc, e, e.cn, e.xT)
        mlp_phase(nc, e)
        sum_phase(nc, e, [row(e.b_row, "L1_attn_b_mlp_proj")])
        output_phase(nc, e, [], None, None, None, e.x_nat, e.x_nat, e.eps5)

        cross(["L1_xattn_" + n for n in ("q_w", "q_b", "k_w", "k_b", "v_w", "v_b", "o_w", "o_b")], False)
        transpose_phase(nc, e, e.x_nat, e.xT)
        gate_phase(nc, e)
        moe_phase(nc, e)
        output_phase(nc, e, [], None, None, None, e.cn, None, e.eps5)


def sum_phase(nc, e, loads):
    with phase(nc) as sem:
        loaded, first = sem("loaded"), sem("first")
        with nc.Block() as block:

            @block.sync
            def _(sp):
                for dst, src in loads:
                    sp.dma_start(dst, src).then_inc(loaded, 16)

            @block.gpsimd
            def _(pool):
                pool.wait_ge(loaded, 16 * len(loads))
                for t in range(NT):
                    nc.gpsimd.tensor_tensor(e.vall[:, t, :], e.vall[:, t, :], e.b_row, ALU.add).then_inc(first, 1)

            @block.vector
            def _(dve):
                for t in range(NT):
                    dve.wait_ge(first, t + 1)
                    nc.vector.tensor_tensor(e.x_nat[:, t, :], e.x_nat[:, t, :], e.vall[:, t, :], ALU.add)


_TRANSPOSED = ["L0_attn_Wq", "L0_attn_Wk", "L0_attn_Wv", "L0_attn_Wo", "L0_xattn_Wq", "L0_xattn_Wk",
               "L0_xattn_Wv", "L0_xattn_Wo", "L0_ffn_weight", "L1_attn_w_attn", "L1_attn_w_proj",
               "L1_attn_w_fc", "L1_attn_w_mlp_proj", "L1_ffn_gate_w"]
_PLAIN = ["L0_attn_q_gamma", "L0_attn_q_beta", "L0_attn_k_gamma", "L0_attn_k_beta", "L0_attn_bo",
          "L0_xattn_bv", "L0_xattn_bo", "L0_ffn_bias", "L1_attn_b_attn",
          "L1_attn_b_proj", "L1_attn_b_mlp_proj", "L1_xattn_q_w", "L1_xattn_k_w", "L1_xattn_v_w", "L1_xattn_v_b", "L1_xattn_o_w", "L1_xattn_o_b",
          "L1_ffn_gate_bias"]

_COLUMNS = ["L0_xattn_bq", "L0_xattn_bk", "L1_attn_b_attn", "L1_attn_b_fc", "L1_xattn_q_b", "L1_xattn_k_b"]


def constants():
    f = np.float32
    rows, cols = np.arange(P)[:, None], np.arange(P)[None, :]
    theta = np.arange(S, dtype=f)[:, None] * np.exp(-(np.arange(0, HD, 2, dtype=f) / f(HD)) * f(np.log(10000.0)))
    cos, sin = np.repeat(np.cos(theta), 2, axis=1), np.repeat(np.sin(theta), 2, axis=1)
    sin = np.concatenate([-sin[:, :HD // 2], sin[:, HD // 2:]], axis=1)
    E = NE - 1
    return {
        "ident": np.eye(P, dtype=f), "masked": f(MASKED) * np.eye(P, dtype=f),
        "upper": np.where(cols > rows, f(MASKED), f(0)),
        "lower": np.where(rows > cols, f(MASKED), f(0)),
        "rope_cos": cos.astype(f), "rope_sin": sin.astype(f),
        "below": (np.arange(E)[None, :] < np.arange(E)[:, None]).astype(f).reshape(-1),
    }


def kernel(**inputs):
    import concourse.bacc as bacc
    from concourse.bass_utils import run_bass_kernel_spmd

    nc = bacc.Bacc("TRN2", target_bir_lowering=False, num_devices=1)
    a = {k: np.asarray(v) for k, v in inputs.items()}
    laid = dict(constants())
    laid["x"] = a["x"][0]
    laid["xT"] = a["x"][0].T
    laid["ctxT"] = a["ctx_1024"][0].T
    laid["mask"] = a["mask_1x1xSxS2_ik0"][0, 0]
    laid["maskT"] = a["mask_1x1xSxS2_ik0"][0, 0].T
    for name in _TRANSPOSED:
        laid[name] = a[name].T
    for name in _PLAIN:
        laid[name] = a[name]
    for name in _COLUMNS:
        laid[name + "_col"] = a[name].reshape(-1, P).T
    for name in ("w1", "w3", "w2"):
        both = np.concatenate([a["L1_ffn_" + name], a["L1_ffn_s" + name][None]])
        laid["moe_" + name] = both.transpose(0, 2, 1).reshape(-1, both.shape[1])
    arrays, dram = {}, {}
    for name, v in laid.items():
        arrays[f"in_{name}"] = np.ascontiguousarray(v)
        dram[name] = nc.dram_tensor(f"in_{name}", v.shape, mybir.dt.from_np(v.dtype), kind="ExternalInput").ap()
    out = nc.dram_tensor("out_x", (S, D), F32, kind="ExternalOutput").ap()
    build(nc, dram, out)
    r = run_bass_kernel_spmd(nc, [arrays], core_ids=[0])
    return r.results[0]["out_x"].reshape(1, S, D)
```

```python
from contextlib import ExitStack, contextmanager

import numpy as np

import concourse.bass as bass
from concourse import mybir

F32 = mybir.dt.float32
BF16 = mybir.dt.bfloat16
F32R = mybir.dt.float32r
I32 = mybir.dt.int32
I16 = mybir.dt.int16
FP8 = mybir.dt.float8e4
ALU = mybir.AluOpType
ACT = mybir.ActivationFunctionType
AX = mybir.AxisListType.X
RMAX = bass.bass_isa.ReduceOp.max

P = 128
S = 2048
S2 = 1601
D = 256
H = 16
HD = D // H
NT = S // P
NT2 = -(-S2 // P)
NC = D // P
CH = 512
HALF = S // 2
SUB = HALF // 4
PARTS = [0, 1, 2, 0, 1, 0], [0, 0, 0, 1, 1, 2]
KQ = HD * 6
KM = KQ + 3
FF = 4 * D
NE = 9
INTER = 512
MASKED = -float(2 ** 30)
SLOTS = 4
FIRST_SEMAPHORE, PHASE_SEMAPHORES = 160, 30
PHASES_SO_FAR = {}


def tiles(n, w):
    return [(a, min(w, n - a)) for a in range(0, n, w)]


@contextmanager
def phase(nc):
    number = nc.next_id()
    turns = PHASES_SO_FAR[id(nc)] = PHASES_SO_FAR.get(id(nc), 0) + 1
    first = FIRST_SEMAPHORE + PHASE_SEMAPHORES * (turns % 2)
    sems = []

    def sem(name):
        assert len(sems) < PHASE_SEMAPHORES
        sems.append(nc.alloc_semaphore(name=f"{name}_{number}", num=first + len(sems)))
        return sems[-1]

    yield sem
    nc.clear_and_free_semaphores(sems)


class Env:
    pass


class Chain:

    def __init__(self, eng, sem, start=0):
        self.eng, self.sem, self.n = eng, sem, start

    def link(self, ins):
        self.n += 1
        ins.then_inc(self.sem, 1)
        self.eng.wait_ge(self.sem, self.n)


def load_phase(nc, e):
    with phase(nc) as sem:
        loaded = sem("loaded")
        with nc.Block() as block:

            @block.sync
            def _(sp):
                pairs = [(e.ident, e.d["ident"])]
                pairs += [(e.wide[:, i * P:(i + 1) * P], e.d[n]) for i, n in enumerate(("masked", "upper", "lower"))]
                pairs += [(e.xT, e.d["xT"].rearrange("(k p) t -> p k t", p=P))]
                for dst, src in pairs:
                    sp.dma_start(dst, src).then_inc(loaded, 16)
                sp.wait_ge(loaded, 16 * len(pairs))

            @block.vector
            def _(dve):
                for vbuf in e.vbuf:
                    nc.vector.memset(vbuf, 1.0)
                nc.vector.memset(e.ones_row, 1.0)
                nc.vector.memset(e.eps5, 1e-5)
                nc.vector.memset(e.eps10, 1e-10)
                dve.wait_ge(loaded, 16 * 5)
                nc.vector.tensor_copy(e.ident16, e.ident)
                for i, dst in enumerate((e.big16, e.upper16, e.lower16)):
                    nc.vector.tensor_copy(dst, e.wide[:, i * P:(i + 1) * P])


def transpose_phase(nc, e, src, dst):
    with phase(nc) as sem:
        turned = sem("turned")
        with nc.Block() as block:
            groups = [(c, g) for g in range(NT // 4) for c in range(NC)]

            @block.tensor
            def _(pe):
                for b, (c, g) in enumerate(groups):
                    for i in range(4):
                        last = nc.tensor.transpose(e.ps[:, b, i * P:(i + 1) * P],
                                                   src[:, 4 * g + i, c * P:(c + 1) * P], e.ident)
                    last.then_inc(turned, 1)

            @block.vector
            def _(dve):
                for b, (c, g) in enumerate(groups):
                    if b % 2 == 0:
                        dve.wait_ge(turned, b + 1)
                        nc.vector.tensor_copy(dst[:, c, g * CH:(g + 1) * CH], e.ps[:, b, :])

            @block.scalar
            def _(act):
                for b, (c, g) in enumerate(groups):
                    if b % 2 == 1:
                        act.wait_ge(turned, b + 1)
                        nc.scalar.activation(dst[:, c, g * CH:(g + 1) * CH], e.ps[:, b, :], ACT.Copy)


def split_phase(nc, e, loads, ahead, jobs):
    work = [(w, bias, scale, src, dst, o, a, n)
            for w, bias, scale, src, length, dst in jobs
            for o in range(NC) for a, n in tiles(length, CH)]
    with phase(nc) as sem:
        loaded, made, whole, high, rest, middle, low = (sem(n) for n in (
            "loaded", "made", "whole", "high", "rest", "middle", "low"))
        ahead_in = sem("ahead_in")
        stored = [sem(f"stored{i}") for i in range(SLOTS)]
        with nc.Block() as block:

            @block.sync
            def _(sp):
                for dst, src in loads:
                    sp.dma_start(dst, src).then_inc(loaded, 16)
                for dst, src in ahead:
                    sp.dma_start(dst, src).then_inc(ahead_in, 16)
                for i, (w, bias, scale, src, dst, o, a, n) in enumerate(work):
                    sp.wait_ge(low, i + 1)
                    sp.wait_ge(middle, i + 1)
                    sp.wait_ge(high, i + 1)
                    sp.dma_start(dst.rearrange("s r t -> r s t")[o * P:(o + 1) * P, :, a:a + n],
                                 e.parts[i % SLOTS][:, :, 0:n]).then_inc(stored[i % SLOTS], 16)
                sp.wait_ge(ahead_in, 16 * len(ahead))
                for j in range(SLOTS):
                    sp.wait_ge(stored[j], 16 * len(range(j, len(work), SLOTS)))

            @block.tensor
            def _(pe):
                if loads:
                    pe.wait_ge(loaded, 16 * len(loads))
                for i, (w, bias, scale, src, dst, o, a, n) in enumerate(work):
                    if i >= 8:
                        pe.wait_ge(whole, i - 7)
                    if w is None:
                        for t in range(n // P):
                            last = nc.tensor.transpose(e.ps[:, i % 8, t * P:(t + 1) * P],
                                                       src[:, a // P + t, o * P:(o + 1) * P], e.ident)
                    else:
                        for c in range(NC):
                            last = nc.tensor.matmul(e.ps[:, i % 8, 0:n], w[:, c, o * P:(o + 1) * P],
                                                    src[:, c, a:a + n], start=(c == 0), stop=(c == NC - 1))
                    last.then_inc(made, 1)

            @block.vector
            def _(dve):
                if loads:
                    dve.wait_ge(loaded, 16 * len(loads))

                def take(i):
                    w, bias, scale, src, dst, o, a, n = work[i]
                    dve.wait_ge(made, i + 1)
                    if i >= SLOTS:
                        dve.wait_ge(high, i - SLOTS + 1)
                    full = e.whole[i % SLOTS][:, 0:n]
                    if bias is None:
                        nc.vector.tensor_scalar(full, e.ps[:, i % 8, 0:n], scale, None, ALU.mult).then_inc(whole, 1)
                    else:
                        nc.vector.tensor_scalar(full, e.ps[:, i % 8, 0:n], bias[:, o:o + 1], scale,
                                                ALU.add, ALU.mult).then_inc(whole, 1)

                take(0)
                take(1)
                for i in range(len(work)):
                    n = work[i][-1]
                    dve.wait_ge(high, i + 1)
                    if i >= SLOTS:
                        dve.wait_ge(low, i - SLOTS + 1)
                    nc.vector.tensor_tensor(e.rest[i % SLOTS][:, 0:n], e.whole[i % SLOTS][:, 0:n],
                                            e.parts[i % SLOTS][:, 0, 0:n], ALU.subtract).then_inc(rest, 1)
                    if i + 2 < len(work):
                        take(i + 2)

            @block.scalar
            def _(act):
                def cut(i, part, src, count, done):
                    n = work[i][-1]
                    act.wait_ge(count, i + 1)
                    nc.scalar.activation(e.parts[i % SLOTS][:, part, 0:n], src[i % SLOTS][:, 0:n], ACT.Copy).then_inc(done, 1)

                for i in range(len(work)):
                    if i >= SLOTS:
                        act.wait_ge(stored[i % SLOTS], 16 * (i // SLOTS))
                    cut(i, 0, e.whole, whole, high)
                    if i:
                        cut(i - 1, 1, e.rest, rest, middle)
                cut(len(work) - 1, 1, e.rest, rest, middle)

            @block.gpsimd
            def _(pool):
                for i, (w, bias, scale, src, dst, o, a, n) in enumerate(work):
                    pool.wait_ge(middle, i + 1)
                    nc.gpsimd.tensor_tensor(e.parts[i % SLOTS][:, 2, 0:n], e.rest[i % SLOTS][:, 0:n],
                                            e.parts[i % SLOTS][:, 1, 0:n], ALU.subtract).then_inc(low, 1)


def attention_phase(nc, e, keys, causal, masked, value, ahead, add_bias=True, masks_ahead=False):
    steps = []
    for half in range(2):
        for t, (a, n) in enumerate(tiles(keys, P)):
            first = max(0, a - half * HALF) if causal else 0
            if first < HALF:
                steps.append((half, t, first, n))
    ns = len(steps)
    half_end = [max(i for i, s in enumerate(steps) if s[0] == half) for half in range(2)]
    units = []
    for t in range(NT):
        if causal:
            pieces = tiles((t + 1) * P, CH)
        else:
            pieces = tiles(keys, -(-keys // -(-keys // CH)))
        units += [(t, i, a, w) for i, (a, w) in enumerate(pieces)]
    nu = len(units)
    assert nu % 2 == 0
    pieces_max = max(u[1] for u in units) + 1
    n_units = nu + 1
    p_slots = 4

    lead = (0.34 if causal else 0.2 if not masked else 0.16) * sum(HALF - s[2] for s in steps)
    width = [HALF - s[2] for s in steps]
    turn = max(i for i in range(ns) if sum(width[i + 1:ns - 2]) >= lead)
    order = list(range(turn + 2, ns)) + list(range(turn + 1))
    share = {i: 0 for i in range(ns)}
    done = 0
    for n, i in enumerate(order):
        upto = nu * sum(width[j] for j in order[:n + 1]) // sum(width[j] for j in order)
        share[i] = (done, upto)
        done = upto
    early = {i: share[i] for i in range(turn + 2, ns)}
    late = {i: share[i] for i in range(turn + 1)}
    early_units = max([b for a, b in early.values()], default=0)

    with phase(nc) as sem:
        sp_waited = sem("sp_waited")
        stacks_in = sem("stacks_in")
        max_out, max_in = sem("max_out"), sem("max_in")
        unit_ready, unit_used, unit_seen = sem("unit_ready"), sem("unit_used"), sem("unit_seen")
        s_ready, exp_done, pv_done = sem("s_ready"), sem("exp_done"), sem("pv_done")
        v_ready = sem("v_ready")
        o_copied, o_turned, o_done = sem("o_copied"), sem("o_turned"), sem("o_done")
        max_chain, norm_chain = sem("max_chain"), sem("norm_chain")
        mpart_set, ones_set = sem("mpart_set"), sem("ones_set")
        wide_ready, wide_used = sem("wide_ready"), sem("wide_used")
        ahead_in = sem("ahead_in")
        v_made, v_kept = sem("v_made"), sem("v_kept")
        mask_in, mask_added, mask_chain, pool_waited = (sem(n) for n in (
            "mask_in", "mask_added", "mask_chain", "pool_waited"))
        v_weights, v_source, v_bias = value
        v_tiles = tiles(keys, P)
        with nc.Block() as block:

            W_PS = [e.ps[:, 3 * i:3 * i + 3, :].rearrange("p a b -> p (a b)") for i in range(2)]
            wides = []
            for t in range(NT):
                n = (t + 1) * P if causal else keys
                wides += [(t, i, a, w) for i, (a, w) in enumerate(tiles(n, n if n <= 3 * CH else -(-n // 2)))]

            def V_PS(t):
                return e.ps[0:v_tiles[t][1], 6 + t % 2, 0:D]

            def number(h, u):
                return h * n_units + u - nu

            S_PS = [e.ps[:, 0:2, :].rearrange("p a b -> p (a b)"), e.ps[:, 2:4, :].rearrange("p a b -> p (a b)")]
            M_PS = [e.ps[:, 4, :], e.ps[:, 5, :]]
            O_PS = [e.ps[:, 6, :], e.ps[:, 7, :]]

            def heads(eng, body):
                body(0, (0, 1, 2), False, True, True)
                body(1, (1, 2, 0), True, True, True)
                with eng.Fori(0, (H - 4) // 3) as three:
                    for j in range(3):
                        body(3 * three + (2 + j), tuple((2 + j + k) % 3 for k in range(3)), True, True, True)
                body(H - 2, tuple((H - 2 + k) % 3 for k in range(3)), True, True, False)
                body(H - 1, tuple((H - 1 + k) % 3 for k in range(3)), True, False, False)

            def masks_before(h):
                return h if isinstance(h, int) and h < 2 else 2 * h - 2

            def p_slot(h, i):
                if i >= p_slots:
                    return i % p_slots, h * ns + i - p_slots + 1
                before = max(j for j in range(ns) if j % p_slots == i)
                return i, (h - 1) * ns + before + 1

            @block.sync
            def _(sp):
                def load(h, buf):
                    for stack, parts, src, n in ((e.ks[buf], PARTS[0], e.kd, keys), (e.qs[buf], PARTS[1], e.qd, S)):
                        for slot, part in enumerate(parts):
                            sp.dma_start(stack[slot * HD:(slot + 1) * HD, 0:n],
                                         src[part, bass.ds(h * HD, HD), 0:n]).then_inc(stacks_in, 16)

                def place_max(h, buf, before):
                    sp.wait_ge(max_chain, h * 4 + 4)
                    sp.sem_inc(sp_waited, 1)
                    if before:
                        sp.wait_ge(max_in, 16 * h)
                        sp.sem_inc(sp_waited, 1)
                    sp.dma_start(e.md.rearrange("s t q -> t s q"), e.mrow).then_inc(max_out, 16)
                    sp.wait_ge(max_out, 16 * (h + 1))
                    sp.sem_inc(sp_waited, 1)
                    sp.dma_start(e.qs[buf][KQ:KM, :], e.md.rearrange("s t q -> s (t q)")).then_inc(max_in, 16)

                def body(h, bufs, has_last, has_next, has_second):
                    if has_second:
                        if has_last:
                            sp.wait_ge(pv_done, h * ns)
                            sp.sem_inc(sp_waited, 1)
                        load(h + 2, bufs[2])
                    if has_next:
                        place_max(h + 1, bufs[1], True)

                load(0, 0)
                load(1, 1)
                for dst, src in ahead:
                    sp.dma_start(dst, src).then_inc(ahead_in, 16)
                place_max(0, 0, False)
                sp.wait_ge(ahead_in, 16 * len(ahead))
                heads(sp, body)

            @block.gpsimd
            def _(pool):
                def values(h, buf):
                    for t, k, n in [(0, keys // P, P)] + ([(keys // P, 1, keys % P)] if keys % P else []):
                        last = nc.gpsimd.tensor_copy(e.vbuf[buf][0:n, t:t + k, 0:HD],
                                                     e.vall[0:n, t:t + k, bass.ds(h * HD, HD)])
                    last.then_inc(v_ready, 1)

                def body(h, bufs, has_last, has_next, has_second):
                    if has_next:
                        if has_last:
                            pool.wait_ge(pv_done, h * ns)
                        values(h + 1, bufs[1])
                    if masks_ahead:
                        if isinstance(h, int) and h == 1:
                            pool.wait_ge(mask_added, 1)
                        add_mask(h)
                        if has_next and not (isinstance(h, int) and h < 2):
                            one_mask(h - 2, S2 - (NT2 - 1) * P if isinstance(h, int) and h == NT2 + 1 else P)

                def stage(src, rows, width):
                    nc.gpsimd.dma_start(e.mask_stage.bitcast(I32)[0:rows, 0:width], src).then_inc(mask_in, 16)

                def add_mask(t):
                    stage(e.d["mask"][bass.ds(t * P, P), :], P, S2)

                def one_mask(t, rows):
                    number = 2 * t + 3
                    full, given = e.mask_stage[0:rows, 0:S], e.mask_stage.bitcast(I32)[0:rows, 0:S]
                    pool.wait_ge(mask_added, t + 3)
                    pool.sem_inc(pool_waited, 1)
                    stage(e.d["maskT"][bass.ds(t * P, rows), :], rows, S)
                    pool.wait_ge(mask_in, 16 * (number + 1))
                    pool.sem_inc(pool_waited, 1)
                    nc.gpsimd.tensor_scalar(full, given, 0.0, None, ALU.is_equal).then_inc(mask_chain, 1)
                    pool.wait_ge(mask_chain, 3 * t + 1)
                    pool.sem_inc(pool_waited, 1)
                    nc.gpsimd.tensor_copy(e.mask_bytes[0:rows, :], full, saturate=False).then_inc(mask_chain, 1)
                    pool.wait_ge(mask_chain, 3 * t + 2)
                    pool.sem_inc(pool_waited, 1)
                    nc.gpsimd.tensor_copy(e.mask_one[0:rows, bass.ds(t, 1), :].rearrange("p o n -> p (o n)").bitcast(I16),
                                          e.mask_bytes[0:rows, :].bitcast(I16)).then_inc(mask_chain, 1)

                if add_bias:
                    pool.wait_ge(ahead_in, 16 * len(ahead))
                    for t in range(NT):
                        nc.gpsimd.tensor_tensor(e.x_nat[:, t, :], e.x_nat[:, t, :], e.b_row, ALU.add)
                pool.wait_ge(v_kept, len(v_tiles))
                values(0, 0)
                heads(pool, body)

            @block.scalar
            def _(act):
                def body(h, bufs, has_last, has_next, has_second):
                    for i, (half, t, first, n) in enumerate(steps):
                        act.wait_ge(s_ready, h * ns + i + 1)
                        slot, free = p_slot(h, i)
                        if has_last or i >= p_slots:
                            act.wait_ge(pv_done, free)
                        nc.scalar.activation(e.prob[slot][0:n, first:HALF], S_PS[i % 2][0:n, first:HALF],
                                             ACT.Exp).then_inc(exp_done, 1)
                for t, (a, n) in enumerate(v_tiles):
                    act.wait_ge(v_made, t + 1)
                    nc.scalar.activation(e.vall[0:n, t, :], V_PS(t), ACT.Copy).then_inc(v_kept, 1)
                heads(act, body)

            @block.tensor
            def _(pe):
                def wide(k):
                    t, i, first, width = wides[k]
                    if k >= 2:
                        pe.wait_ge(wide_used, k - 1)
                    for a, w in tiles(width, CH):
                        diagonal = causal and first + a + w == (t + 1) * P
                        last = nc.tensor.matmul(W_PS[k % 2][:, a:a + w], e.qs[0][0:KQ, t * P:(t + 1) * P],
                                                e.ks[0][0:KQ, first + a:first + a + w], start=True, stop=not diagonal)
                        if diagonal:
                            last = nc.tensor.matmul(W_PS[k % 2][:, a + w - P:a + w], e.ident16, e.upper16,
                                                    start=False, stop=True)
                    last.then_inc(wide_ready, 1)

                def unit(h, buf, u):
                    t, i, a, w = units[u]
                    g = number(h, u)
                    pe.wait_ge(unit_used, g - 1 if u >= 2 else g - u)
                    diagonal = causal and a + w == (t + 1) * P
                    last = nc.tensor.matmul(M_PS[u % 2][:, 0:w], e.qs[buf][0:KQ, t * P:(t + 1) * P],
                                            e.ks[buf][0:KQ, a:a + w], start=True, stop=not diagonal)
                    if diagonal:
                        last = nc.tensor.matmul(M_PS[u % 2][:, w - P:w], e.ident16, e.upper16,
                                                start=False, stop=True)
                    last.then_inc(unit_ready, 1)

                def turn_max(h):
                    if not (isinstance(h, int) and h == 0):
                        pe.wait_ge(unit_used, number(h, nu) - 1)
                    pe.wait_ge(max_chain, h * 4 + 1)
                    nc.tensor.transpose(M_PS[nu % 2][0:NT, 0:P], e.mfin, e.ident).then_inc(unit_ready, 1)

                def scores(h, buf, i, before=True, between=None):
                    half, t, first, n = steps[i]
                    if before or i >= 2:
                        pe.wait_ge(exp_done, h * ns + i - 1)
                    if i == 0:
                        pe.wait_ge(max_in, 16 * (h + 1))
                    kt = e.ks[buf][0:KM, t * P:t * P + n]
                    on_diagonal = causal and t * P >= half * HALF
                    for b in range(2):
                        lo = max(first, b * CH)
                        if lo >= (b + 1) * CH:
                            continue
                        if b == 1 and between:
                            between()
                        diagonal = on_diagonal and lo == first
                        last = nc.tensor.matmul(S_PS[i % 2][0:n, lo:(b + 1) * CH], kt,
                                                e.qs[buf][0:KM, half * HALF + lo:half * HALF + (b + 1) * CH],
                                                start=True, stop=not (diagonal or masked))
                        if diagonal:
                            last = nc.tensor.matmul(S_PS[i % 2][0:n, lo:lo + P], e.ident16, e.lower16,
                                                    start=False, stop=True)
                        if masked:
                            last = nc.tensor.matmul(S_PS[i % 2][0:n, lo:(b + 1) * CH], e.big16[0:n, 0:n],
                                                    e.mask_one[0:n, t, half * HALF + lo:half * HALF + (b + 1) * CH],
                                                    start=False, stop=True)
                    last.then_inc(s_ready, 1)

                def product(h, buf, i, before):
                    half, t, first, n = steps[i]
                    pe.wait_ge(exp_done, h * ns + i + 1)
                    if t == 0:
                        if half == 0:
                            pe.wait_ge(v_ready, h + 1)
                        if before:
                            pe.wait_ge(o_done, (h - 1) * 2 + half + 1)
                    slot = i % p_slots
                    for j in range(4):
                        lo = max(first - j * SUB, 0)
                        if lo >= SUB:
                            continue
                        stop = t == (half * HALF + (j + 1) * SUB) // P - 1 if causal else i == half_end[half]
                        last = nc.tensor.matmul(O_PS[half][32 * j:32 * j + 32, lo:SUB], e.vbuf[buf][0:n, t, :],
                                                e.prob[slot][0:n, j * SUB + lo:(j + 1) * SUB],
                                                start=(t == 0), stop=stop)
                    last.then_inc(pv_done, 1)

                def turn_out(h, half):
                    pe.wait_ge(o_copied, h * 2 + half + 1)
                    for c in range(2):
                        last = nc.tensor.transpose(O_PS[half][:, SUB + c * P:SUB + (c + 1) * P],
                                                   e.osb[half][:, c * P:(c + 1) * P], e.ident)
                    last.then_inc(o_turned, 1)

                def body(h, bufs, has_last, has_next, has_second):
                    for i in range(ns):
                        now = []
                        if has_next and i in late:
                            now = [(h + 1, bufs[1], u) for u in range(*late[i])]
                        if has_second and i in early:
                            if i == turn + 2:
                                pe.wait_ge(stacks_in, 16 * 12 * (h + 3))
                            now = [(h + 2, bufs[2], u) for u in range(*early[i])]
                        if i == turn + 1 and has_next:
                            turn_max(h + 1)

                        def some(n):
                            for _ in range(min(n, len(now))):
                                unit(*now.pop(0))

                        quarter = -(-len(now) // 4)
                        some(quarter)
                        if i + 2 < ns:
                            scores(h, bufs[0], i + 2, between=lambda: some(quarter))
                        elif has_next:
                            scores(h + 1, bufs[1], i + 2 - ns, between=lambda: some(quarter))
                        some(quarter)
                        product(h, bufs[0], i, has_last)
                        some(len(now))
                        if i == half_end[0] + 2:
                            turn_out(h, 0)
                        if i == 3 and has_last:
                            turn_out(h - 1, 1)
                    if not has_next:
                        turn_out(h, 1)

                def value_tile(t):
                    a, n = v_tiles[t]
                    if t >= 2:
                        pe.wait_ge(v_kept, t - 1)
                    for c in range(NC):
                        last = nc.tensor.matmul(V_PS(t), v_source[:, c, a:a + n], v_weights[:, c, :],
                                                start=(c == 0), stop=(c == NC - 1 and not v_bias))
                    if v_bias:
                        last = nc.tensor.matmul(V_PS(t), e.ones_row[0:1, 0:n], e.bv_row[0:1, :], start=False, stop=True)
                    last.then_inc(v_made, 1)

                for t in range(len(v_tiles)):
                    value_tile(t)
                pe.wait_ge(stacks_in, 16 * 24)
                for k in range(len(wides)):
                    wide(k)
                turn_max(0)
                for u in range(early_units):
                    unit(1, 1, u)
                pe.wait_ge(ones_set, 3)
                pe.wait_ge(v_kept, len(v_tiles))
                scores(0, 0, 0, before=False)
                scores(0, 0, 1, before=False)
                heads(pe, body)

            @block.vector
            def _(dve):
                def wide(k):
                    t, i, a, w = wides[k]
                    dve.wait_ge(wide_ready, k + 1)
                    if masked:
                        if k >= 2:
                            dve.wait_ge(wide_used, k - 1)
                        unused = e.scrap[:, 2 * (k % 2):2 * (k % 2) + 2, :].rearrange("p s n -> p (s n)")[:, 0:w]
                        nc.vector.tensor_tensor_reduce(out=unused, in0=W_PS[k % 2][:, 0:w], in1=e.mask_add[:, t, a:a + w],
                                                       scale=1.0, scalar=-3.0e38, op0=ALU.add, op1=ALU.max,
                                                       accum_out=e.mpart[:, t, i:i + 1]).then_inc(wide_used, 1)
                    else:
                        nc.vector.tensor_reduce(e.mpart[:, t, i:i + 1], W_PS[k % 2][:, 0:w], AX, ALU.max).then_inc(wide_used, 1)

                def unit(h, u):
                    t, i, a, w = units[u]
                    g = number(h, u)
                    dve.wait_ge(unit_ready, g + 1)
                    src = M_PS[u % 2][:, 0:w]
                    if masked:
                        if u >= 4 or not (isinstance(h, int) and h == 1):
                            dve.wait_ge(unit_used, g - 3)
                        dve.sem_inc(unit_seen, 1)
                        nc.vector.tensor_tensor_reduce(out=e.scrap[:, u % 4, 0:w], in0=src, in1=e.mask_add[:, t, a:a + w],
                                                       scale=1.0, scalar=-3.0e38, op0=ALU.add, op1=ALU.max,
                                                       accum_out=e.mpart[:, t, i:i + 1]).then_inc(unit_used, 1)
                    else:
                        nc.vector.tensor_reduce(e.mpart[:, t, i:i + 1], src, AX, ALU.max).then_inc(unit_used, 1)

                def finish_max(h):
                    if isinstance(h, int) and h == 0:
                        dve.wait_ge(wide_used, len(wides))
                    else:
                        dve.wait_ge(unit_used, number(h, nu))
                    nc.vector.tensor_reduce(e.mfin, e.mpart[:, :, 0:pieces_max], AX, ALU.max).then_inc(max_chain, 1)

                def cut_max(h, before=True):
                    chain = Chain(dve, max_chain, h * 4 + 1)
                    dve.wait_ge(unit_ready, number(h, nu) + 1)
                    turned = M_PS[nu % 2][0:NT, 0:P]
                    if before:
                        dve.wait_ge(max_out, 16 * h)
                    chain.link(nc.vector.tensor_scalar(e.mrow[:, 0, :], turned, -1.0, None, ALU.mult))
                    chain.link(nc.vector.scalar_tensor_tensor(out=e.mrest, in0=turned, scalar=-1.0,
                                                              in1=e.mrow[:, 0, :], op0=ALU.mult, op1=ALU.subtract))
                    nc.vector.tensor_copy(e.mrow[:, 1, :], e.mrest).then_inc(unit_used, 1)
                    dve.wait_ge(unit_used, number(h, nu) + 1)
                    nc.vector.tensor_tensor(e.mrow[:, 2, :], e.mrest, e.mrow[:, 1, :], ALU.subtract).then_inc(max_chain, 1)

                def copy_out(h, half):
                    dve.wait_ge(pv_done, h * ns + half_end[half] + 1)
                    nc.vector.tensor_copy(e.osb[half], O_PS[half][:, 0:SUB]).then_inc(o_copied, 1)

                def normalise(h, half):
                    dve.wait_ge(o_turned, h * 2 + half + 1)
                    turned = O_PS[half][:, SUB:2 * SUB].rearrange("p (c j r) -> p j c r", c=2, j=4)
                    nc.vector.reciprocal(e.rsum, turned[:, :, :, HD]).then_inc(norm_chain, 1)
                    dve.wait_ge(norm_chain, h * 2 + half + 1)
                    out = e.cn[:, half * 8:half * 8 + 8, bass.ds(h * HD, HD)].rearrange("p (j c) d -> p j c d", j=4)
                    nc.vector.tensor_tensor(out, turned[:, :, :, 0:HD],
                                            e.rsum.unsqueeze(3).broadcast_to([P, 4, 2, HD]), ALU.mult).then_inc(o_done, 1)

                def body(h, bufs, has_last, has_next, has_second):
                    for i in range(ns):
                        if i == half_end[0] + 2:
                            copy_out(h, 0)
                        if i == 2 and has_last:
                            copy_out(h - 1, 1)
                        if has_next and i in late:
                            for u in range(*late[i]):
                                unit(h + 1, u)
                        if has_next and i == turn:
                            finish_max(h + 1)
                        if has_next and i == turn + 1:
                            cut_max(h + 1)
                        if has_second and i in early:
                            for u in range(*early[i]):
                                unit(h + 2, u)
                        if i == half_end[0] + 3:
                            normalise(h, 0)
                        if i == 4 and has_last:
                            normalise(h - 1, 1)
                        if i == 7 and masks_ahead:
                            dve.wait_ge(mask_in, 16 * (masks_before(h) + 1))
                            nc.vector.tensor_scalar(e.mask_add[:, bass.ds(h, 1), :].rearrange("p o n -> p (o n)"),
                                                    e.mask_stage.bitcast(I32)[:, 0:S2], 0.0, MASKED,
                                                    ALU.is_equal, ALU.mult).then_inc(mask_added, 1)
                    if not has_next:
                        copy_out(h, 1)
                        normalise(h, 1)

                nc.vector.memset(e.mpart, -3.0e38).then_inc(mpart_set, 1)
                for ks in e.ks:
                    nc.vector.memset(ks[KQ:KM, :], 1.0).then_inc(ones_set, 1)
                dve.wait_ge(mpart_set, 1)
                for k in range(len(wides)):
                    wide(k)
                finish_max(0)
                cut_max(0, before=False)
                for u in range(early_units):
                    unit(1, u)
                heads(dve, body)


def rope_phase(nc, e):
    G = 4
    N = G * 2 * H
    groups = NT // G
    with phase(nc) as sem:
        loaded, made, centred, squared, spread, rooted, inverse, scaled = (sem(n) for n in (
            "loaded", "made", "centred", "squared", "spread", "rooted", "inverse", "scaled"))
        x_in = sem("x_in")
        chain_sem, pool_sem, spread_tables = sem("chain"), sem("pool_chain"), sem("spread_tables")
        with nc.Block() as block:
            loads = [(e.w_a[:, :, 0:D], e.d["L0_attn_Wq"]), (e.w_a[:, :, D:2 * D], e.d["L0_attn_Wk"]),
                     (e.rope_cos, e.d["rope_cos"].rearrange("(t p) c -> p t c", p=P)),
                     (e.rope_sin, e.d["rope_sin"].rearrange("(t p) c -> p t c", p=P))]
            small = [(e.gamma_s[:, 0, :], "L0_attn_q_gamma"), (e.gamma_s[:, 1, :], "L0_attn_k_gamma"),
                     (e.beta_s[:, 0, :], "L0_attn_q_beta"), (e.beta_s[:, 1, :], "L0_attn_k_beta")]
            n_loads = len(loads) + len(small)

            def group_ps(g):
                return e.ps[:, (g % 2) * G:(g % 2) * G + G, :].rearrange("p t (r d) -> p (t r) d", d=HD)

            def rows(tile):
                return tile.rearrange("p (r d) -> p r d", d=HD)

            @block.sync
            def _(sp):
                for dst, src in loads[:2]:
                    sp.dma_start(dst, src.rearrange("(k p) o -> p k o", p=P)).then_inc(loaded, 16)
                for dst, src in loads[2:]:
                    sp.dma_start(dst, src).then_inc(loaded, 16)
                for dst, name in small:
                    sp.dma_start(dst, e.d[name].partition_broadcast(P)).then_inc(loaded, 16)
                sp.dma_start(e.x_nat, e.d["x"].rearrange("(t p) c -> p t c", p=P)).then_inc(x_in, 16)
                sp.wait_ge(x_in, 16)

            @block.tensor
            def _(pe):
                pe.wait_ge(loaded, 16 * n_loads)
                for g in range(groups):
                    if g >= 2:
                        pe.wait_ge(centred, g - 1)
                    for i in range(G):
                        t = g * G + i
                        for c in range(NC):
                            last = nc.tensor.matmul(e.ps[:, (g % 2) * G + i, :], e.xT[:, c, t * P:(t + 1) * P],
                                                    e.w_a[:, c, :], start=(c == 0), stop=(c == NC - 1))
                    last.then_inc(made, 1)

            @block.scalar
            def _(act):
                for g in range(groups):
                    act.wait_ge(centred, g + 1)
                    if g >= 2:
                        act.wait_ge(spread, g - 1)
                    nc.scalar.activation(e.r_sq[g % 2], e.r_xc[g % 2], ACT.Square).then_inc(squared, 1)
                    act.wait_ge(spread, g + 1)
                    nc.scalar.activation(e.r_std[g % 2], e.r_var[g % 2], ACT.Sqrt, bias=e.eps5, scale=1.0 / HD).then_inc(rooted, 1)

            @block.gpsimd
            def _(pool):
                chain = Chain(pool, pool_sem)
                for g in range(groups):
                    pool.wait_ge(inverse, g + 1)
                    xc = e.r_xc[g % 2]
                    chain.link(nc.gpsimd.tensor_tensor(rows(xc), rows(xc), e.r_inv[g % 2].unsqueeze(2).broadcast_to([P, N, HD]), ALU.mult))
                    four = xc.rearrange("p (t c) -> p t c", t=G)
                    if g == 0:
                        pool.wait_ge(spread_tables, 1)
                    chain.link(nc.gpsimd.tensor_tensor(four, four, e.gamma.unsqueeze(1).broadcast_to([P, G, 2 * D]), ALU.mult))
                    nc.gpsimd.tensor_tensor(four, four, e.beta.unsqueeze(1).broadcast_to([P, G, 2 * D]), ALU.add).then_inc(scaled, 1)

            @block.vector
            def _(dve):
                chain = Chain(dve, chain_sem)
                dve.wait_ge(loaded, 16 * n_loads)
                for table, src in ((e.gamma, e.gamma_s), (e.beta, e.beta_s)):
                    last = nc.vector.tensor_copy(table.rearrange("p (a h d) -> p a h d", a=2, d=HD),
                                                 src.unsqueeze(2).broadcast_to([P, 2, H, HD]))
                last.then_inc(spread_tables, 1)

                def norm(g):
                    ps = group_ps(g)
                    dve.wait_ge(made, g + 1)
                    chain.link(nc.vector.tensor_reduce(e.r_sum[g % 2], ps, AX, ALU.add))
                    nc.vector.scalar_tensor_tensor(out=rows(e.r_xc[g % 2]), in0=e.r_sum[g % 2].unsqueeze(2).broadcast_to([P, N, HD]),
                                                   scalar=-1.0 / HD, in1=ps, op0=ALU.mult, op1=ALU.add).then_inc(centred, 1)
                    dve.wait_ge(squared, g + 1)
                    if g >= 2:
                        dve.wait_ge(rooted, g - 1)
                    nc.vector.tensor_reduce(e.r_var[g % 2], rows(e.r_sq[g % 2]), AX, ALU.add).then_inc(spread, 1)
                    dve.wait_ge(rooted, g + 1)
                    nc.vector.reciprocal(e.r_inv[g % 2], e.r_std[g % 2]).then_inc(inverse, 1)

                def rotate(g):
                    dve.wait_ge(scaled, g + 1)
                    x = e.r_xc[g % 2].rearrange("p (t r d) -> p t r d", t=G, d=HD)
                    pairs = e.r_xc[g % 2].rearrange("p (t r d two) -> p t r d two", t=G, two=2, d=HD // 2)
                    out = e.qkn[:, g * G:(g + 1) * G, :].rearrange("p t (r d) -> p t r d", d=HD)
                    tmp = e.r_sq[g % 2].rearrange("p (t r d) -> p t r d", t=G, d=HD)
                    ts = slice(g * G, (g + 1) * G)
                    for t in range(G):
                        c = e.rope_cos[:, g * G + t, :].unsqueeze(1).broadcast_to([P, 2 * H, HD])
                        s = e.rope_sin[:, g * G + t, :].unsqueeze(1).broadcast_to([P, 2 * H, HD])
                        nc.vector.tensor_tensor(out[:, t], x[:, t], c, ALU.mult)
                        nc.vector.tensor_tensor(tmp[:, t, :, 0:HD // 2], pairs[:, t, :, :, 1], s[:, :, 0:HD // 2], ALU.mult)
                        last = nc.vector.tensor_tensor(tmp[:, t, :, HD // 2:], pairs[:, t, :, :, 0], s[:, :, HD // 2:], ALU.mult)
                    chain.link(last)
                    chain.link(nc.vector.tensor_tensor(e.qkn[:, ts, :].rearrange("p t c -> p (t c)"),
                                                       e.qkn[:, ts, :].rearrange("p t c -> p (t c)"), e.r_sq[g % 2], ALU.add))

                norm(0)
                for g in range(groups):
                    if g + 1 < groups:
                        norm(g + 1)
                    rotate(g)


def output_phase(nc, e, loads, products, addend, bias_row, total, normed, eps, scale=None, turn=True):
    with phase(nc) as sem:
        loaded, made, used, biased = sem("loaded"), sem("made"), sem("used"), sem("biased")
        measured, rooted, chain_sem, stored = sem("measured"), sem("rooted"), sem("chain"), sem("stored")
        normed_sem, turned = sem("normed"), sem("turned")
        groups = [(c, g) for g in range(NT // 4) for c in range(NC)] if turn else []
        with nc.Block() as block:
            store = normed is None

            def keep(copy, b, **more):
                c, g = groups[b]
                return copy(e.xT[:, c, g * CH:(g + 1) * CH], e.ps[:, b, :], **more)
            dst = e.cn if store else normed

            @block.sync
            def _(sp):
                for d, s in loads:
                    sp.dma_start(d, s).then_inc(loaded, 16)
                if store:
                    for t in range(0, NT, 4):
                        sp.wait_ge(normed_sem, t + 4)
                        sp.dma_start(e.out.rearrange("(t p) c -> p t c", p=P)[:, t:t + 4, :],
                                     dst[:, t:t + 4, :]).then_inc(stored, 16)
                    sp.wait_ge(stored, 16 * NT // 4)

            @block.gpsimd
            def _(pool):
                if bias_row is not None and scale is None:
                    for t in range(NT):
                        nc.gpsimd.tensor_tensor(total[:, t, :], addend[:, t, :], bias_row, ALU.add).then_inc(biased, 1)

            @block.tensor
            def _(pe):
                if products is not None:
                    if loads:
                        pe.wait_ge(loaded, 16 * len(loads))
                    for t in range(NT):
                        if t >= 8:
                            pe.wait_ge(used, t - 7)
                        products(t, e.ps[:, t % 8, 0:D]).then_inc(made, 1)
                for b, (c, g) in enumerate(groups):
                    pe.wait_ge(normed_sem, 4 * g + 4)
                    for i in range(4):
                        last = nc.tensor.transpose(e.ps[:, b, i * P:(i + 1) * P],
                                                   dst[:, 4 * g + i, c * P:(c + 1) * P], e.ident)
                    last.then_inc(turned, 1)

            @block.vector
            def _(dve):
                chain = Chain(dve, chain_sem)
                if loads:
                    dve.wait_ge(loaded, 16 * len(loads))
                for t in range(NT):
                    y = total[:, t, :]
                    if products is not None:
                        dve.wait_ge(made, t + 1)
                        ps = e.ps[:, t % 8, 0:D]
                        if scale is not None:
                            nc.vector.scalar_tensor_tensor(out=e.rounded[t % 2], in0=ps, scalar=scale, in1=bias_row,
                                                           op0=ALU.mult, op1=ALU.add).then_inc(used, 1)
                            dve.wait_ge(used, t + 1)
                            chain.link(nc.vector.tensor_tensor(y, addend[:, t, :], e.rounded[t % 2], ALU.add))
                        else:
                            a = addend
                            if bias_row is not None:
                                dve.wait_ge(biased, t + 1)
                                a = total
                            nc.vector.tensor_tensor(y, ps, a[:, t, :], ALU.add).then_inc(used, 1)
                            dve.wait_ge(used, t + 1)
                    chain.link(nc.vector.bn_stats(e.stats[:, t, :], y))
                    last = nc.vector.bn_aggr(e.mv[:, t, :], e.stats[:, t, :])
                last.then_inc(measured, 1)
                dve.wait_ge(rooted, 1)
                chain.link(nc.vector.reciprocal(e.rstd, e.std))
                for t in range(NT):
                    nc.vector.tensor_scalar(dst[:, t, :], total[:, t, :], e.mv[:, t, 0:1], e.rstd[:, t:t + 1],
                                            ALU.subtract, ALU.mult).then_inc(normed_sem, 1)
                for b in range(1, len(groups), 2):
                    dve.wait_ge(turned, b + 1)
                    keep(nc.vector.tensor_copy, b)

            @block.scalar
            def _(act):
                act.wait_ge(measured, 1)
                nc.scalar.activation(e.std, e.mv[:, :, 1], ACT.Sqrt, bias=eps).then_inc(rooted, 1)
                for b in range(0, len(groups), 2):
                    act.wait_ge(turned, b + 1)
                    keep(nc.scalar.activation, b, func=ACT.Copy)


def fp8_phase(nc, e):
    with phase(nc) as sem:
        loaded, amax, chain_sem, reduced = sem("loaded"), sem("amax"), sem("chain"), sem("reduced")
        piece_done, piece_steps = [sem(f"piece_done{k}") for k in range(2)], [0, 0]
        with nc.Block() as block:
            w = e.w_a[:, :, 0:D]
            jobs = [(e.xT[:, c, a:a + n], e.xq[:, c, a:a + n], 0) for c in range(NC) for a, n in tiles(S, CH)]
            jobs += [(w[:, c, :], e.wq[:, c, :], 1) for c in range(NC)]

            @block.sync
            def _(sp):
                sp.dma_start(w, e.d["L0_ffn_weight"].rearrange("(k p) o -> p k o", p=P)).then_inc(loaded, 16)
                sp.dma_start(e.b_row, e.d["L0_ffn_bias"].partition_broadcast(P)).then_inc(loaded, 16)

            @block.gpsimd
            def _(pool):
                pool.wait_ge(amax, 2)
                nc.gpsimd.partition_all_reduce(e.amax_all, e.amax, P, RMAX).then_inc(reduced, 1)

            @block.vector
            def _(dve):
                chain = Chain(dve, chain_sem)
                nc.vector.tensor_reduce(e.amax[:, 0:1], e.x_nat.rearrange("p t c -> p (t c)"), AX, ALU.max,
                                        apply_absolute_value=True).then_inc(amax, 1)
                dve.wait_ge(loaded, 32)
                nc.vector.tensor_reduce(e.amax[:, 1:2], w, mybir.AxisListType.XY, ALU.max,
                                        apply_absolute_value=True).then_inc(amax, 1)
                dve.wait_ge(reduced, 1)
                chain.link(nc.vector.tensor_scalar(e.amax_all, e.amax_all, 1e-12, None, ALU.max))
                chain.link(nc.vector.reciprocal(e.qscale, e.amax_all))
                chain.link(nc.vector.tensor_scalar(e.qscale, e.qscale, 448.0, 448.0, ALU.mult, ALU.min))
                chain.link(nc.vector.reciprocal(e.descale, e.qscale))
                chain.link(nc.vector.tensor_tensor(e.descale2, e.descale[:, 0:1], e.descale[:, 1:2], ALU.mult))
                for pair in range(0, len(jobs), 2):
                    two = []
                    for i, (src, dst, which) in enumerate(jobs[pair:pair + 2]):
                        n = src.shape[1]
                        two.append((src, dst, which, e.whole[i][:, 0:n], e.rest[i][:, 0:n]))

                    def both(step):
                        for k, piece in enumerate(two):
                            dve.wait_ge(piece_done[k], piece_steps[k])
                            step(*piece).then_inc(piece_done[k], 1)
                            piece_steps[k] += 1

                    both(lambda src, dst, which, v, m: nc.vector.tensor_scalar(
                        v, src, e.qscale[:, which:which + 1], 448.0, ALU.mult, ALU.min))
                    both(lambda src, dst, which, v, m: nc.vector.tensor_scalar(v, v, -448.0, None, ALU.max))
                    both(lambda src, dst, which, v, m: nc.vector.tensor_scalar(
                        m.bitcast(I32), v.bitcast(I32), 0x7F800000, None, ALU.bitwise_and))
                    both(lambda src, dst, which, v, m: nc.vector.tensor_scalar(
                        m, m, 2.0 ** -6, 1.5 * 2.0 ** 20, ALU.max, ALU.mult))
                    both(lambda src, dst, which, v, m: nc.vector.tensor_tensor(v, v, m, ALU.add))
                    both(lambda src, dst, which, v, m: nc.vector.tensor_tensor(dst, v, m, ALU.subtract))


def mlp_phase(nc, e):
    nf = FF // P
    with phase(nc) as sem:
        loaded, up_ready, act_done, down_ready, added = (sem(n) for n in (
            "loaded", "up_ready", "act_done", "down_ready", "added"))
        with nc.Block() as block:
            chunks = tiles(S, CH)

            @block.sync
            def _(sp):
                sp.dma_start(e.w_fc, e.d["L1_attn_w_fc"].rearrange("(k p) o -> p k o", p=P)).then_inc(loaded, 16)
                sp.dma_start(e.w_mp, e.d["L1_attn_w_mlp_proj"].rearrange("(k p) o -> p k o", p=P)).then_inc(loaded, 16)
                sp.dma_start(e.b_fc, e.d["L1_attn_b_fc_col"]).then_inc(loaded, 16)
                sp.dma_start(e.b_row, e.d["L1_attn_b_mlp_proj"].partition_broadcast(P)).then_inc(loaded, 16)

            @block.tensor
            def _(pe):
                pe.wait_ge(loaded, 64)

                def up(i, a):
                    for f in range(nf):
                        g = i * nf + f
                        if g >= 4:
                            pe.wait_ge(act_done, g - 3)
                        for c in range(NC):
                            last = nc.tensor.matmul(e.ps[:, g % 4, :], e.w_fc[:, c, f * P:(f + 1) * P],
                                                    e.xT[:, c, a:a + CH], start=(c == 0), stop=(c == NC - 1))
                        last.then_inc(up_ready, 1)

                def down(i):
                    pe.wait_ge(act_done, (i + 1) * nf)
                    for t in range(4):
                        g = i * 4 + t
                        if g >= 4:
                            pe.wait_ge(added, g - 3)
                        for f in range(nf):
                            last = nc.tensor.matmul(e.ps[:, 4 + g % 4, 0:D], e.hT[i % 2][:, f, t * P:(t + 1) * P],
                                                    e.w_mp[:, f, :], start=(f == 0), stop=False)
                        last = nc.tensor.matmul(e.ps[:, 4 + g % 4, 0:D], e.ones_row, e.b_row[0:1, :], start=False, stop=True)
                        last.then_inc(down_ready, 1)

                for i, (a, n) in enumerate(chunks):
                    up(i, a)
                    if i:
                        down(i - 1)
                down(len(chunks) - 1)

            @block.scalar
            def _(act):
                act.wait_ge(loaded, 64)
                for i in range(len(chunks)):
                    if i >= 2:
                        act.wait_ge(down_ready, (i - 1) * 4)
                    for f in range(nf):
                        act.wait_ge(up_ready, i * nf + f + 1)
                        nc.scalar.activation(e.hT[i % 2][:, f, :], e.ps[:, (i * nf + f) % 4, :], ACT.Gelu_apprx_tanh,
                                             bias=e.b_fc[:, f:f + 1]).then_inc(act_done, 1)

            @block.vector
            def _(dve):
                for t in range(NT):
                    dve.wait_ge(down_ready, t + 1)
                    nc.vector.tensor_tensor(e.vall[:, t, :], e.vall[:, t, :], e.ps[:, 4 + t % 4, 0:D],
                                            ALU.add).then_inc(added, 1)
                    dve.wait_ge(added, t + 1)
                    nc.vector.tensor_tensor(e.x_nat[:, t, :], e.x_nat[:, t, :], e.vall[:, t, :], ALU.add)


def load_expert(sp, e, x, arrived):
    for dst, name in zip(e.moe_in, ("w1", "w3", "w2")):
        src = e.d["moe_" + name]
        rows = src.shape[0] // NE
        sp.dma_start(dst, src[bass.ds(x * rows, rows), :].rearrange("(k p) o -> p k o", p=P)).then_inc(arrived, 16)


def gate_phase(nc, e):
    E = NE - 1
    with phase(nc) as sem:
        loaded, made, exped, chain_sem, copied = sem("loaded"), sem("made"), sem("exped"), sem("chain"), sem("copied")
        centred, first_weights = sem("centred"), sem("first_weights")
        with nc.Block() as block:
            shape3, shape4 = [P, NT, E], [P, NT, E, E]

            @block.sync
            def _(sp):
                sp.dma_start(e.w_gate, e.d["L1_ffn_gate_w"].rearrange("(k p) o -> p k o", p=P)).then_inc(loaded, 16)
                sp.dma_start(e.b_gate, e.d["L1_ffn_gate_bias"].partition_broadcast(P)).then_inc(loaded, 16)
                sp.dma_start(e.below, e.d["below"].partition_broadcast(P)).then_inc(loaded, 16)
                load_expert(sp, e, 0, first_weights)
                sp.wait_ge(first_weights, 16 * 3)

            @block.gpsimd
            def _(pool):
                nc.gpsimd.tensor_copy(e.cn, e.x_nat).then_inc(copied, 1)

            @block.tensor
            def _(pe):
                pe.wait_ge(loaded, 48)
                for t in range(NT):
                    for c in range(NC):
                        last = nc.tensor.matmul(e.ps[:, 0, t * E:(t + 1) * E], e.xT[:, c, t * P:(t + 1) * P],
                                                e.w_gate[:, c, :], start=(c == 0), stop=(c == NC - 1))
                last.then_inc(made, 1)

            @block.scalar
            def _(act):
                act.wait_ge(centred, 1)
                nc.scalar.activation(e.g_p, e.g_p, ACT.Exp).then_inc(exped, 1)

            @block.vector
            def _(dve):
                chain = Chain(dve, chain_sem)
                logits = e.ps[:, 0, 0:NT * E].rearrange("p (t e) -> p t e", e=E)
                nc.vector.memset(e.comb, 1.0).then_inc(chain_sem, 1)
                chain.n += 1
                dve.wait_ge(loaded, 48)
                dve.wait_ge(made, 1)
                chain.link(nc.vector.tensor_reduce(e.g_r, logits, AX, ALU.max))
                nc.vector.tensor_tensor(e.g_p, logits, e.g_r.unsqueeze(2).broadcast_to(shape3), ALU.subtract).then_inc(centred, 1)
                dve.wait_ge(exped, 1)
                chain.link(nc.vector.tensor_reduce(e.g_r, e.g_p, AX, ALU.add))
                chain.link(nc.vector.reciprocal(e.g_r, e.g_r))
                chain.link(nc.vector.tensor_tensor(e.g_p, e.g_p, e.g_r.unsqueeze(2).broadcast_to(shape3), ALU.mult))
                chain.link(nc.vector.tensor_tensor(e.g_b, e.g_p, e.b_gate.unsqueeze(1).broadcast_to(shape3), ALU.add))
                rival = e.g_b.unsqueeze(2).broadcast_to(shape4)
                own = e.g_b.unsqueeze(3).broadcast_to(shape4)
                chain.link(nc.vector.tensor_tensor(e.g_eq, rival, own, ALU.is_equal))
                chain.link(nc.vector.tensor_tensor(e.g_eq.rearrange("p t i j -> p t (i j)"), e.g_eq.rearrange("p t i j -> p t (i j)"),
                                                   e.below.unsqueeze(1).broadcast_to([P, NT, E * E]), ALU.mult))
                chain.link(nc.vector.tensor_tensor(e.g_gt, rival, own, ALU.is_gt))
                chain.link(nc.vector.tensor_tensor(e.g_gt, e.g_gt, e.g_eq, ALU.add))
                chain.link(nc.vector.tensor_reduce(e.g_b, e.g_gt, AX, ALU.add))
                chain.link(nc.vector.tensor_scalar(e.g_b, e.g_b, 2.0, None, ALU.is_lt))
                chain.link(nc.vector.tensor_tensor(e.comb[:, :, 0:E], e.g_b, e.g_p, ALU.mult))


def moe_phase(nc, e):
    ni = INTER // P
    nch = S // CH
    with phase(nc) as sem:
        weights_in, weights_chain, weights_ready = sem("weights_in"), sem("weights_chain"), sem("weights_ready")
        weight_col, pool_waited = sem("weight_col"), sem("pool_waited")
        x_rounded, x_ready = sem("x_rounded"), sem("x_ready")
        ab_ready, silu_done, h_made, h_rounded, h_ready, y_ready, y_added = (sem(n) for n in (
            "ab_ready", "silu_done", "h_made", "h_rounded", "h_ready", "y_ready", "y_added"))
        with nc.Block() as block:

            def experts(eng, body):
                for x in range(3):
                    body(x, x % 2)
                with eng.Fori(0, (NE - 5) // 2) as pair:
                    body(2 * pair + 3, 1)
                    body(2 * pair + 4, 0)
                for x in range(NE - 2, NE):
                    body(x, x % 2)

            def known(x, limit=1):
                return isinstance(x, int) and x < limit

            @block.sync
            def _(sp):
                with sp.Fori(1, NE) as x:
                    sp.wait_ge(weights_ready, 3 * x)
                    load_expert(sp, e, x, weights_in)

            def weight_parts(par, m):
                return (w[m].rearrange("p k n -> p (k n)") for w in (e.moe_in, *e.moe_w[par]))

            @block.gpsimd
            def _(pool):
                def split(x, par, m):
                    pool.wait_ge(weights_in, 16 * 3 * x)
                    pool.sem_inc(pool_waited, 1)
                    full, rounded, rest = weight_parts(par, m)
                    nc.gpsimd.tensor_copy(rounded, full).then_inc(weights_chain, 1)
                    pool.wait_ge(weights_chain, 3 * x + m + 1)
                    nc.gpsimd.tensor_tensor(rest, full, rounded.bitcast(F32), ALU.subtract).then_inc(weights_ready, 1)

                def body(x, par):
                    if not known(x, 2):
                        pool.wait_ge(y_added, (x - 1) * NT)
                    nc.gpsimd.tensor_copy(e.comb_x[par], e.comb[:, :, bass.ds(x, 1)].rearrange("p t o -> p (t o)")
                                          ).then_inc(weight_col, 1)
                    for c in range(nch):
                        if c and not (isinstance(x, int) and x == NE - 1):
                            if c == 1 and not known(x):
                                pool.wait_ge(y_ready, x * NT)
                            split(x + 1, 1 - par, c - 1)
                        for i in range(ni):
                            pool.wait_ge(h_rounded, x * nch * ni + c * ni + i + 1)
                            nc.gpsimd.tensor_tensor(e.moe_h[c % 2][1][:, i, :], e.moe_f[i % 2],
                                                    e.moe_h[c % 2][0][:, i, :].bitcast(F32), ALU.subtract).then_inc(h_ready, 1)
                experts(pool, body)

            @block.tensor
            def _(pe):
                def three(out, wr, wl, xr, xl, first, last):
                    nc.tensor.matmul(out, wr, xr, start=first, stop=False)
                    nc.tensor.matmul(out, wr, xl, start=False, stop=False)
                    return nc.tensor.matmul(out, wl, xr, start=False, stop=last)

                def up(x, par, c):
                    for i in range(ni):
                        k = x * nch * ni + c * ni + i
                        if not (isinstance(x, int) and k < 2):
                            pe.wait_ge(h_made, k - 1)
                        for b in range(2):
                            for h in range(NC):
                                wr, wl = (w[b][:, h, i * P:(i + 1) * P] for w in e.moe_w[par])
                                xr, xl = (p[:, h, c * CH:(c + 1) * CH] for p in e.x_parts)
                                last = three(e.ps[:, 2 * (i % 2) + b, :], wr, wl, xr, xl, h == 0, h == NC - 1)
                        last.then_inc(ab_ready, 1)

                def down(x, par, c):
                    pe.wait_ge(h_ready, x * nch * ni + (c + 1) * ni)
                    for t in range(4):
                        g = x * NT + c * 4 + t
                        if not (isinstance(x, int) and g < 4):
                            pe.wait_ge(y_added, g - 3)
                        for i in range(ni):
                            hr, hl = (h[:, i, t * P:(t + 1) * P] for h in e.moe_h[c % 2])
                            wr, wl = (w[2][:, i, :] for w in e.moe_w[par])
                            last = three(e.ps[:, 4 + t, 0:D], hr, hl, wr, wl, i == 0, i == ni - 1)
                        last.then_inc(y_ready, 1)

                def body(x, par):
                    pe.wait_ge(weights_ready, 3 * (x + 1))
                    for c in range(nch):
                        if known(x):
                            pe.wait_ge(x_ready, 2 * (c + 1))
                        up(x, par, c)
                        if c:
                            down(x, par, c - 1)
                        elif not known(x):
                            down(x - 1, 1 - par, nch - 1)
                experts(pe, body)
                down(NE - 1, 0, nch - 1)

            @block.scalar
            def _(act):
                def silu(k, i, started):
                    act.wait_ge(ab_ready, k + 1)
                    if started:
                        act.wait_ge(h_made, k - 1)
                    nc.scalar.activation(e.moe_s[i % 2], e.ps[:, 2 * (i % 2), :], ACT.Silu).then_inc(silu_done, 1)

                def rounded(k, c, i):
                    act.wait_ge(h_made, k + 1)
                    nc.scalar.activation(e.moe_h[c % 2][0][:, i, :], e.moe_f[i % 2], ACT.Copy).then_inc(h_rounded, 1)

                def body(x, par):
                    for c in range(nch):
                        first = x * nch * ni + c * ni
                        silu(first, 0, not (known(x) and c == 0))
                        if not (isinstance(x, int) and x * nch + c < 2):
                            act.wait_ge(y_ready, x * NT + (c - 1) * 4)
                        for i in range(ni):
                            if i + 1 < ni:
                                silu(first + i + 1, i + 1, not (known(x) and c == 0 and i == 0))
                            rounded(first + i, c, i)

                for m in range(3):
                    full, rounded_part, rest = weight_parts(0, m)
                    nc.scalar.activation(rounded_part, full, ACT.Copy).then_inc(weights_chain, 1)
                for c in range(nch):
                    for h in range(NC):
                        cols = slice(c * CH, (c + 1) * CH)
                        nc.scalar.activation(e.x_parts[0][:, h, cols], e.xT[:, h, cols], ACT.Copy).then_inc(x_rounded, 1)
                experts(act, body)

            @block.vector
            def _(dve):
                def gated(x, c):
                    for i in range(ni):
                        k = x * nch * ni + c * ni + i
                        dve.wait_ge(silu_done, k + 1)
                        if not (isinstance(x, int) and k < 2):
                            dve.wait_ge(h_ready, k - 1)
                        nc.vector.tensor_tensor(e.moe_f[i % 2], e.moe_s[i % 2], e.ps[:, 2 * (i % 2) + 1, :],
                                                ALU.mult).then_inc(h_made, 1)

                def add(x, par, c):
                    dve.wait_ge(weight_col, x + 1)
                    for t in range(4):
                        g = x * NT + c * 4 + t
                        dve.wait_ge(y_ready, g + 1)
                        tile = e.cn[:, c * 4 + t, :]
                        if not known(x):
                            dve.wait_ge(y_added, g + 1 - NT)
                        nc.vector.scalar_tensor_tensor(out=tile, in0=e.ps[:, 4 + t, 0:D],
                                                       scalar=e.comb_x[par][:, c * 4 + t:c * 4 + t + 1], in1=tile,
                                                       op0=ALU.mult, op1=ALU.add).then_inc(y_added, 1)

                def body(x, par):
                    for c in range(nch):
                        gated(x, c)
                        if c:
                            add(x, par, c - 1)
                        elif not known(x):
                            add(x - 1, 1 - par, nch - 1)

                for m in range(3):
                    full, rounded_part, rest = weight_parts(0, m)
                    dve.wait_ge(weights_chain, m + 1)
                    nc.vector.tensor_tensor(rest, full, rounded_part.bitcast(F32), ALU.subtract).then_inc(weights_ready, 1)
                for c in range(nch):
                    for h in range(NC):
                        cols = slice(c * CH, (c + 1) * CH)
                        dve.wait_ge(x_rounded, NC * c + h + 1)
                        nc.vector.tensor_tensor(e.x_parts[1][:, h, cols], e.xT[:, h, cols],
                                                e.x_parts[0][:, h, cols].bitcast(F32), ALU.subtract).then_inc(x_ready, 1)
                experts(dve, body)
                add(NE - 1, 0, nch - 1)


def build(nc, dram, out):
    e = Env()
    e.d, e.out = dram, out
    with ExitStack() as ctx, ExitStack() as early:
        def sb(name, cols, dt=F32, rows=P, until=ctx):
            return until.enter_context(nc.sbuf_tensor(name, [rows, cols], dt))[:, :]

        def dr(name, shape, dt):
            return nc.dram_tensor(name, shape, dt, kind="Internal").ap()

        e.qd, e.kd = dr("q_parts", (3, D, S), BF16), dr("k_parts", (3, D, S), BF16)
        e.md = dr("max_parts", (3, NT, P), BF16)

        def natural(ap):
            return ap.rearrange("p (t c) -> p t c", c=D)

        def halves(ap):
            return ap.rearrange("p (k n) -> p k n", k=NC)

        e.x_nat = natural(sb("x_nat", NT * D))
        e.xT = halves(sb("xT", NC * S))
        e.cn = natural(sb("cn", NT * D))
        e.vall = natural(sb("vall", NT * D))
        e.osb = [sb(f"osb{i}", SUB) for i in range(2)]
        e.ident = sb("ident", P)
        e.ident16, e.big16 = sb("ident16", P, BF16), sb("big16", P, BF16)
        e.upper16, e.lower16 = sb("upper16", P, BF16), sb("lower16", P, BF16)
        e.b_row = sb("b_row", D)
        e.bv_row = sb("bv_row", D)
        bcol = sb("bcol", 4)
        e.bq_col, e.bk_col = bcol[:, 0:2], bcol[:, 2:4]
        e.mpart = sb("mpart", NT * 4).rearrange("p (t i) -> p t i", i=4)
        e.ones_row = sb("ones_row", P, F32, 1)
        e.mfin = sb("mfin", NT)
        e.mrow = sb("mrow", 3 * P, BF16, NT).rearrange("t (s q) -> t s q", s=3)
        e.mrest = sb("mrest", P, F32, NT)
        e.rsum = sb("rsum", 8).rearrange("p (j c) -> p j c", j=4)
        e.scrap = sb("scrap", 4 * CH, BF16).rearrange("p (s n) -> p s n", s=4)
        e.stats = sb("stats", NT * 6).rearrange("p (t s) -> p t s", s=6)
        e.mv = sb("mv", NT * 2).rearrange("p (t s) -> p t s", s=2)
        e.std, e.rstd = sb("std", NT), sb("rstd", NT)
        small = sb("small", 16)
        e.eps5, e.eps10 = small[:, 0:1], small[:, 1:2]
        e.amax, e.amax_all = small[:, 2:4], small[:, 4:6]
        e.qscale, e.descale, e.descale2 = small[:, 8:10], small[:, 10:12], small[:, 12:13]
        e.ps = ctx.enter_context(nc.psum_tensor("ps", [P, 8, CH], F32))
        e.comb = sb("comb", NT * NE).rearrange("p (t x) -> p t x", t=NT)
        e.comb_x = [sb(f"comb_x{i}", NT) for i in range(2)]
        arena = sb("arena", 19500, until=early)
        stacks = sb("stacks", 6 * S // 2, until=early)
        probs = sb("probs", 4 * HALF, until=early)
        vbufs = sb("vbufs", 3 * NT * 32, until=early)
        wbuf = sb("wbuf", 4 * 2 * D, until=early)
        e.vbuf = [vbufs[:, i * NT * 32:(i + 1) * NT * 32].rearrange("p (t r) -> p t r", r=32) for i in range(3)]
        e.w_a = halves(wbuf[:, 0:1024])
        e.w_v = halves(wbuf[:, 1024:1536])
        e.w_o = halves(wbuf[:, 1536:2048])

        s16 = stacks.bitcast(BF16)
        e.ks = [s16[:, i * S:(i + 1) * S] for i in range(3)]
        e.qs = [s16[:, (3 + i) * S:(4 + i) * S] for i in range(3)]
        e.prob = [probs[:, i * HALF:(i + 1) * HALF] for i in range(4)]
        e.ctxT = probs[:, 0:NC * S2].rearrange("p (k n) -> p k n", k=NC)
        slot_words = 2 * CH + 3 * CH // 2
        slots = [stacks[:, i * slot_words:(i + 1) * slot_words] for i in range(SLOTS - 1)]
        slots.append(e.cn.rearrange("p t c -> p (t c)")[:, 0:slot_words])
        e.whole, e.rest = [s[:, 0:CH] for s in slots], [s[:, CH:2 * CH] for s in slots]
        e.parts = [s[:, 2 * CH:].bitcast(BF16).rearrange("p (s n) -> p s n", s=3) for s in slots]

        e.mask_add = arena[:, 0:NT * S2 // 2].bitcast(BF16).rearrange("p (t n) -> p t n", t=NT)
        at = NT * S2 // 2
        e.mask_one = arena[:, at:at + NT2 * S // 4].bitcast(FP8).rearrange("p (t n) -> p t n", t=NT2)
        e.mask_stage = wbuf
        e.mask_bytes = e.scrap.rearrange("p s n -> p (s n)").bitcast(FP8)[:, 0:S]

        e.wide = arena[:, 0:3 * P]

        a = 0

        def take(n):
            nonlocal a
            a += n
            return arena[:, a - n:a]
        e.qkn = take(NT * 2 * D).rearrange("p (t c) -> p t c", t=NT)
        e.r_xc, e.r_sq = [take(2048) for _ in range(2)], [take(2048) for _ in range(2)]
        e.rope_cos, e.rope_sin = e.vall[:, 0], e.vall[:, 1]
        e.rope_cos, e.rope_sin = (v.rearrange("p (t d) -> p t d", t=NT) for v in (e.rope_cos, e.rope_sin))
        cnf = e.cn.rearrange("p t c -> p (t c)")
        e.gamma, e.beta = cnf[:, 0:512], cnf[:, 512:1024]
        e.gamma_s, e.beta_s = (cnf[:, 1024 + 32 * i:1056 + 32 * i].rearrange("p (a d) -> p a d", a=2) for i in range(2))
        e.r_sum, e.r_var, e.r_std, e.r_inv = ([cnf[:, 1088 + 256 * i + 128 * j:1088 + 256 * i + 128 * (j + 1)] for j in range(2)]
                                              for i in range(4))

        e.xq = arena[:, 0:S].bitcast(BF16).rearrange("p (k n) -> p k n", k=NC)
        e.wq = arena[:, S:S + D].bitcast(BF16).rearrange("p (k n) -> p k n", k=NC)
        rounded = arena[:, S + D:S + 2 * D].bitcast(BF16)
        e.rounded = [rounded[:, i * D:(i + 1) * D] for i in range(2)]

        a = 0
        e.w_fc = take(NC * FF).rearrange("p (k n) -> p k n", k=NC)
        e.w_mp = take(FF // P * D).rearrange("p (k n) -> p k n", n=D)
        e.hT = [take(FF // P * CH).rearrange("p (f n) -> p f n", n=CH) for _ in range(2)]
        e.b_fc = take(FF // P)

        E = NE - 1
        vf = e.vall.rearrange("p t c -> p (t c)")
        a = 0

        def take_p(n):
            nonlocal a
            a += n
            return probs[:, a - n:a]
        e.w_gate = take_p(NC * E).rearrange("p (k n) -> p k n", k=NC)
        e.b_gate, e.below = take_p(E), take_p(E * E)
        e.g_r = take_p(NT)
        e.g_p, e.g_b = (take_p(NT * E).rearrange("p (t x) -> p t x", t=NT) for _ in range(2))
        e.g_eq, e.g_gt = (take_p(NT * E * E).rearrange("p (t i j) -> p t i j", t=NT, i=E) for _ in range(2))

        def weights(pool):
            return [pool[:, 0:NC * INTER].rearrange("p (k n) -> p k n", k=NC),
                    pool[:, NC * INTER:2 * NC * INTER].rearrange("p (k n) -> p k n", k=NC),
                    pool[:, 2 * NC * INTER:].rearrange("p (k n) -> p k n", n=D)]
        whole = 2 * NC * INTER + INTER // P * D
        e.moe_in = weights(vf[:, 0:whole])
        e.moe_s = [vf[:, whole + i * CH:whole + (i + 1) * CH] for i in range(2)]

        def expert_memory():
            early.close()
            e.moe_w = [[weights(sb(f"moe_w{par}{part}", whole, F32R)) for part in range(2)] for par in range(2)]
            e.moe_h = [[sb(f"moe_h{par}{part}", INTER // P * CH, F32R).rearrange("p (i n) -> p i n", n=CH)
                        for part in range(2)] for par in range(2)]
            e.moe_f = [sb(f"moe_f{i}", CH) for i in range(2)]
            e.x_parts = [sb(f"x_part{i}", NC * S, F32R).rearrange("p (k n) -> p k n", k=NC) for i in range(2)]

        d = dram

        def mat(dst, name):
            return dst, d[name].rearrange("(k p) o -> p k o", p=P)

        def row(dst, name):
            return dst, d[name].partition_broadcast(P)

        def col(dst, name):
            return dst, d[name + "_col"]

        def from_xT(w):
            def products(t, bank):
                for c in range(NC):
                    last = nc.tensor.matmul(bank, e.xT[:, c, t * P:(t + 1) * P], w[:, c, :],
                                            start=(c == 0), stop=(c == NC - 1))
                return last
            return products

        def quantised(t, bank):
            for c in range(NC):
                last = nc.tensor.matmul(bank, e.xq[:, c, t * P:(t + 1) * P], e.wq[:, c, :],
                                        start=(c == 0), stop=(c == NC - 1))
            return last

        q_scale = HD ** -0.5
        wq_a, wk_a = e.w_a[:, :, 0:D], e.w_a[:, :, D:2 * D]

        load_phase(nc, e)
        rope_phase(nc, e)
        split_phase(nc, e, [], [mat(e.w_v, "L0_attn_Wv")], [(None, None, q_scale, e.qkn[:, :, 0:D], S, e.qd),
                                (None, None, 1.0, e.qkn[:, :, D:2 * D], S, e.kd)])
        attention_phase(nc, e, S, True, False, (e.w_v, e.xT, False),
                        [row(e.b_row, "L0_attn_bo")], masks_ahead=True)
        transpose_phase(nc, e, e.cn, e.xT)
        output_phase(nc, e, [mat(e.w_o, "L0_attn_Wo")], from_xT(e.w_o),
                     e.x_nat, None, e.x_nat, e.x_nat, e.eps5)

        def cross(names, masked):
            wq, bq, wk, bk, wv, bv, wo, bo = names
            split_phase(nc, e, [mat(wq_a, wq), mat(wk_a, wk), col(e.bq_col, bq), col(e.bk_col, bk),
                                (e.ctxT, d["ctxT"].rearrange("(k p) t -> p k t", p=P))],
                        [mat(e.w_v, wv), row(e.bv_row, bv)],
                        [(wq_a, e.bq_col, q_scale, e.xT, S, e.qd), (wk_a, e.bk_col, 1.0, e.ctxT, S2, e.kd)])
            attention_phase(nc, e, S2, False, masked, (e.w_v, e.ctxT, True),
                            [mat(e.w_o, wo), row(e.b_row, bo)])
            transpose_phase(nc, e, e.cn, e.xT)
            output_phase(nc, e, [], from_xT(e.w_o), e.x_nat, None,
                         e.x_nat, e.x_nat, e.eps5)

        cross(["L0_xattn_" + n for n in ("Wq", "bq", "Wk", "bk", "Wv", "bv", "Wo", "bo")], True)
        fp8_phase(nc, e)
        output_phase(nc, e, [], quantised, e.x_nat, e.b_row, e.x_nat, e.x_nat, e.eps5, scale=e.descale2,
                     turn=False)

        output_phase(nc, e, [], None, None, None, e.x_nat, e.cn, e.eps10)
        w, b = d["L1_attn_w_attn"], d["L1_attn_b_attn"]
        split_phase(nc, e, [(e.w_a, w[:, 0:2 * D].rearrange("(k p) o -> p k o", p=P)),
                            (e.bq_col, d["L1_attn_b_attn_col"][:, 0:NC]),
                            (e.bk_col, d["L1_attn_b_attn_col"][:, NC:2 * NC])],
                    [(e.w_v, w[:, 2 * D:3 * D].rearrange("(k p) o -> p k o", p=P)),
                     (e.bv_row, b[2 * D:3 * D].partition_broadcast(P))],
                    [(wq_a, e.bq_col, q_scale, e.xT, S, e.qd), (wk_a, e.bk_col, 1.0, e.xT, S, e.kd)])
        attention_phase(nc, e, S, True, False, (e.w_v, e.xT, True),
                        [mat(e.w_o, "L1_attn_w_proj"), row(e.b_row, "L1_attn_b_proj")], add_bias=False)
        transpose_phase(nc, e, e.cn, e.xT)
        output_phase(nc, e, [], from_xT(e.w_o),
                     e.x_nat, e.b_row, e.vall, e.cn, e.eps10)
        mlp_phase(nc, e)
        output_phase(nc, e, [], None, None, None, e.x_nat, e.x_nat, e.eps5)

        cross(["L1_xattn_" + n for n in ("q_w", "q_b", "k_w", "k_b", "v_w", "v_b", "o_w", "o_b")], False)
        gate_phase(nc, e)
        expert_memory()
        moe_phase(nc, e)
        output_phase(nc, e, [], None, None, None, e.cn, None, e.eps5, turn=False)


_TRANSPOSED = ["L0_attn_Wq", "L0_attn_Wk", "L0_attn_Wv", "L0_attn_Wo", "L0_xattn_Wq", "L0_xattn_Wk",
               "L0_xattn_Wv", "L0_xattn_Wo", "L0_ffn_weight", "L1_attn_w_attn", "L1_attn_w_proj",
               "L1_attn_w_fc", "L1_attn_w_mlp_proj", "L1_ffn_gate_w"]
_PLAIN = ["L0_attn_q_gamma", "L0_attn_q_beta", "L0_attn_k_gamma", "L0_attn_k_beta", "L0_attn_bo",
          "L0_xattn_bv", "L0_xattn_bo", "L0_ffn_bias", "L1_attn_b_attn",
          "L1_attn_b_proj", "L1_attn_b_mlp_proj", "L1_xattn_q_w", "L1_xattn_k_w", "L1_xattn_v_w", "L1_xattn_v_b", "L1_xattn_o_w", "L1_xattn_o_b",
          "L1_ffn_gate_bias"]

_COLUMNS = ["L0_xattn_bq", "L0_xattn_bk", "L1_attn_b_attn", "L1_attn_b_fc", "L1_xattn_q_b", "L1_xattn_k_b"]


def constants():
    f = np.float32
    rows, cols = np.arange(P)[:, None], np.arange(P)[None, :]
    theta = np.arange(S, dtype=f)[:, None] * np.exp(-(np.arange(0, HD, 2, dtype=f) / f(HD)) * f(np.log(10000.0)))
    cos, sin = np.repeat(np.cos(theta), 2, axis=1), np.repeat(np.sin(theta), 2, axis=1)
    sin = np.concatenate([-sin[:, :HD // 2], sin[:, HD // 2:]], axis=1)
    E = NE - 1
    return {
        "ident": np.eye(P, dtype=f), "masked": f(MASKED) * np.eye(P, dtype=f),
        "upper": np.where(cols > rows, f(MASKED), f(0)),
        "lower": np.where(rows > cols, f(MASKED), f(0)),
        "rope_cos": cos.astype(f), "rope_sin": sin.astype(f),
        "below": (np.arange(E)[None, :] < np.arange(E)[:, None]).astype(f).reshape(-1),
    }


def kernel(**inputs):
    import concourse.bacc as bacc
    from concourse.bass_utils import run_bass_kernel_spmd

    nc = bacc.Bacc("TRN2", target_bir_lowering=False, num_devices=1)
    a = {k: np.asarray(v) for k, v in inputs.items()}
    laid = dict(constants())
    laid["x"] = a["x"][0]
    laid["xT"] = a["x"][0].T
    laid["ctxT"] = a["ctx_1024"][0].T
    laid["mask"] = a["mask_1x1xSxS2_ik0"][0, 0]
    laid["maskT"] = a["mask_1x1xSxS2_ik0"][0, 0].T
    for name in _TRANSPOSED:
        laid[name] = a[name].T
    for name in _PLAIN:
        laid[name] = a[name]
    for name in _COLUMNS:
        laid[name + "_col"] = a[name].reshape(-1, P).T
    for name in ("w1", "w3", "w2"):
        both = np.concatenate([a["L1_ffn_" + name], a["L1_ffn_s" + name][None]])
        laid["moe_" + name] = both.transpose(0, 2, 1).reshape(-1, both.shape[1])
    arrays, dram = {}, {}
    for name, v in laid.items():
        arrays[f"in_{name}"] = np.ascontiguousarray(v)
        dram[name] = nc.dram_tensor(f"in_{name}", v.shape, mybir.dt.from_np(v.dtype), kind="ExternalInput").ap()
    out = nc.dram_tensor("out_x", (S, D), F32, kind="ExternalOutput").ap()
    build(nc, dram, out)
    r = run_bass_kernel_spmd(nc, [arrays], core_ids=[0])
    return r.results[0]["out_x"].reshape(1, S, D)
```
